# Optimizing a Trainium2 kernel written in Bass

```python
import numpy as np
import jax
import jax.numpy as jnp

def _softmax(x, axis=-1):
    return jax.nn.softmax(x, axis=axis)

def _gelu(x):
    return jax.nn.gelu(x, approximate=True)

def _silu(x):
    return jax.nn.silu(x)

def _sigmoid(x):
    return jax.nn.sigmoid(x)

def _layernorm(x, axis=-1, eps=1e-05):
    m = jnp.mean(x, axis=axis, keepdims=True)
    v = jnp.var(x, axis=axis, keepdims=True)
    return (x - m) / jnp.sqrt(v + eps)

def _scatter_add(tgt, idx, src, axis=0):
    return tgt.at[idx].add(src)

def _segment_sum(src, seg, n):
    return jax.ops.segment_sum(src, seg, n)
kernel_name = 'mk_lm_tower_d1_tok_ids2048_r4_d5c4a8'

def setup_inputs(seed: int=0):
    np.random.seed(seed)
    _w = jnp.asarray

    def _rec_inputs():
        import jax
        import jax.numpy as jnp
        _rk = jax.random.key(seed)
        x = jax.random.randint(jax.random.fold_in(_rk, 1), (32, 128), 0, 12564, jnp.int32)
        return x
    x = _rec_inputs()

    def _L0_tok_setup():
        import jax, jax.numpy as jnp
        import numpy as np
        VOCAB = 50257
        DIM = 512
        PADDING_IDX = 0
        key = jax.random.key(seed)
        k_ids, k_w = jax.random.split(key)
        input_ids = jax.random.randint(k_ids, (8, 1024), 0, VOCAB, dtype=jnp.int64 if jax.config.jax_enable_x64 else jnp.int32)
        weight = jax.random.normal(k_w, (VOCAB, DIM), dtype=jnp.float32)
        weight = weight.at[PADDING_IDX].set(0.0)
        return {'input_ids': input_ids, 'weight': weight}
    _L0_tok_all = _L0_tok_setup()
    _L0_tok_in = {k: v for k, v in _L0_tok_all.items() if k in ('weight',)}
    del _L0_tok_all

    def _L0_attn_setup():
        import jax, jax.numpy as jnp
        import numpy as np
        HEADS = 16
        HIDDEN = 512
        HEAD_DIM = HIDDEN // HEADS
        key = jax.random.key(seed)
        ks = jax.random.split(key, 9)
        s = 1.0 / np.sqrt(HIDDEN)
        inp = {'x': jax.random.normal(ks[0], (2, 512, HIDDEN), dtype=jnp.float32)}
        for i, name in enumerate(['q', 'k', 'v', 'out']):
            inp[f'W{name}'] = jax.random.uniform(ks[1 + 2 * i], (HIDDEN, HIDDEN), minval=-s, maxval=s, dtype=jnp.float32)
            inp[f'b{name}'] = jax.random.uniform(ks[2 + 2 * i], (HIDDEN,), minval=-s, maxval=s, dtype=jnp.float32)
        return inp
    _L0_attn_all = _L0_attn_setup()
    _L0_attn_in = {k: v for k, v in _L0_attn_all.items() if k in ('Wq', 'bq', 'Wk', 'bk', 'Wv', 'bv', 'Wout', 'bout')}
    del _L0_attn_all

    def _L0_ffn_setup():
        import jax, jax.numpy as jnp
        import numpy as np
        H = 512
        I_MOE = 352
        I_SH = 1408
        E = 8
        TOP_K = 2
        B, S = (1, 512)

        def _silu_and_mul(gu, inter):
            return jax.nn.silu(gu[..., :inter]) * gu[..., inter:]
        key = jax.random.key(seed)
        ks = jax.random.split(key, 7)
        sc = 0.02
        return {'hidden_states': jax.random.normal(ks[0], (B, S, H), jnp.float32), 'W_router': jax.random.normal(ks[1], (E, H), jnp.float32) * sc, 'W_sgate': jax.random.normal(ks[2], (1, H), jnp.float32) * sc, 'Ws_gate_up': jax.random.normal(ks[3], (H, 2 * I_SH), jnp.float32) * sc, 'Ws_down': jax.random.normal(ks[4], (I_SH, H), jnp.float32) * sc, 'We_gate_up': jax.random.normal(ks[5], (E, H, 2 * I_MOE), jnp.float32) * sc, 'We_down': jax.random.normal(ks[6], (E, I_MOE, H), jnp.float32) * sc}
    _L0_ffn_all = _L0_ffn_setup()
    _L0_ffn_in = {k: v for k, v in _L0_ffn_all.items() if k in ('W_router', 'W_sgate', 'Ws_gate_up', 'Ws_down', 'We_gate_up', 'We_down')}
    del _L0_ffn_all
    return {'x': x, 'L0_tok_weight': _L0_tok_in['weight'], 'L0_attn_Wq': _L0_attn_in['Wq'], 'L0_attn_bq': _L0_attn_in['bq'], 'L0_attn_Wk': _L0_attn_in['Wk'], 'L0_attn_bk': _L0_attn_in['bk'], 'L0_attn_Wv': _L0_attn_in['Wv'], 'L0_attn_bv': _L0_attn_in['bv'], 'L0_attn_Wout': _L0_attn_in['Wout'], 'L0_attn_bout': _L0_attn_in['bout'], 'L0_ffn_W_router': _L0_ffn_in['W_router'], 'L0_ffn_W_sgate': _L0_ffn_in['W_sgate'], 'L0_ffn_Ws_gate_up': _L0_ffn_in['Ws_gate_up'], 'L0_ffn_Ws_down': _L0_ffn_in['Ws_down'], 'L0_ffn_We_gate_up': _L0_ffn_in['We_gate_up'], 'L0_ffn_We_down': _L0_ffn_in['We_down']}

def reference(x, L0_tok_weight, L0_attn_Wq, L0_attn_bq, L0_attn_Wk, L0_attn_bk, L0_attn_Wv, L0_attn_bv, L0_attn_Wout, L0_attn_bout, L0_ffn_W_router, L0_ffn_W_sgate, L0_ffn_Ws_gate_up, L0_ffn_Ws_down, L0_ffn_We_gate_up, L0_ffn_We_down):
    import jax
    import jax.numpy as jnp

    def _L0_tok_ref(input_ids, weight):
        import jax, jax.numpy as jnp
        import numpy as np
        VOCAB = 50257
        DIM = 512
        PADDING_IDX = 0
        return jnp.take(weight, input_ids, axis=0)

    def _L0_attn_ref(x, Wq, bq, Wk, bk, Wv, bv, Wout, bout):
        import jax, jax.numpy as jnp
        import numpy as np
        HEADS = 16
        HIDDEN = 512
        HEAD_DIM = HIDDEN // HEADS
        bsz, seq_len, _ = x.shape
        q = x @ Wq.T + bq
        k = x @ Wk.T + bk
        v = x @ Wv.T + bv
        q = q.reshape(bsz, seq_len, HEADS, HEAD_DIM).transpose(0, 2, 1, 3)
        k = k.reshape(bsz, seq_len, HEADS, HEAD_DIM).transpose(0, 2, 1, 3)
        v = v.reshape(bsz, seq_len, HEADS, HEAD_DIM).transpose(0, 2, 1, 3)
        scale = HEAD_DIM ** 0.5
        scores = jnp.einsum('bhqd,bhkd->bhqk', q, k) / scale
        weights = jax.nn.softmax(scores, axis=-1)
        attn = jnp.einsum('bhqk,bhkd->bhqd', weights, v)
        attn = attn.transpose(0, 2, 1, 3).reshape(bsz, seq_len, HIDDEN)
        return attn @ Wout.T + bout

    def _L0_ffn_ref(hidden_states, W_router, W_sgate, Ws_gate_up, Ws_down, We_gate_up, We_down):
        import jax, jax.numpy as jnp
        import numpy as np
        H = 512
        I_MOE = 352
        I_SH = 1408
        E = 8
        TOP_K = 2
        B, S = (1, 512)

        def _silu_and_mul(gu, inter):
            return jax.nn.silu(gu[..., :inter]) * gu[..., inter:]
        orig_shape = hidden_states.shape
        x = hidden_states.reshape(-1, H)
        T = x.shape[0]
        logits = x @ W_router.T
        probs = jax.nn.softmax(logits.astype(jnp.float32), axis=-1)
        rw, sel = jax.lax.top_k(probs, TOP_K)
        rw = rw.astype(x.dtype)
        combine = jnp.zeros((T, E), x.dtype).at[jnp.arange(T)[:, None], sel].add(rw)
        sh = _silu_and_mul(x @ Ws_gate_up, I_SH) @ Ws_down
        shared_out = sh * jax.nn.sigmoid(x @ W_sgate.T)
        gu = jnp.einsum('th,ehi->eti', x, We_gate_up)
        h = _silu_and_mul(gu, I_MOE)
        eo = jnp.einsum('eti,eih->eth', h, We_down)
        sparse_out = jnp.einsum('eth,te->th', eo, combine)
        return (shared_out + sparse_out).reshape(orig_shape)
    h = _L0_tok_ref(x, L0_tok_weight)
    h = h + _L0_attn_ref(_layernorm(h, axis=-1), L0_attn_Wq, L0_attn_bq, L0_attn_Wk, L0_attn_bk, L0_attn_Wv, L0_attn_bv, L0_attn_Wout, L0_attn_bout)
    h = h + _L0_ffn_ref(_layernorm(h, axis=-1), L0_ffn_W_router, L0_ffn_W_sgate, L0_ffn_Ws_gate_up, L0_ffn_Ws_down, L0_ffn_We_gate_up, L0_ffn_We_down)
    return h

_drawn_inputs = setup_inputs


def setup_inputs(seed=0):
    import zlib

    import numpy as np

    out = dict(_drawn_inputs(seed))
    spreads = {}
    factors = {'L0_attn_Wq': 4.939,
     'L0_attn_bq': 8.0,
     'L0_attn_Wk': 4.858,
     'L0_attn_bk': 64.0,
     'L0_attn_bv': 3.792,
     'L0_ffn_W_router': 5.563,
     'L0_ffn_W_sgate': 51.912,
     'L0_ffn_We_gate_up': 4.813,
     'L0_ffn_We_down': 4.802,
     'L0_ffn_Ws_gate_up': 4.776,
     'L0_ffn_Ws_down': 4.785}
    for name, (base, spread) in spreads.items():
        noise = np.random.default_rng([zlib.crc32(name.encode()), seed]).standard_normal(out[name].shape)
        drawn = base * np.exp(spread * noise) if base else spread * noise
        out[name] = jnp.asarray(drawn.astype(out[name].dtype))
    for name, factor in factors.items():
        out[name] = (out[name] * factor).astype(out[name].dtype)
    return out
```

```python
from contextlib import ExitStack

import concourse.bass as bass
from concourse import mybir

F32 = mybir.dt.float32
F32R = mybir.dt.float32r
I32 = mybir.dt.int32
U32 = mybir.dt.uint32
ACT = mybir.ActivationFunctionType
ALU = mybir.AluOpType
AX_X = mybir.AxisListType.X

P = 128
DIM = 512
NC = DIM // P
HEADS = 16
HD = DIM // HEADS
EXPERTS = 8
I_MOE = 352
I_SH = 1408
TOPK = 2
TB = 4
GT = TB * P
EPS = 1e-5
LOGITS = EXPERTS + 1


class Stage:

    def __init__(self, new_sem, name, per, dma=False, lanes=1, credit=True):
        assert per % lanes == 0
        self.credits = per // lanes if credit else 0
        self.per, self.lanes, self.unit = per, lanes, 16 if dma else 1
        self.sems = [new_sem(name if lanes == 1 else f"{name}{n}") for n in range(lanes)]

    def inc(self, n=0):
        return self.sems[n % self.lanes], self.unit

    def done(self, n, i=0):
        per = self.per // self.lanes
        return self.sems[n % self.lanes], (i * per + (self.credits + n // self.lanes + 1)) * self.unit

    def credit(self, eng):
        if self.credits:
            for s in self.sems:
                eng.sem_inc(s, self.credits * self.unit)


class Count:

    def __init__(self, sem):
        self.sem, self.base, self.lap, self.k = sem, 0, 0, 0

    def tick(self):
        self.k += 1
        return self.sem, 1

    def so_far(self):
        return self.sem, self.base + self.lap + self.k

    def enter(self, i, per):
        self.base, self.lap, self.k, self.per = self.base + self.k, i * per, 0, per

    def leave(self, n):
        assert self.k == self.per, (self.sem, self.k)
        self.base, self.lap, self.k = self.base + n * self.per, 0, 0


def split_product(pe, out, stationary, moving, first, last):
    (sh, sl), (mh, ml) = stationary, moving
    pe.matmul(out, sh, mh, start=first, stop=False)
    pe.matmul(out, sh, ml, start=False, stop=False)
    return pe.matmul(out, sl, mh, start=False, stop=last)


class Norm:

    def __init__(self, new_sem, sb, name, slots):
        self.slots = slots
        self.stats = sb(f"{name}_stats", [P, slots, 6])
        self.mean_var = sb(f"{name}_mean_var", [P, slots, 2])
        self.small = sb(f"{name}_small", [P, slots, 6])


def attention_phase(nc, new_sem, keep, io, scratch):
    x_ids, table = io["x"], io["L0_tok_weight"]
    groups = x_ids.shape[0] // TB
    last = groups - 1

    with ExitStack() as mem:
        def sb(name, shape, dt=F32):
            return mem.enter_context(nc.sbuf_tensor(name, shape, dt))

        def ps(name, shape):
            return mem.enter_context(nc.psum_tensor(name, shape, F32))

        def stage(name, per, **kw):
            s = Stage(new_sem, name, per, **kw)
            stages.append(s)
            return s

        stages = []
        eye = keep["eye"]
        weights = {"q": "L0_attn_Wq", "k": "L0_attn_Wk", "v": "L0_attn_Wv", "o": "L0_attn_Wout"}
        w_hi = {w: sb(f"w_{w}_hi", [P, NC, DIM], F32R) for w in weights}
        w_lo = {w: sb(f"w_{w}_lo", [P, NC, DIM], F32R) for w in weights}
        arena = sb("arena", [P, 2 * NC, DIM])
        w_raw = [arena[:, n * NC:(n + 1) * NC, :] for n in range(2)]
        router_raw = sb("router_raw", [LOGITS, DIM])
        router_t = sb("router_t", [P, NC, LOGITS])
        bias_qk = sb("bias_qk", [P, 2, NC])
        bias_v = sb("bias_v", [P, DIM])
        bias_o = sb("bias_o", [P, DIM])
        ids = sb("ids", [P, groups * TB], I32)
        ids_now = sb("ids_now", [P, TB], I32)

        h = [sb(f"h{b}", [P, DIM]) for b in range(TB)]
        res = [sb(f"res{b}", [P, DIM]) for b in range(TB)]
        xn = [sb(f"xn_{b}", [P, DIM]) for b in range(TB)]
        xt_hi = sb("xt_hi", [P, NC, GT], F32R)
        xt_lo = sb("xt_lo", [P, NC, GT], F32R)
        q_hi, q_lo = ([sb(f"q_{part}{n}", [P, GT], F32R) for n in range(2)] for part in ("hi", "lo"))
        k_hi, k_lo = ([sb(f"k_{part}{n}", [P, TB, 4, P], F32R) for n in range(2)] for part in ("hi", "lo"))
        v_rows = sb("v_rows", [P, TB, HEADS, HD + 1])
        norm = Norm(new_sem, sb, "ln", 2 * TB)
        row_max = sb("row_max", [P, 2, NC])
        diff, prob, prob_t = ([arena[:, m + n, :].rearrange("p (h k) -> p h k", k=P) for n in range(2)]
                              for m in (0, 2, 4))
        inv_sum = sb("inv_sum", [P, 2, NC])
        att = [sb(f"att{b}", [P, HEADS, HD]) for b in range(TB)]
        att_t = [(sb(f"att_t_hi{n}", [P, NC, P], F32R), sb(f"att_t_lo{n}", [P, NC, P], F32R)) for n in range(2)]
        h2 = [arena[:, 6 + n, :] for n in range(2)]
        xn2 = [sb(f"xn2_{n}", [P, DIM]) for n in range(2)]
        xn2_t = [sb(f"xn2_t{n}", [P, NC, P]) for n in range(2)]

        px = [ps(f"px{n}", [P, DIM]) for n in range(2)]
        score = [ps(f"score{n}", [P, NC, P]) for n in range(2)]
        pt = [ps(f"pt{n}", [P, NC, P]) for n in range(2)]
        av = [ps(f"av{n}", [P, NC, HD + 1]) for n in range(2)]

        UNITS = NC * TB

        h_in = stage("h_in", TB, dma=True, lanes=TB, credit=False)
        res_done = stage("res_done", TB)
        xn_turned = stage("xn_turned", TB)
        q_made, k_made, v_made = stage("q_made", NC), stage("k_made", NC), stage("v_made", TB)
        scored = stage("scored", UNITS)
        prob_turned = stage("prob_turned", UNITS)
        av_made = stage("av_made", UNITS)
        att_turned = stage("att_turned", TB)
        o_made = stage("o_made", TB)
        xn2_turned = stage("xn2_turned", TB)
        logits_made = stage("logits_made", TB)
        xt_hi_done = stage("xt_hi_done", TB)
        q_hi_done, k_hi_done = stage("q_hi_done", NC), stage("k_hi_done", NC)
        exp_done = stage("exp_done", UNITS)
        prob_t_done = stage("prob_t_done", UNITS)
        att_hi_done = stage("att_hi_done", TB)
        xn2_t_done = stage("xn2_t_done", TB)
        y0_done = [stage(f"y0_done{n}", TB) for n in (1, 2)]
        var_done = [stage(f"var_done{n}", TB) for n in (1, 2)]
        xn_done = stage("xn_done", TB)
        xt_lo_done = stage("xt_lo_done", TB)
        q_lo_done, k_lo_done, v_done = stage("q_lo_done", NC), stage("k_lo_done", NC), stage("v_done", TB)
        diff_done = stage("diff_done", UNITS)
        att_done = stage("att_done", UNITS)
        att_lo_done = stage("att_lo_done", TB)
        h2_done = stage("h2_done", TB)
        xn2_done = stage("xn2_done", TB)
        logits_done = stage("logits_done", TB)
        h2_out = stage("h2_out", TB, dma=True, lanes=2)
        xn2_out = stage("xn2_out", TB, dma=True, lanes=2)

        credits_given = new_sem("credits_given")
        eye_zeroed, eye_ready, ones_ready = new_sem("eye_zeroed"), new_sem("eye_ready"), new_sem("ones_ready")
        k_zeroed = new_sem("k_zeroed")
        w_in = [new_sem(f"w_in_{w}") for w in weights]
        router_in, bias_in, ids_in = new_sem("router_in"), new_sem("bias_in"), new_sem("ids_in")
        ids_copied, pool_go = new_sem("ids_copied"), new_sem("pool_go")
        w_turned, w_hi_done, w_lo_done = new_sem("w_turned"), new_sem("w_hi_done"), new_sem("w_lo_done")
        dve_step, dve_go, act_step = new_sem("dve_step"), new_sem("dve_go"), new_sem("act_step")

        drained_by = {"q": q_lo_done, "k": k_lo_done, "v": v_done, "xt": xt_lo_done, "ot": att_lo_done, "o": h2_done,
                      "x2t": xn2_t_done, "logit": logits_done}
        px_uses = ([("q", 0), ("k", 0)] + [("v", b) for b in range(TB)]
                   + [(w, c) for c in range(1, NC) for w in ("q", "k")] + [("xt", b) for b in range(TB)])
        for s in range(TB + 4):
            for kind, lag in (("ot", 0), ("o", 1), ("x2t", 3), ("logit", 4)):
                if 0 <= s - lag < TB:
                    px_uses.append((kind, s - lag))
        assert len(px_uses) % 2 == 0

        def bank(kind, n):
            return px[px_uses.index((kind, n)) % 2]

        def bank_free(kind, n, i, more=True):
            uses = [u for u in px_uses if more or u[0] != "xt"]
            at = uses.index((kind, n)) - 2
            kind, n = uses[at]
            return drained_by[kind].done(n, i + (kind == "xt") - (at < 0))

        block = mem.enter_context(nc.Block())

        @block.sync
        def _(sp):
            for n, w in enumerate(weights):
                if n >= 2:
                    sp.wait_ge(w_turned, NC * (n - 1))
                sp.dma_start(w_raw[n % 2][:], io[weights[w]].rearrange("(c p) n -> p c n", p=P)).then_inc(w_in[n], 16)
                if n == 1:
                    for s in stages:
                        s.credit(sp)
                    sp.sem_inc(credits_given, 1)
                    with nc.allow_non_contiguous_dma(reason="token ids and biases, one per partition"):
                        sp.dma_start(ids[:], x_ids.rearrange("b p -> p b")).then_inc(ids_in, 16)
                        for m, name in enumerate(("L0_attn_bq", "L0_attn_bk")):
                            sp.dma_start(bias_qk[:, m, :], io[name].rearrange("(c p) -> p c", p=P)).then_inc(bias_in, 16)
                    for dst, name in ((bias_v, "L0_attn_bv"), (bias_o, "L0_attn_bout")):
                        sp.dma_start(dst[:], io[name].rearrange("(a d) -> a d", a=1).broadcast_to((P, DIM)))\
                          .then_inc(bias_in, 16)
                    sp.dma_start(router_raw[0:EXPERTS, :], io["L0_ffn_W_router"]).then_inc(router_in, 16)
                    sp.dma_start(router_raw[EXPERTS:LOGITS, :], io["L0_ffn_W_sgate"]).then_inc(router_in, 16)

            with sp.Fori(0, groups) as i:
                for b in range(TB):
                    rows = bass.ds((i * TB + b) * P, P)
                    sp.wait_ge(*h2_done.done(b, i))
                    sp.dma_start(scratch["h2"][rows, :], h2[b % 2]).then_inc(*h2_out.inc(b))
                    sp.wait_ge(*xn2_done.done(b, i))
                    sp.dma_start(scratch["xn2"][rows, :], xn2[b % 2][:]).then_inc(*xn2_out.inc(b))
            for b in (TB - 2, TB - 1):
                sp.wait_ge(*h2_out.done(b, last))
                sp.wait_ge(*xn2_out.done(b, last))

        @block.gpsimd
        def _(pool):
            pool.memset(eye[:], 0.0).then_inc(eye_zeroed, 1)
            pool.memset(v_rows[:, :, :, HD:HD + 1], 1.0).then_inc(ones_ready, 1)
            pool.wait_ge(eye_zeroed, 1)
            pool.affine_select(out=eye[:], in_=eye[:], compare_op=ALU.not_equal, fill=1.0, base=0,
                               pattern=[[-1, P]], channel_multiplier=1).then_inc(eye_ready, 1)
            for tile in (*k_hi, *k_lo):
                pool.memset(tile[:].bitcast(F32), 0.0).then_inc(k_zeroed, 1)
            pool.wait_ge(credits_given, 1)
            pool.wait_ge(ids_in, 16)
            pool.wait_ge(bias_in, 64)
            with pool.Fori(0, groups) as i:
                pool.wait_ge(*xn_done.done(TB - 1, i - 1))
                pool.wait_ge(*res_done.done(TB - 1, i - 1))
                pool.sem_inc(pool_go, 1)
                pool.tensor_copy(ids_now[:], ids[:, bass.ds(i * TB, TB)]).then_inc(ids_copied, 1)
                pool.wait_ge(ids_copied, i + 1)
                pool.sem_inc(pool_go, 1)
                for b in range(TB):
                    pool.indirect_dma_start(
                        out=h[b][:], out_offset=None, in_=table,
                        in_offset=bass.IndirectOffsetOnAxis(ap=ids_now[:, b:b + 1].bitcast(U32), axis=0),
                    ).then_inc(*h_in.inc(b))
                for b in range(TB):
                    pool.wait_ge(*h_in.done(b, i))
                    pool.wait_ge(*h2_done.done(b, i - 1))
                    pool.tensor_tensor(res[b][:], h[b][:], bias_o[:], ALU.add).then_inc(*res_done.inc())

        @block.scalar
        def _(act):
            act.preload_act_table_set("natural_log_exp_and_others")
            steps = Count(act_step)

            def rsqrt(slot, i):
                act.wait_ge(*var_done[slot // TB].done(slot % TB, i))
                act.activation(norm.small[:, slot, 1:2], norm.small[:, slot, 0:1], ACT.Ln).then_inc(*steps.tick())
                act.wait_ge(*steps.so_far())
                act.activation(norm.small[:, slot, 2:3], norm.small[:, slot, 1:2], ACT.Exp, scale=-0.5)\
                   .then_inc(*y0_done[slot // TB].inc())

            def xt_split(b, i, src):
                act.wait_ge(*xn_turned.done(b, i))
                act.wait_ge(*k_made.done(NC - 1, i - 1))
                act.activation(xt_hi[:, :, b * P:(b + 1) * P], src[:].rearrange("p (c n) -> p c n", c=NC), ACT.Copy)\
                   .then_inc(*xt_hi_done.inc())

            for n in range(len(weights) * NC):
                act.wait_ge(w_turned, n + 1)
                act.activation(w_hi["qkvo"[n // NC]][:, n % NC, :], px[n % 2][:], ACT.Copy).then_inc(w_hi_done, 1)
            act.wait_ge(bias_in, 64)
            act.wait_ge(k_zeroed, 4)
            act.wait_ge(credits_given, 1)
            for b in range(TB):
                rsqrt(b, 0)
            for b in range(TB):
                xt_split(b, 0, px[b % 2])

            def q_split(c, i):
                act.wait_ge(*q_made.done(c, i))
                act.wait_ge(*scored.done(4 * c - 5, i))
                act.activation(q_hi[c % 2][:], bank("q", c)[:], ACT.Identity, bias=bias_qk[:, 0, c:c + 1])\
                   .then_inc(*q_hi_done.inc())

            def k_split(c, i):
                act.wait_ge(*k_made.done(c, i))
                act.wait_ge(*scored.done(4 * c - 5, i))
                for r in range(4):
                    x = act.activation(k_hi[c % 2][r * HD:(r + 1) * HD, :, r, :],
                                       bank("k", c)[r * HD:(r + 1) * HD, :].rearrange("p (b k) -> p b k", k=P),
                                       ACT.Identity, bias=bias_qk[r * HD:(r + 1) * HD, 1, c:c + 1])
                x.then_inc(*k_hi_done.inc())

            def group(i, more):
                q_split(0, i)
                k_split(0, i)
                for s in range(UNITS + 4):
                    if s < UNITS:
                        act.wait_ge(*diff_done.done(s, i))
                        act.wait_ge(*prob_turned.done(s - 2, i))
                        act.activation(prob[s % 2][:], diff[s % 2][:], ACT.Exp, scale=float(HD) ** -0.5)\
                           .then_inc(*exp_done.inc())
                    u = s - 2
                    if 0 <= u < UNITS:
                        act.wait_ge(*prob_turned.done(u, i))
                        act.wait_ge(*av_made.done(u - 2, i))
                        act.activation(prob_t[u % 2][:], pt[u % 2][:], ACT.Copy).then_inc(*prob_t_done.inc())
                    if s % 4 == 0 and s // 4 + 1 < NC:
                        q_split(s // 4 + 1, i)
                    if s % 4 == 2 and s // 4 + 1 < NC:
                        k_split(s // 4 + 1, i)
                    if more and s % 4 == 3 and s < UNITS:
                        rsqrt(s // 4, i + 1)
                if more:
                    for b in range(TB):
                        xt_split(b, i + 1, bank("xt", b))
                for s in range(TB + 4):
                    if s < TB:
                        act.wait_ge(*att_turned.done(s, i))
                        act.wait_ge(*o_made.done(s - 2, i))
                        act.activation(att_t[s % 2][0][:], bank("ot", s)[:].rearrange("p (c n) -> p c n", c=NC),
                                       ACT.Copy).then_inc(*att_hi_done.inc())
                    b = s - 1
                    if 0 <= b < TB:
                        rsqrt(TB + b, i)
                    b = s - 3
                    if 0 <= b < TB:
                        act.wait_ge(*xn2_turned.done(b, i))
                        act.wait_ge(*logits_made.done(b - 2, i))
                        act.activation(xn2_t[b % 2][:], bank("x2t", b)[:].rearrange("p (c n) -> p c n", c=NC),
                                       ACT.Copy).then_inc(*xn2_t_done.inc())

            with act.Fori(0, last) as i:
                steps.enter(i, 2 * TB)
                group(i, True)
                steps.leave(last)
            group(last, False)

        @block.vector
        def _(dve):
            steps, holds = Count(dve_step), Count(dve_go)

            def link(ins):
                ins.then_inc(*steps.tick())
                dve.wait_ge(*steps.so_far())

            def norm_stats(slot, src):
                dve.bn_stats(norm.stats[:, slot, :], src).then_inc(*steps.tick())
                dve.wait_ge(*steps.so_far())
                dve.sem_inc(dve_go, 1)
                link(dve.bn_aggr(norm.mean_var[:, slot, :], norm.stats[:, slot, :]))
                dve.tensor_scalar(norm.small[:, slot, 0:1], norm.mean_var[:, slot, 1:2], EPS, None, ALU.add)\
                   .then_inc(*var_done[slot // TB].inc())

            def norm_rows(slot, i, src, dst):
                s = norm.small[:, slot, :]
                dve.wait_ge(*y0_done[slot // TB].done(slot % TB, i))
                link(dve.scalar_tensor_tensor(out=s[:, 3:4], in0=s[:, 2:3], scalar=s[:, 0:1], in1=s[:, 2:3],
                                              op0=ALU.mult, op1=ALU.mult))
                link(dve.tensor_scalar(s[:, 4:5], s[:, 3:4], -0.5, 1.5, ALU.mult, ALU.add))
                link(dve.tensor_tensor(s[:, 5:6], s[:, 2:3], s[:, 4:5], ALU.mult))
                return dve.tensor_scalar(dst, src, norm.mean_var[:, slot, 0:1], s[:, 5:6], ALU.subtract, ALU.mult)

            def norm1_stats(b, i):
                dve.wait_ge(*h_in.done(b, i))
                norm_stats(b, h[b][:])

            def norm1_rows(b, i):
                dve.wait_ge(*xn_turned.done(b, i - 1))
                norm_rows(b, i, h[b][:], xn[b][:]).then_inc(*xn_done.inc())

            def xt_split(b, i, src):
                dve.wait_ge(*xt_hi_done.done(b, i))
                cols = slice(b * P, (b + 1) * P)
                dve.tensor_tensor(xt_lo[:, :, cols], src[:].rearrange("p (c n) -> p c n", c=NC),
                                  xt_hi[:, :, cols].bitcast(F32), ALU.subtract).then_inc(*xt_lo_done.inc())

            for n in range(len(weights) * NC):
                w, c = "qkvo"[n // NC], n % NC
                dve.wait_ge(w_hi_done, n + 1)
                dve.tensor_tensor(w_lo[w][:, c, :], px[n % 2][:], w_hi[w][:, c, :].bitcast(F32), ALU.subtract)\
                   .then_inc(w_lo_done, 1)
            dve.wait_ge(w_turned, len(weights) * NC + 1)
            dve.tensor_copy(router_t[:], px[0][:, 0:NC * LOGITS].rearrange("p (c n) -> p c n", c=NC)).then_inc(w_lo_done, 1)
            dve.wait_ge(credits_given, 1)
            for b in range(TB):
                norm1_stats(b, 0)
            for b in range(TB):
                norm1_rows(b, 0)
            for b in range(TB):
                xt_split(b, 0, px[b % 2])
            dve.wait_ge(bias_in, 64)
            dve.wait_ge(ones_ready, 1)
            dve.wait_ge(k_zeroed, 4)

            def q_split(c, i):
                dve.wait_ge(*q_hi_done.done(c, i))
                dve.scalar_tensor_tensor(out=q_lo[c % 2][:], in0=bank("q", c)[:], scalar=bias_qk[:, 0, c:c + 1],
                                         in1=q_hi[c % 2][:].bitcast(F32), op0=ALU.add, op1=ALU.subtract)\
                   .then_inc(*q_lo_done.inc())

            def k_split(c, i):
                dve.wait_ge(*k_hi_done.done(c, i))
                for r in range(4):
                    rows = slice(r * HD, (r + 1) * HD)
                    x = dve.scalar_tensor_tensor(out=k_lo[c % 2][rows, :, r, :],
                                                 in0=bank("k", c)[rows, :].rearrange("p (b k) -> p b k", k=P),
                                                 scalar=bias_qk[rows, 1, c:c + 1],
                                                 in1=k_hi[c % 2][rows, :, r, :].bitcast(F32),
                                                 op0=ALU.add, op1=ALU.subtract)
                x.then_inc(*k_lo_done.inc())

            def group(i, more):
                q_split(0, i)
                k_split(0, i)
                for b in range(TB):
                    dve.wait_ge(*v_made.done(b, i))
                    dve.wait_ge(*av_made.done(UNITS - 1, i - 1))
                    dve.tensor_tensor(v_rows[:, b, :, 0:HD], bank("v", b)[:].rearrange("p (h d) -> p h d", d=HD),
                                      bias_v[:].rearrange("p (h d) -> p h d", d=HD), ALU.add).then_inc(*v_done.inc())
                for s in range(UNITS + 4):
                    if s < UNITS:
                        m = row_max[:, s % 2, :]
                        dve.wait_ge(*scored.done(s, i))
                        link(dve.reduce_max(m, score[s % 2][:], AX_X))
                        dve.wait_ge(*exp_done.done(s - 2, i))
                        dve.tensor_tensor(diff[s % 2][:], score[s % 2][:], m.unsqueeze(2).broadcast_to((P, NC, P)),
                                          ALU.subtract).then_inc(*diff_done.inc())
                    u = s - 4
                    if u >= 0:
                        c, b, inv = u // 4, u % 4, inv_sum[:, u % 2, :]
                        dve.wait_ge(*av_made.done(u, i))
                        link(dve.reciprocal(inv.unsqueeze(2), av[u % 2][:, :, HD:HD + 1]))
                        dve.wait_ge(*att_turned.done(b, i - 1))
                        dve.tensor_tensor(att[b][:, 4 * c:4 * c + 4, :], av[u % 2][:, :, 0:HD],
                                          inv.unsqueeze(2).broadcast_to((P, NC, HD)), ALU.mult).then_inc(*att_done.inc())
                    if s % 4 == 0 and s // 4 + 1 < NC:
                        q_split(s // 4 + 1, i)
                    if s % 4 == 2 and s // 4 + 1 < NC:
                        k_split(s // 4 + 1, i)
                    if more and s % 4 == 3 and s < UNITS:
                        norm1_stats(s // 4, i + 1)
                    if more and s % 4 == 0 and s >= 4:
                        norm1_rows(s // 4 - 1, i + 1)
                if more:
                    for b in range(TB):
                        xt_split(b, i + 1, bank("xt", b))
                for s in range(TB + 4):
                    if s < TB:
                        dve.wait_ge(*att_hi_done.done(s, i))
                        hi, lo = att_t[s % 2]
                        dve.tensor_tensor(lo[:], bank("ot", s)[:].rearrange("p (c n) -> p c n", c=NC),
                                          hi[:].bitcast(F32), ALU.subtract).then_inc(*att_lo_done.inc())
                    b = s - 1
                    if 0 <= b < TB:
                        dve.wait_ge(*o_made.done(b, i))
                        dve.wait_ge(*res_done.done(b, i))
                        dve.wait_ge(*h2_out.done(b - 2, i))
                        dve.wait_ge(*xn2_done.done(b - 2, i))
                        dve.tensor_tensor(h2[b % 2], bank("o", b)[:], res[b][:], ALU.add).then_inc(*h2_done.inc())
                        dve.wait_ge(*h2_done.done(b, i))
                        norm_stats(TB + b, h2[b % 2])
                    b = s - 2
                    if 0 <= b < TB:
                        dve.wait_ge(*xn2_out.done(b - 2, i))
                        dve.wait_ge(*xn2_turned.done(b - 2, i))
                        norm_rows(TB + b, i, h2[b % 2], xn2[b % 2][:]).then_inc(*xn2_done.inc())
                    b = s - 4
                    if 0 <= b < TB:
                        dve.wait_ge(*logits_made.done(b, i))
                        dve.tensor_copy(keep["logits"][:, bass.ds(i * TB + b, 1), :],
                                        bank("logit", b)[:, 0:LOGITS].unsqueeze(1)).then_inc(*logits_done.inc())

            with dve.Fori(0, last) as i:
                steps.enter(i, 2 * UNITS + 2 * TB * (2 + 3))
                group(i, True)
                steps.leave(last)
            group(last, False)

        @block.tensor
        def _(pe):
            pe.wait_ge(eye_ready, 1)

            def turn(dst, src, cols=P, rows=P):
                for c in range(NC):
                    x = pe.transpose(dst[:, c * rows:(c + 1) * rows], src(c), eye[0:rows, 0:rows])
                return x

            for n in range(len(weights) * NC):
                w, c = n // NC, n % NC
                if c == 0:
                    pe.wait_ge(w_in[w], 16)
                if n >= 2:
                    pe.wait_ge(w_lo_done, n - 1)
                turn(px[n % 2], lambda oc: w_raw[w % 2][:, oc, c * P:(c + 1) * P]).then_inc(w_turned, 1)
            pe.wait_ge(router_in, 32)
            pe.wait_ge(w_lo_done, len(weights) * NC - 1)
            turn(px[0], lambda c: router_raw[:, c * P:(c + 1) * P], rows=LOGITS).then_inc(w_turned, 1)
            pe.wait_ge(credits_given, 1)
            pe.wait_ge(w_lo_done, len(weights) * NC + 1)
            for b in range(TB):
                pe.wait_ge(*xn_done.done(b, 0))
                if b >= 2:
                    pe.wait_ge(*xt_lo_done.done(b - 2, 0))
                turn(px[b % 2], lambda c: xn[b][:, c * P:(c + 1) * P]).then_inc(*xn_turned.inc())

            def project(w, oc, i, made):
                pe.wait_ge(*bank_free(w, oc, i))
                for ic in range(NC):
                    x = split_product(pe, bank(w, oc)[:], [m[w][:, ic, oc * P:(oc + 1) * P] for m in (w_hi, w_lo)],
                                      [m[:, ic, :] for m in (xt_hi, xt_lo)], ic == 0, ic == NC - 1)
                x.then_inc(*made.inc())

            def group(i, more):
                pe.wait_ge(*xt_lo_done.done(TB - 1, i))
                project("q", 0, i, q_made)
                project("k", 0, i, k_made)
                for b in range(TB):
                    pe.wait_ge(*bank_free("v", b, i))
                    for ic in range(NC):
                        x = split_product(pe, bank("v", b)[:], [m[:, ic, b * P:(b + 1) * P] for m in (xt_hi, xt_lo)],
                                          [m["v"][:, ic, :] for m in (w_hi, w_lo)], ic == 0, ic == NC - 1)
                    x.then_inc(*v_made.inc())

                for s in range(UNITS + 3):
                    if s < UNITS:
                        c, b = s // 4, s % 4
                        if b == 0:
                            pe.wait_ge(*q_lo_done.done(c, i))
                            pe.wait_ge(*k_lo_done.done(c, i))
                        pe.wait_ge(*diff_done.done(s - 2, i))
                        split_product(pe, score[s % 2][:].rearrange("p h k -> p (h k)"),
                                      [m[c % 2][:, b * P:(b + 1) * P] for m in (q_hi, q_lo)],
                                      [m[c % 2][:, b, :, :].rearrange("p h k -> p (h k)") for m in (k_hi, k_lo)],
                                      True, True).then_inc(*scored.inc())
                    u = s - 2
                    if 0 <= u < UNITS:
                        pe.wait_ge(*prob_t_done.done(u - 2, i))
                        pe.wait_ge(*exp_done.done(u, i))
                        for r in range(4):
                            x = pe.transpose(pt[u % 2][:, r, :], prob[u % 2][:, r, :], eye[:])
                        x.then_inc(*prob_turned.inc())
                    u = s - 3
                    if 0 <= u < UNITS:
                        c, b = u // 4, u % 4
                        if c == 0:
                            pe.wait_ge(*v_done.done(b, i))
                        pe.wait_ge(*att_done.done(u - 2, i))
                        pe.wait_ge(*prob_t_done.done(u, i))
                        for r in range(4):
                            x = pe.matmul(av[u % 2][:, r, :], prob_t[u % 2][:, r, :], v_rows[:, b, 4 * c + r, :],
                                          start=True, stop=True)
                        x.then_inc(*av_made.inc())
                    if s % 4 == 0 and s // 4 + 1 < NC:
                        project("q", s // 4 + 1, i, q_made)
                    if s % 4 == 2 and s // 4 + 1 < NC:
                        project("k", s // 4 + 1, i, k_made)
                if more:
                    for b in range(TB):
                        pe.wait_ge(*xn_done.done(b, i + 1))
                        pe.wait_ge(*bank_free("xt", b, i))
                        turn(bank("xt", b), lambda c: xn[b][:, c * P:(c + 1) * P]).then_inc(*xn_turned.inc())
                for s in range(TB + 4):
                    if s < TB:
                        rows = att[s][:].rearrange("p h d -> p (h d)")
                        pe.wait_ge(*att_done.done(UNITS - TB + s, i))
                        pe.wait_ge(*bank_free("ot", s, i, more))
                        turn(bank("ot", s), lambda c: rows[:, c * P:(c + 1) * P]).then_inc(*att_turned.inc())
                    b = s - 1
                    if 0 <= b < TB:
                        pe.wait_ge(*bank_free("o", b, i, more))
                        pe.wait_ge(*att_lo_done.done(b, i))
                        for ic in range(NC):
                            x = split_product(pe, bank("o", b)[:], [m[:, ic, :] for m in att_t[b % 2]],
                                              [m["o"][:, ic, :] for m in (w_hi, w_lo)], ic == 0, ic == NC - 1)
                        x.then_inc(*o_made.inc())
                    b = s - 3
                    if 0 <= b < TB:
                        pe.wait_ge(*bank_free("x2t", b, i, more))
                        pe.wait_ge(*xn2_done.done(b, i))
                        turn(bank("x2t", b), lambda c: xn2[b % 2][:, c * P:(c + 1) * P]).then_inc(*xn2_turned.inc())
                    b = s - 4
                    if 0 <= b < TB:
                        pe.wait_ge(*bank_free("logit", b, i, more))
                        pe.wait_ge(*xn2_t_done.done(b, i))
                        for c in range(NC):
                            x = pe.matmul(bank("logit", b)[:, 0:LOGITS], xn2_t[b % 2][:, c, :], router_t[:, c, :],
                                          start=c == 0, stop=c == NC - 1)
                        x.then_inc(*logits_made.inc())

            with pe.Fori(0, last) as i:
                group(i, True)
            group(last, False)


def routing_phase(nc, new_sem, keep, io, scratch):
    logits, gates, slots = keep["logits"], keep["gates"], keep["slots"]
    tiles = logits.shape[1]
    slot_cols = keep["slot_token"].shape[1]
    slot_tiles = slot_cols // TB
    E = EXPERTS

    with ExitStack() as mem:
        def sb(name, shape, dt=F32):
            return mem.enter_context(nc.sbuf_tensor(name, shape, dt))

        def over_experts(x):
            return x.broadcast_to((P, tiles, E))

        shifted = sb("shifted", [P, tiles, E])
        expd = sb("expd", [P, tiles, E])
        probs = sb("probs", [P, tiles, E])
        row = sb("row", [P, tiles, 1])
        row_inv = sb("row_inv", [P, tiles, 1])
        first_of = sb("first_of", [P, 1, E])
        equal = sb("equal", [P, tiles, E])
        index = sb("index", [P, tiles, E])
        least = sb("least", [P, tiles, 1])
        rest = sb("rest", [P, tiles, E])
        chosen = [sb(f"chosen{k}", [P, tiles, E]) for k in range(TOPK)]
        either = sb("either", [P, tiles, E])
        before = sb("before", [P, P])
        ones = sb("ones", [P, P])
        totals = sb("totals", [P, tiles, E])
        run = [sb(f"run{n}", [P, 2 * tiles, E]) for n in range(2)]
        tile_run = [sb(f"tile_run{n}", [P, 2 * E]) for n in range(2)]
        count_int = sb("count_int", [P, E], I32)
        tiles_int = sb("tiles_int", [P, E], I32)
        tiles_of = sb("tiles_of", [P, E])
        base = sb("base", [P, 1, E])
        slot_of = sb("slot_of", [P, tiles, E])
        slot_f = sb("slot_f", [P, TOPK, tiles])
        slot_part = [sb(f"slot_part{n}", [P, TOPK, tiles], I32) for n in range(2)]
        slot_lo = sb("slot_lo", [P, TOPK * tiles])
        slot_hi = sb("slot_hi", [P, TOPK * tiles])
        int_iota = sb("int_iota", [P, P], I32)
        lane = sb("lane", [P, P])
        token_int = sb("token_int", [P, tiles], I32)
        token = sb("token", [P, tiles])
        under = sb("under", [P, slot_tiles, E])
        expert_f = sb("expert_f", [P, slot_tiles, 1])
        expert_int = keep["tile_expert"]
        hot_lo = [sb(f"hot_lo{n}", [P, P], F32R) for n in range(2)]
        hot_hi = [sb(f"hot_hi{n}", [P, slot_cols], F32R) for n in range(2)]
        rank_ps = mem.enter_context(nc.psum_tensor("rank_ps", [P, tiles * E], F32))
        total_ps = mem.enter_context(nc.psum_tensor("total_ps", [P, tiles * E], F32))
        slot_ps = mem.enter_context(nc.psum_tensor("slot_ps", [P, slot_cols], F32))

        iotas, ones_set, before_set, before_cut = (new_sem(n) for n in ("iotas", "ones_set", "before_set", "before_cut"))
        step = new_sem("route_step")
        shifted_done, exp_ready, either_done = new_sem("shifted_done"), new_sem("exp_ready"), new_sem("either_done")
        gate_done = new_sem("gate_done")
        ranked, hot_made, hot_used = new_sem("ranked"), new_sem("hot_made"), new_sem("hot_used")
        block = mem.enter_context(nc.Block())

        @block.gpsimd
        def _(pool):
            pool.memset(before[:], 0.0).then_inc(before_set, 1)
            pool.memset(ones[:], 1.0).then_inc(ones_set, 1)
            pool.iota(int_iota[:], pattern=[[1, P]], base=0, channel_multiplier=0).then_inc(iotas, 1)
            pool.iota(token_int[:], pattern=[[P, tiles]], base=0, channel_multiplier=1).then_inc(iotas, 1)
            pool.wait_ge(before_set, 1)
            pool.affine_select(out=before[:], in_=before[:], compare_op=ALU.is_ge, fill=1.0, base=0,
                               pattern=[[-1, P]], channel_multiplier=1).then_inc(before_cut, 1)

        @block.scalar
        def _(act):
            act.wait_ge(shifted_done, 1)
            act.activation(expd[:], shifted[:], ACT.Exp).then_inc(exp_ready, 1)
            act.activation(gates[:, :, TOPK:TOPK + 1], logits[:, :, E:E + 1], ACT.Sigmoid).then_inc(gate_done, 1)
            act.wait_ge(gate_done, 1)

        @block.tensor
        def _(pe):
            pe.wait_ge(either_done, 1)
            pe.wait_ge(before_cut, 1)
            pe.wait_ge(ones_set, 1)
            picked = either[:].rearrange("p t e -> p (t e)")
            pe.matmul(rank_ps[:], before[:], picked, start=True, stop=True).then_inc(ranked, 1)
            pe.matmul(total_ps[:], ones[:], picked, start=True, stop=True).then_inc(ranked, 1)
            n = TOPK * tiles
            pe.wait_ge(hot_made, 1)
            pe.matmul(slot_ps[:], hot_lo[0][:], hot_hi[0][:], start=True, stop=False).then_inc(hot_used, 1)
            for k in range(1, n):
                pe.wait_ge(hot_made, k + 1)
                pe.matmul(slot_ps[:], hot_lo[k % 2][:], hot_hi[k % 2][:], start=False, stop=k == n - 1).then_inc(hot_used, 1)

        @block.vector
        def _(dve):
            steps = Count(step)

            def link(ins):
                ins.then_inc(*steps.tick())
                dve.wait_ge(*steps.so_far())

            scores = logits[:, :, 0:E]
            link(dve.reduce_max(row[:], scores, AX_X))
            dve.tensor_tensor(shifted[:], scores, over_experts(row[:]), ALU.subtract).then_inc(shifted_done, 1)
            dve.wait_ge(iotas, 2)
            dve.tensor_copy(lane[:], int_iota[:]).then_inc(*steps.tick())
            dve.tensor_copy(token[:], token_int[:]).then_inc(*steps.tick())
            dve.tensor_scalar(first_of[:, 0, :], int_iota[:, 0:E], float(-E), None, ALU.add).then_inc(*steps.tick())
            for r in (*run, *tile_run):
                dve.memset(r[:], 0.0).then_inc(*steps.tick())
            dve.wait_ge(exp_ready, 1)
            link(dve.tensor_reduce(row[:], expd[:], AX_X, ALU.add))
            link(dve.reciprocal(row_inv[:], row[:]))
            link(dve.tensor_tensor(probs[:], expd[:], over_experts(row_inv[:]), ALU.mult))
            left = probs
            for k in range(TOPK):
                best = gates[:, :, k:k + 1]
                link(dve.reduce_max(best, left[:], AX_X))
                link(dve.tensor_tensor(equal[:], left[:], over_experts(best), ALU.is_equal))
                link(dve.tensor_tensor(index[:], equal[:], first_of[:].broadcast_to((P, tiles, E)), ALU.mult))
                link(dve.tensor_reduce(least[:], index[:], AX_X, ALU.min))
                link(dve.tensor_tensor(chosen[k][:], index[:], over_experts(least[:]), ALU.is_equal))
                if k == 0:
                    link(dve.scalar_tensor_tensor(out=rest[:], in0=chosen[k][:], scalar=-2.0, in1=probs[:],
                                                  op0=ALU.mult, op1=ALU.add))
                    left = rest
            dve.tensor_tensor(either[:], chosen[0][:], chosen[1][:], ALU.add).then_inc(either_done, 1)
            dve.wait_ge(ranked, 2)
            tot = total_ps[:].rearrange("p (t e) -> p t e", e=E)
            link(dve.tensor_copy(totals[:], tot))
            link(dve.tensor_copy(run[0][:, tiles:, :], totals[:]))
            cur, shift = 0, 1
            while shift < tiles:
                link(dve.tensor_tensor(run[1 - cur][:, tiles:, :], run[cur][:, tiles:, :],
                                       run[cur][:, tiles - shift:2 * tiles - shift, :], ALU.add))
                cur, shift = 1 - cur, 2 * shift
            through = run[cur][:, tiles:, :]
            link(dve.tensor_scalar(count_int[:], through[:, tiles - 1, :], float(GT - 1), None, ALU.add))
            link(dve.tensor_scalar(tiles_int[:], count_int[:], GT.bit_length() - 1, None, ALU.arith_shift_right))
            link(dve.tensor_copy(tiles_of[:], tiles_int[:]))
            link(dve.tensor_copy(tile_run[0][:, E:], tiles_of[:]))
            at, shift = 0, 1
            while shift < E:
                link(dve.tensor_tensor(tile_run[1 - at][:, E:], tile_run[at][:, E:],
                                       tile_run[at][:, E - shift:2 * E - shift], ALU.add))
                at, shift = 1 - at, 2 * shift
            ends = tile_run[at][:, E:]
            link(dve.tensor_tensor(base[:, 0, :], ends, tiles_of[:], ALU.subtract))
            link(dve.tensor_scalar(base[:, 0, :], base[:, 0, :], float(GT), None, ALU.mult))
            link(dve.tensor_tensor(slot_of[:], rank_ps[:].rearrange("p (t e) -> p t e", e=E), through, ALU.add))
            link(dve.tensor_tensor(slot_of[:], slot_of[:], totals[:], ALU.subtract))
            link(dve.tensor_tensor(slot_of[:], slot_of[:], base[:].broadcast_to((P, tiles, E)), ALU.add))
            for k in range(TOPK):
                link(dve.tensor_tensor(index[:], chosen[k][:], slot_of[:], ALU.mult))
                link(dve.tensor_reduce(slot_f[:, k, :].unsqueeze(2), index[:], AX_X, ALU.add))
            link(dve.tensor_copy(slots[:], slot_f[:]))
            link(dve.tensor_scalar(slot_part[0][:], slots[:], P - 1, None, ALU.bitwise_and))
            link(dve.tensor_scalar(slot_part[1][:], slots[:], P.bit_length() - 1, None, ALU.arith_shift_right))
            link(dve.tensor_copy(slot_lo[:], slot_part[0][:].rearrange("p k t -> p (k t)")))
            link(dve.tensor_copy(slot_hi[:], slot_part[1][:].rearrange("p k t -> p (k t)")))
            link(dve.tensor_tensor(under[:], ends.unsqueeze(1).broadcast_to((P, slot_tiles, E)),
                                   lane[:, 0:slot_tiles].unsqueeze(2).broadcast_to((P, slot_tiles, E)), ALU.is_le))
            link(dve.tensor_reduce(expert_f[:], under[:], AX_X, ALU.add))
            link(dve.tensor_scalar(expert_int[:], expert_f[:, :, 0], float(E - 1), None, ALU.min))
            for n in range(TOPK * tiles):
                if n >= 2:
                    dve.wait_ge(hot_used, n - 1)
                dve.tensor_scalar(hot_lo[n % 2][:], lane[:], slot_lo[:, n:n + 1], None, ALU.is_equal)
                dve.tensor_scalar(hot_hi[n % 2][:], lane[:, 0:slot_cols], slot_hi[:, n:n + 1],
                                  token[:, n % tiles:n % tiles + 1], ALU.is_equal, ALU.mult).then_inc(hot_made, 1)
            dve.wait_ge(hot_used, TOPK * tiles)
            link(dve.tensor_copy(keep["slot_token"][:], slot_ps[:]))


def ffn_phase(nc, new_sem, keep, io, scratch, shared):
    eye = keep["eye"]
    tag = "s" if shared else "e"
    inner = I_SH if shared else I_MOE
    NM = -(-inner // P)
    size = [min(P, inner - m * P) for m in range(NM)]
    tiles = (scratch["h2"].shape[0] // GT) if shared else keep["slot_token"].shape[1] // TB
    last = tiles - 1
    SQ = 2 * (I_SH // P)
    assert NM % 2 == 1

    with ExitStack() as mem:
        def sb(name, shape, dt=F32):
            return mem.enter_context(nc.sbuf_tensor(f"{tag}_{name}", shape, dt))

        def ps(name, shape):
            return mem.enter_context(nc.psum_tensor(f"{tag}_{name}", shape, F32))

        def stage(name, per, **kw):
            s = Stage(new_sem, f"{tag}_{name}", per, **kw)
            stages.append(s)
            return s

        stages = []
        if shared:
            gu_hi, gu_lo = keep["gu_hi"], keep["gu_lo"]
            dn_hi, dn_lo = sb("dn_hi", [P, NM, DIM], F32R), sb("dn_lo", [P, NM, DIM], F32R)
            dn_raw = [sb(f"dn_raw{n}", [P, DIM]) for n in range(2)]
        else:
            gu_hi, gu_lo = sb("gu_hi", [P, 2, NC, inner], F32R), sb("gu_lo", [P, 2, NC, inner], F32R)
            gu_raw = [sb(f"gu_raw{m}", [P, 2, NC, size[m]]) for m in range(NM)]
            dn_hi, dn_lo = sb("dn_hi", [P, NM, DIM], F32R), sb("dn_lo", [P, NM, DIM], F32R)
            dn_raw = [sb(f"dn_raw{m}", [P, DIM]) for m in range(NM)]
            sh_raw = [sb(f"sh_raw{n}", [P, NC, P]) for n in range(1)]
            rows_now = sb("rows_now", [P, TB], I32)
        x = [sb(f"x{b}", [P, DIM]) for b in range(TB)]
        xt_hi, xt_lo = sb("xt_hi", [P, NC, GT], F32R), sb("xt_lo", [P, NC, GT], F32R)
        silu = [sb(f"silu{n}", [P, GT]) for n in range(2)]
        act_f = [sb(f"act{n}", [P, GT]) for n in range(2)]
        act_hi = [sb(f"act_hi{n}", [P, GT], F32R) for n in range(2)]
        act_lo = [sb(f"act_lo{n}", [P, GT], F32R) for n in range(2)]
        out = [sb(f"out{n}", [P, DIM]) for n in range(2)]
        if shared:
            picked = [[sb(f"picked{k}{n}", [P, DIM]) for n in range(2)] for k in range(TOPK)]
            slots_now = sb("slots_now", [P, TOPK, TB], I32)
            gates_now = sb("gates_now", [P, TB, TOPK + 1])
        banks = [ps(f"bank{n}", [P, GT]) for n in range(4)]
        acc = [ps(f"acc{b}", [P, DIM]) for b in range(TB)]

        x_turned = stage("x_turned", TB)
        gate_made, up_made = stage("gate_made", NM), stage("up_made", NM)
        down_made = stage("down_made", NM)
        xt_hi_done = stage("xt_hi_done", TB)
        silu_done, act_hi_done = stage("silu_done", NM), stage("act_hi_done", NM)
        xt_lo_done = stage("xt_lo_done", TB)
        act_done, act_lo_done = stage("act_done", NM), stage("act_lo_done", NM)
        if shared:
            x_in = stage("x_in", TB, dma=True, lanes=TB)
            res_in = stage("res_in", TB, dma=True, lanes=2)
            picked_in = [stage(f"picked_in{k}", TB, dma=True, lanes=2, credit=False) for k in range(TOPK)]
            slots_copied, gates_copied = stage("slots_copied", 1), stage("gates_copied", 1)
            joined = [stage(f"joined{n}", TB) for n in range(1 + TOPK)]
            acc_read = joined[0]
            dn_in = [new_sem(f"s_dn_in{n}") for n in range(2)]
            dn_hi_ready, dn_lo_ready = new_sem("s_dn_hi_ready"), new_sem("s_dn_lo_ready")
        else:
            x_in = stage("x_in", TB, dma=True, lanes=TB, credit=False)
            acc_read = stage("acc_read", TB)
            gu_in = stage("gu_in", NM, dma=True, lanes=NM)
            gu_in.unit = 32
            dn_in = stage("dn_in", NM, dma=True, lanes=NM)
            gu_hi_done, gu_lo_done = stage("gu_hi_done", NM), stage("gu_lo_done", NM)
            dn_hi_done, dn_lo_done = stage("dn_hi_done", NM), stage("dn_lo_done", NM)
            sh_in = stage("sh_in", 1, dma=True)
            sh_hi_done, sh_lo_done = stage("sh_hi_done", 1), stage("sh_lo_done", 1)
            rows_copied = new_sem("e_rows_copied")
        out_sent = stage("out_sent", TB, dma=True, lanes=2)
        pool_go, sp_go = new_sem(f"{tag}_pool_go"), new_sem(f"{tag}_sp_go")
        credits_given = new_sem(f"{tag}_credits")

        uses = []
        for m in range(NM):
            first = 0 if m % 2 else 2
            uses += [(("gate", m), first, silu_done), (("up", m), first + 1, act_done)]
            if m == NM - 1:
                uses += [(("x", b), b % 2, xt_lo_done) for b in range(TB)]

        def bank(kind, n):
            return next(banks[w] for use, w, _ in uses if use == (kind, n))

        def bank_free(kind, n, i, more=True):
            own = [u for u in uses if more or u[0][0] != "x"]
            at = next(k for k, u in enumerate(own) if u[0] == (kind, n))
            where = own[at][1]
            if any(u[1] == where for u in own[:at]):
                (what, k), _, by = [u for u in own[:at] if u[1] == where][-1]
                back = 0
            else:
                (what, k), _, by = [u for u in uses if u[1] == where][-1]
                back = 1
            return by.done(k, i - back + (what == "x"))

        def gu_parts(which, m):
            if shared:
                q = which * NM + m
                return lambda ic: [w[:, q, ic, :] for w in (gu_hi, gu_lo)]
            return lambda ic: [w[:, which, ic, m * P:m * P + size[m]] for w in (gu_hi, gu_lo)]

        block = mem.enter_context(nc.Block())

        @block.sync
        def _(sp):
            for s in stages:
                s.credit(sp)
            sp.sem_inc(credits_given, 1)
            if shared:
                for m in range(NM):
                    if m >= 2:
                        sp.wait_ge(dn_lo_ready, m - 1)
                    sp.dma_start(dn_raw[m % 2][:], io["L0_ffn_Ws_down"][m * P:(m + 1) * P, :]).then_inc(dn_in[m % 2], 16)

                def load_x(i):
                    for b in range(TB):
                        sp.wait_ge(*x_turned.done(b, i - 1))
                        sp.dma_start(x[b][:], scratch["xn2"][bass.ds((i * TB + b) * P, P), :]).then_inc(*x_in.inc(b))

                def tile(i, more):
                    if more:
                        load_x(i + 1)
                    for b in range(TB):
                        rows = bass.ds((i * TB + b) * P, P)
                        sp.wait_ge(*out_sent.done(b - 2, i))
                        sp.dma_start(out[b % 2][:], scratch["h2"][rows, :]).then_inc(*res_in.inc(b))
                        if b >= 1:
                            send(b - 1, i)
                    send(TB - 1, i)

                def send(b, i):
                    sp.wait_ge(*joined[TOPK].done(b, i))
                    sp.dma_start(io["out"][bass.ds((i * TB + b) * P, P), :], out[b % 2][:]).then_inc(*out_sent.inc(b))

                load_x(0)
                with sp.Fori(0, last) as i:
                    tile(i, True)
                tile(last, False)
                for b in (TB - 2, TB - 1):
                    sp.wait_ge(*out_sent.done(b, last))
            else:
                def tile(j, more):
                    sp.sem_inc(sp_go, 1)
                    e = sp.value_load(keep["tile_expert"][0:1, bass.ds(j, 1)], min_val=0, max_val=EXPERTS - 1)
                    gu = io["L0_ffn_We_gate_up"][bass.ds(e, 1)].rearrange("a (c p) (w n) -> p (a w) c n", p=P, w=2)
                    dn = io["L0_ffn_We_down"][bass.ds(e, 1)].rearrange("a i n -> (a i) n")
                    for m in range(NM):
                        sp.wait_ge(*gu_lo_done.done(m, j - 1))
                        for w in range(2):
                            sp.dma_start(gu_raw[m][:, w, :, :], gu[:, w, :, m * P:m * P + size[m]])\
                              .then_inc(gu_in.sems[m], 16)
                    for m in range(NM):
                        sp.wait_ge(*dn_lo_done.done(m, j - 1))
                        sp.dma_start(dn_raw[m][0:size[m], :], dn[m * P:m * P + size[m], :]).then_inc(*dn_in.inc(m))
                    if more:
                        sp.wait_ge(*sh_lo_done.done(0, j - 1))
                        sp.dma_start(sh_raw[0][:], io["L0_ffn_Ws_gate_up"][:, bass.ds(j * P, P)]
                                     .rearrange("(c p) n -> p c n", p=P)).then_inc(*sh_in.inc())

                assert last == SQ
                with sp.Fori(0, last) as j:
                    tile(j, True)
                tile(last, False)

        @block.gpsimd
        def _(pool):
            if shared:
                with pool.Fori(0, tiles) as i:
                    pool.wait_ge(*joined[TOPK].done(TB - 1, i - 1))
                    pool.sem_inc(pool_go, 1)
                    pool.tensor_copy(slots_now[:], keep["slots"][:, :, bass.ds(i * TB, TB)]).then_inc(*slots_copied.inc())
                    pool.wait_ge(*slots_copied.done(0, i))
                    for b in range(TB):
                        pool.wait_ge(*joined[TOPK].done(b - 2, i))
                        pool.sem_inc(pool_go, 1)
                        for k in range(TOPK):
                            pool.indirect_dma_start(
                                out=picked[k][b % 2][:], out_offset=None, in_=scratch["expert_rows"],
                                in_offset=bass.IndirectOffsetOnAxis(ap=slots_now[:, k, b:b + 1].bitcast(U32), axis=0),
                            ).then_inc(*picked_in[k].inc(b))
            else:
                def gather(j):
                    pool.tensor_copy(rows_now[:], keep["slot_token"][:, bass.ds(j * TB, TB)]).then_inc(rows_copied, 1)
                    pool.wait_ge(rows_copied, j + 1)
                    pool.sem_inc(pool_go, 1)
                    for b in range(TB):
                        pool.indirect_dma_start(
                            out=x[b][:], out_offset=None, in_=scratch["xn2"],
                            in_offset=bass.IndirectOffsetOnAxis(ap=rows_now[:, b:b + 1].bitcast(U32), axis=0),
                        ).then_inc(*x_in.inc(b))

                pool.wait_ge(credits_given, 1)
                gather(0)
                with pool.Fori(1, tiles) as j:
                    for b in range(TB):
                        pool.wait_ge(*x_in.done(b, j - 1))
                    pool.wait_ge(*x_turned.done(TB - 1, j - 1))
                    pool.sem_inc(pool_go, 1)
                    gather(j)

        @block.scalar
        def _(act):
            act.preload_act_table(ACT.Silu)
            act.wait_ge(credits_given, 1)

            def x_split(b, i):
                act.wait_ge(*x_turned.done(b, i))
                act.wait_ge(*up_made.done(NM - 1, i - 1))
                act.activation(xt_hi[:, :, b * P:(b + 1) * P], bank("x", b)[:].rearrange("p (c n) -> p c n", c=NC),
                               ACT.Copy).then_inc(*xt_hi_done.inc())

            def gu_split(m, j):
                act.wait_ge(*gu_in.done(m, j))
                act.wait_ge(*up_made.done(m, j - 1))
                for w in range(2):
                    y = act.activation(gu_hi[:, w, :, m * P:m * P + size[m]], gu_raw[m][:, w, :, :], ACT.Copy)
                y.then_inc(*gu_hi_done.inc())

            def dn_split(m, j):
                act.wait_ge(*dn_in.done(m, j))
                act.wait_ge(*down_made.done(m, j - 1))
                act.activation(dn_hi[0:size[m], m, :], dn_raw[m][0:size[m], :], ACT.Copy).then_inc(*dn_hi_done.inc())

            if shared:
                for m in range(NM):
                    act.wait_ge(dn_in[m % 2], 16 * (m // 2 + 1))
                    act.activation(dn_hi[:, m, :], dn_raw[m % 2][:], ACT.Copy).then_inc(dn_hi_ready, 1)
            else:
                for m in range(NM):
                    gu_split(m, 0)
            for b in range(TB):
                x_split(b, 0)

            def tile(i, more):
                for m in range(NM):
                    n = size[m]
                    act.wait_ge(*gate_made.done(m, i))
                    act.wait_ge(*act_done.done(m - 2, i))
                    act.activation(silu[m % 2][0:n, :], bank("gate", m)[0:n, :], ACT.Silu).then_inc(*silu_done.inc())
                    act.wait_ge(*act_done.done(m, i))
                    act.wait_ge(*down_made.done(m - 2, i))
                    act.activation(act_hi[m % 2][0:n, :], act_f[m % 2][0:n, :], ACT.Copy).then_inc(*act_hi_done.inc())
                    if not shared:
                        if m == 0:
                            dn_split(0, i)
                            dn_split(1, i)
                        if m == 1:
                            dn_split(2, i)
                            if more:
                                act.wait_ge(*sh_in.done(0, i))
                                act.activation(keep["gu_hi"][:, bass.ds(i, 1), :, :].rearrange("p a c n -> p (a c) n"),
                                               sh_raw[0][:], ACT.Copy).then_inc(*sh_hi_done.inc())
                        if more:
                            gu_split(m, i + 1)
                if more:
                    for b in range(TB):
                        x_split(b, i + 1)
                if not shared:
                    for b in range(TB):
                        act.wait_ge(*down_made.done(NM - 1, i))
                        act.wait_ge(*out_sent.done(b - 2, i))
                        act.activation(out[b % 2][:], acc[b][:], ACT.Copy).then_inc(*acc_read.inc())
                        act.wait_ge(*acc_read.done(b, i))
                        act.dma_start(scratch["expert_rows"][bass.ds((i * TB + b) * P, P), :], out[b % 2][:])\
                           .then_inc(*out_sent.inc(b))

            with act.Fori(0, last) as i:
                tile(i, True)
            tile(last, False)
            if not shared:
                for b in (TB - 2, TB - 1):
                    act.wait_ge(*out_sent.done(b, last))

        @block.vector
        def _(dve):
            dve.wait_ge(credits_given, 1)

            def x_split(b, i):
                cols = slice(b * P, (b + 1) * P)
                dve.wait_ge(*xt_hi_done.done(b, i))
                dve.tensor_tensor(xt_lo[:, :, cols], bank("x", b)[:].rearrange("p (c n) -> p c n", c=NC),
                                  xt_hi[:, :, cols].bitcast(F32), ALU.subtract).then_inc(*xt_lo_done.inc())

            def gu_split(m, j):
                dve.wait_ge(*gu_hi_done.done(m, j))
                for w in range(2):
                    cols = slice(m * P, m * P + size[m])
                    y = dve.tensor_tensor(gu_lo[:, w, :, cols], gu_raw[m][:, w, :, :], gu_hi[:, w, :, cols].bitcast(F32),
                                          ALU.subtract)
                y.then_inc(*gu_lo_done.inc())

            def dn_split(m, j):
                n = size[m]
                dve.wait_ge(*dn_hi_done.done(m, j))
                dve.tensor_tensor(dn_lo[0:n, m, :], dn_raw[m][0:n, :], dn_hi[0:n, m, :].bitcast(F32), ALU.subtract)\
                   .then_inc(*dn_lo_done.inc())

            if shared:
                for m in range(NM):
                    dve.wait_ge(dn_hi_ready, m + 1)
                    dve.tensor_tensor(dn_lo[:, m, :], dn_raw[m % 2][:], dn_hi[:, m, :].bitcast(F32), ALU.subtract)\
                       .then_inc(dn_lo_ready, 1)
            else:
                for m in range(NM):
                    gu_split(m, 0)
            for b in range(TB):
                x_split(b, 0)

            def tile(i, more):
                if shared:
                    dve.wait_ge(*joined[TOPK].done(TB - 1, i - 1))
                    dve.tensor_copy(gates_now[:], keep["gates"][:, bass.ds(i * TB, TB), :]).then_inc(*gates_copied.inc())
                for m in range(NM):
                    n = size[m]
                    dve.wait_ge(*silu_done.done(m, i))
                    dve.wait_ge(*up_made.done(m, i))
                    dve.wait_ge(*act_lo_done.done(m - 2, i))
                    dve.tensor_tensor(act_f[m % 2][0:n, :], bank("up", m)[0:n, :], silu[m % 2][0:n, :], ALU.mult)\
                       .then_inc(*act_done.inc())
                    dve.wait_ge(*act_hi_done.done(m, i))
                    dve.tensor_tensor(act_lo[m % 2][0:n, :], act_f[m % 2][0:n, :], act_hi[m % 2][0:n, :].bitcast(F32),
                                      ALU.subtract).then_inc(*act_lo_done.inc())
                    if not shared:
                        if m == 0:
                            dn_split(0, i)
                            dn_split(1, i)
                        if m == 1:
                            dn_split(2, i)
                            if more:
                                block_now = bass.ds(i, 1)
                                dve.wait_ge(*sh_hi_done.done(0, i))
                                dve.tensor_tensor(keep["gu_lo"][:, block_now, :, :].rearrange("p a c n -> p (a c) n"),
                                                  sh_raw[0][:],
                                                  keep["gu_hi"][:, block_now, :, :].rearrange("p a c n -> p (a c) n")
                                                  .bitcast(F32), ALU.subtract).then_inc(*sh_lo_done.inc())
                        if more:
                            gu_split(m, i + 1)
                if more:
                    for b in range(TB):
                        x_split(b, i + 1)
                if shared:
                    dve.wait_ge(*gates_copied.done(0, i))
                    dve.wait_ge(*down_made.done(NM - 1, i))
                    for b in range(TB):
                        o = out[b % 2]
                        dve.wait_ge(*res_in.done(b, i))
                        dve.scalar_tensor_tensor(out=o[:], in0=acc[b][:], scalar=gates_now[:, b, TOPK:TOPK + 1], in1=o[:],
                                                 op0=ALU.mult, op1=ALU.add).then_inc(*joined[0].inc())
                        for k in range(TOPK):
                            dve.wait_ge(*picked_in[k].done(b, i))
                            dve.wait_ge(*joined[k].done(b, i))
                            dve.scalar_tensor_tensor(out=o[:], in0=picked[k][b % 2][:], scalar=gates_now[:, b, k:k + 1],
                                                     in1=o[:], op0=ALU.mult, op1=ALU.add).then_inc(*joined[k + 1].inc())

            with dve.Fori(0, last) as i:
                tile(i, True)
            tile(last, False)

        @block.tensor
        def _(pe):
            pe.wait_ge(credits_given, 1)

            def x_turn(b, i, free):
                pe.wait_ge(*x_in.done(b, i))
                pe.wait_ge(*free)
                for c in range(NC):
                    y = pe.transpose(bank("x", b)[:, c * P:(c + 1) * P], x[b][:, c * P:(c + 1) * P], eye[:])
                y.then_inc(*x_turned.inc())

            for b in range(TB):
                x_turn(b, 0, xt_lo_done.done(b - 2, 0))

            def tile(i, more):
                def down(m):
                    n = size[m]
                    if shared:
                        if isinstance(i, int) or m == NM - 1:
                            pass
                        pe.wait_ge(dn_lo_ready, m + 1)
                    else:
                        pe.wait_ge(*dn_lo_done.done(m, i))
                    pe.wait_ge(*act_lo_done.done(m, i))
                    for b in range(TB):
                        if m == 0:
                            pe.wait_ge(*acc_read.done(b, i - 1))
                        cols = slice(b * P, (b + 1) * P)
                        y = split_product(pe, acc[b][:], [a[m % 2][0:n, cols] for a in (act_hi, act_lo)],
                                          [w[0:n, m, :] for w in (dn_hi, dn_lo)], m == 0, m == NM - 1)
                    y.then_inc(*down_made.inc())

                pe.wait_ge(*xt_lo_done.done(TB - 1, i))
                for m in range(NM):
                    if not shared:
                        pe.wait_ge(*gu_lo_done.done(m, i))
                    for w, (kind, made) in enumerate((("gate", gate_made), ("up", up_made))):
                        parts = gu_parts(w, m)
                        pe.wait_ge(*bank_free(kind, m, i, more))
                        for ic in range(NC):
                            y = split_product(pe, bank(kind, m)[0:size[m], :], parts(ic),
                                              [a[:, ic, :] for a in (xt_hi, xt_lo)], ic == 0, ic == NC - 1)
                        y.then_inc(*made.inc())
                    if m >= 1:
                        down(m - 1)
                if more:
                    for b in range(TB):
                        x_turn(b, i + 1, bank_free("x", b, i))
                down(NM - 1)

            with pe.Fori(0, last) as i:
                tile(i, True)
            tile(last, False)


def program(nc, io):
    tokens = io["x"].shape[0] * io["x"].shape[1]
    assert io["x"].shape[1] == P
    slot_tiles = (tokens * TOPK + EXPERTS * (GT - 1)) // GT
    with ExitStack() as ctx:
        def new_sem(name):
            return ctx.enter_context(nc.semaphore(name))

        def sb(name, shape, dt=F32):
            return ctx.enter_context(nc.sbuf_tensor(name, shape, dt))

        scratch = {name: nc.dram_tensor(f"{name}_dram", (rows, DIM), F32, kind="Internal").ap()
                   for name, rows in (("h2", tokens), ("xn2", tokens), ("expert_rows", slot_tiles * GT))}
        keep = {
            "eye": sb("eye", [P, P]),
            "logits": sb("logits", [P, tokens // P, LOGITS]),
            "gates": sb("gates", [P, tokens // P, TOPK + 1]),
            "slots": sb("slots", [P, TOPK, tokens // P], I32),
            "slot_token": sb("slot_token", [P, slot_tiles * TB], I32),
            "tile_expert": sb("tile_expert", [P, slot_tiles], I32),
        }
        attention_phase(nc, new_sem, keep, io, scratch)
        routing_phase(nc, new_sem, keep, io, scratch)
        blocks = 2 * (I_SH // P)
        keep["gu_hi"] = sb("gu_hi", [P, blocks, NC, P], F32R)
        keep["gu_lo"] = sb("gu_lo", [P, blocks, NC, P], F32R)
        ffn_phase(nc, new_sem, keep, io, scratch, shared=False)
        ffn_phase(nc, new_sem, keep, io, scratch, shared=True)


_INS = ["x", "L0_tok_weight", "L0_attn_Wq", "L0_attn_bq", "L0_attn_Wk", "L0_attn_bk", "L0_attn_Wv", "L0_attn_bv",
        "L0_attn_Wout", "L0_attn_bout", "L0_ffn_W_router", "L0_ffn_W_sgate", "L0_ffn_Ws_gate_up", "L0_ffn_Ws_down",
        "L0_ffn_We_gate_up", "L0_ffn_We_down"]


def kernel(**inputs):
    import numpy as _np
    import concourse.bacc as _bacc
    from concourse import mybir as _mybir
    from concourse.bass_utils import run_bass_kernel_spmd as _run

    nc = _bacc.Bacc("TRN2", target_bir_lowering=False, num_devices=1)
    arrays, io = {}, {}
    for name in _INS:
        a = _np.ascontiguousarray(inputs[name])
        arrays[f"in_{name}_dram"] = a
        io[name] = nc.dram_tensor(f"in_{name}_dram", a.shape, _mybir.dt.from_np(a.dtype), kind="ExternalInput").ap()
    shape = (*inputs["x"].shape, DIM)
    out = nc.dram_tensor("out_0_dram", shape, _mybir.dt.float32, kind="ExternalOutput").ap()
    io["out"] = out.rearrange("s t d -> (s t) d")
    program(nc, io)
    r = _run(nc, [arrays], core_ids=[0])
    return r.results[0]["out_0_dram"]
```

```python
from contextlib import ExitStack

import concourse.bass as bass
from concourse import mybir

F32 = mybir.dt.float32
F32R = mybir.dt.float32r
I32 = mybir.dt.int32
U32 = mybir.dt.uint32
ACT = mybir.ActivationFunctionType
ALU = mybir.AluOpType
AX_X = mybir.AxisListType.X

P = 128
DIM = 512
NC = DIM // P
HEADS = 16
HD = DIM // HEADS
EXPERTS = 8
I_MOE = 352
I_SH = 1408
TOPK = 2
TB = 4
GT = TB * P
EPS = 1e-5
LOGITS = EXPERTS + 1


class Stage:

    def __init__(self, new_sem, name, per, dma=False, lanes=1, credit=True):
        assert per % lanes == 0
        self.credits = per // lanes if credit else 0
        self.per, self.lanes, self.unit = per, lanes, 16 if dma else 1
        self.sems = [new_sem(name if lanes == 1 else f"{name}{n}") for n in range(lanes)]

    def inc(self, n=0):
        return self.sems[n % self.lanes], self.unit

    def done(self, n, i=0):
        per = self.per // self.lanes
        return self.sems[n % self.lanes], (i * per + (self.credits + n // self.lanes + 1)) * self.unit

    def credit(self, eng):
        if self.credits:
            for s in self.sems:
                eng.sem_inc(s, self.credits * self.unit)


class Count:

    def __init__(self, sem):
        self.sem, self.base, self.lap, self.k = sem, 0, 0, 0

    def tick(self):
        self.k += 1
        return self.sem, 1

    def so_far(self):
        return self.sem, self.base + self.lap + self.k

    def enter(self, i, per):
        self.base, self.lap, self.k, self.per = self.base + self.k, i * per, 0, per

    def leave(self, n):
        assert self.k == self.per, (self.sem, self.k)
        self.base, self.lap, self.k = self.base + n * self.per, 0, 0


def split_product(pe, out, stationary, moving, first, last):
    (sh, sl), (mh, ml) = stationary, moving
    pe.matmul(out, sh, mh, start=first, stop=False)
    pe.matmul(out, sh, ml, start=False, stop=False)
    return pe.matmul(out, sl, mh, start=False, stop=last)


def attention_phase(nc, new_sem, keep, io, scratch):
    x_ids, table = io["x"], io["L0_tok_weight"]
    groups = x_ids.shape[0] // TB
    last = groups - 1
    SCALE = float(HD) ** -0.5

    with ExitStack() as mem:
        def sb(name, shape, dt=F32):
            return mem.enter_context(nc.sbuf_tensor(name, shape, dt))

        def ps(name, shape):
            return mem.enter_context(nc.psum_tensor(name, shape, F32))

        def stage(name, per, **kw):
            s = Stage(new_sem, name, per, **kw)
            stages.append(s)
            return s

        stages = []
        eye = keep["eye"]
        weights = {"q": "L0_attn_Wq", "k": "L0_attn_Wk", "v": "L0_attn_Wv", "o": "L0_attn_Wout"}
        w_hi = {w: sb(f"w_{w}_hi", [P, NC, DIM], F32R) for w in weights}
        w_lo = {w: sb(f"w_{w}_lo", [P, NC, DIM], F32R) for w in weights}
        arena = sb("arena", [P, 2 * NC, DIM])
        w_raw = [arena[:, n * NC:(n + 1) * NC, :] for n in range(2)]
        router_t = sb("router_t", [P, NC, LOGITS])
        bias_in_t = sb("bias_in_t", [P, 3, NC])
        bias_q = sb("bias_q", [P, NC])
        bias_o = sb("bias_o", [P, DIM])
        ids = sb("ids", [P, groups * TB], I32)
        ids_now, ids_then = sb("ids_now", [P, TB], I32), sb("ids_then", [P, TB], I32)

        h = [sb(f"h{b}", [P, DIM]) for b in range(TB)]
        res = [sb(f"res{b}", [P, DIM]) for b in range(TB)]
        xt_hi = sb("xt_hi", [P, NC, GT], F32R)
        xt_lo = sb("xt_lo", [P, NC, GT], F32R)
        q_hi, q_lo = ([sb(f"q_{part}{n}", [P, GT], F32R) for n in range(2)] for part in ("hi", "lo"))
        k_parts = [sb(f"k_parts{n}", [P, 2, TB, P], F32R) for n in range(2)]
        k_diag = [sb(f"k_diag{n}", [P, 2, TB, 4, P], F32R) for n in range(2)]
        v_rows = sb("v_rows", [P, TB, HEADS, HD + 1])
        stats = sb("stats", [P, 2 * TB, 6])
        mean_var = sb("mean_var", [P, 2 * TB, 2])
        small = sb("small", [P, 2 * TB, 6])
        minus_max = sb("minus_max", [P, 2, 4])
        prob, prob_t = ([arena[:, m + n, :].rearrange("p (h k) -> p h k", k=P) for n in range(2)] for m in (0, 2))
        xn2 = [arena[:, 4 + n, :] for n in range(2)]
        xn2_t = [arena[:, 6 + n, :].rearrange("p (c n) -> p c n", c=NC) for n in range(2)]
        inv_sum = sb("inv_sum", [P, 2, 4])
        att = [sb(f"att{b}", [P, HEADS, HD]) for b in range(TB)]
        att_t = [(sb(f"att_t_hi{b}", [P, NC, P], F32R), sb(f"att_t_lo{b}", [P, NC, P], F32R)) for b in range(TB)]
        router_raw = att[0][0:LOGITS].rearrange("p h d -> p (h d)")

        px = [ps(f"px{n}", [P, DIM]) for n in range(2)]
        score = [ps(f"score{n}", [P, 4, P]) for n in range(2)]
        pt = [ps(f"pt{n}", [P, 4, P]) for n in range(2)]
        av = [ps(f"av{n}", [P, 4, HD + 1]) for n in range(2)]

        UNITS = NC * TB

        h_in = stage("h_in", TB, dma=True, lanes=TB, credit=False)
        res_in = stage("res_in", TB, dma=True, lanes=TB, credit=False)
        ids_copied = stage("ids_copied", 1)
        res_done = stage("res_done", TB)
        xn_turned = stage("xn_turned", TB)
        q_made, k_made, v_made = stage("q_made", NC), stage("k_made", NC), stage("v_made", TB)
        scored = stage("scored", UNITS)
        prob_turned = stage("prob_turned", UNITS)
        av_made = stage("av_made", UNITS)
        att_turned = stage("att_turned", TB)
        o_made = stage("o_made", TB)
        xn2_turned = stage("xn2_turned", TB)
        logits_made = stage("logits_made", TB)
        xt_hi_done = stage("xt_hi_done", TB)
        q_hi_done, k_hi_done, v_done = stage("q_hi_done", NC), stage("k_hi_done", NC), stage("v_done", TB)
        exp_done = stage("exp_done", UNITS)
        prob_t_done = stage("prob_t_done", UNITS)
        att_hi_done = stage("att_hi_done", TB)
        xn2_t_done = stage("xn2_t_done", TB)
        y0_done = [stage(f"y0_done{n}", TB) for n in (1, 2)]
        var_done = [stage(f"var_done{n}", TB) for n in (1, 2)]
        xn_done = stage("xn_done", TB)
        xt_lo_done = stage("xt_lo_done", TB)
        q_lo_done, k_lo_done = stage("q_lo_done", NC), stage("k_lo_done", NC)
        max_done = stage("max_done", UNITS)
        att_done = stage("att_done", UNITS)
        att_lo_done = stage("att_lo_done", TB)
        h2_done = stage("h2_done", TB)
        xn2_done = stage("xn2_done", TB)
        logits_done = stage("logits_done", TB)
        k_spread = stage("k_spread", NC, dma=True, lanes=2)
        k_spread.unit = 4 * 16
        h2_out = stage("h2_out", TB, dma=True, lanes=TB)
        xn2_out = stage("xn2_out", TB, dma=True, lanes=2)

        credits_given = new_sem("credits_given")
        eye_zeroed, eye_ready, ones_ready = new_sem("eye_zeroed"), new_sem("eye_ready"), new_sem("ones_ready")
        k_zeroed = new_sem("k_zeroed")
        w_in = [new_sem(f"w_in_{w}") for w in weights]
        router_in, bias_in, ids_in = new_sem("router_in"), new_sem("bias_in"), new_sem("ids_in")
        pool_go, sp_go = keep["pool_go"], keep["sp_go"]
        w_turned, w_hi_done, w_lo_done = new_sem("w_turned"), new_sem("w_hi_done"), new_sem("w_lo_done")
        bv_hi_done, bv_lo_done, bias_made, bias_done = (new_sem(n) for n in ("bv_hi_done", "bv_lo_done", "bias_made", "bias_done"))
        dve_step, dve_go, act_step = new_sem("dve_step"), new_sem("dve_go"), new_sem("act_step")

        FILL = {
            0: [("v", 0), ("k", 1)], 1: [("ot", 0), ("v", 1), ("q", 1)], 2: [("ot", 1), ("v", 2)], 3: [("ot", 2), ("v", 3)],
            4: [("ot", 3), ("k", 2)], 5: [("q", 2)], 6: [("o", 0)], 7: [("o", 1)],
            8: [("x2t", 0), ("k", 3)], 9: [("x2t", 1), ("logit", 0), ("q", 3)],
            10: [("logit", 1)] + [("xt", b) for b in range(TB)], 11: [("o", 2)],
            12: [("k", 0), ("o", 3)], 13: [("x2t", 2), ("q", 0)], 14: [("x2t", 3), ("logit", 2)], 15: [("logit", 3)],
        }
        OF_NEXT = {("q", 0), ("k", 0)} | {("xt", b) for b in range(TB)}
        OF_BEFORE = ("ot", "o", "x2t", "logit")
        H2_ROWS = {7: 0, 8: 1, 12: 2, 13: 3}
        NORM1_STATS = {3: 0, 4: 1, 5: 2, 6: 3}
        NORM1_ROWS = {5: 0, 6: 1, 7: 2, 8: 3}
        drained_by = {"q": q_lo_done, "k": k_lo_done, "v": v_done, "xt": xt_lo_done, "ot": att_lo_done, "o": h2_done,
                      "x2t": xn2_t_done, "logit": logits_done}
        every_use = [use for s in range(UNITS) for use in FILL[s]]
        assert len(every_use) % 2 == 0

        def group_of(use, i):
            return i + 1 if use in OF_NEXT else i - 1 if use[0] in OF_BEFORE else i

        def uses_of(own, more, before):
            return [u for u in every_use if (before if u[0] in OF_BEFORE else more if u in OF_NEXT else own)]

        def fill(s, own, more, before):
            return [u for u in FILL[s] if u in uses_of(own, more, before)]

        def bank(use):
            return px[every_use.index(use) % 2]

        def bank_free(use, i, flags, flags_before):
            now, then = uses_of(*flags), uses_of(*flags_before)
            same = [u for u in now[:now.index(use)] if bank(u) is bank(use)]
            if same:
                return drained_by[same[-1][0]].done(same[-1][1], group_of(same[-1], i))
            prior = [u for u in then if bank(u) is bank(use)][-1]
            return drained_by[prior[0]].done(prior[1], group_of(prior, i - 1))

        FIRST, MIDDLE, FINAL, TAIL = (True, True, False), (True, True, True), (True, False, True), (False, False, True)

        def chunks(t):
            return t.rearrange("p (c n) -> p c n", c=NC)

        block = mem.enter_context(nc.Block())

        @block.sync
        def _(sp):
            for n, w in enumerate(weights):
                if n >= 2:
                    sp.wait_ge(w_turned, NC * (n - 1))
                sp.dma_start(w_raw[n % 2], io[weights[w]].rearrange("(c p) n -> p c n", p=P)).then_inc(w_in[n], 16)
                if n == 1:
                    with nc.allow_non_contiguous_dma(reason="token ids and biases, one per partition"):
                        sp.dma_start(ids[:], x_ids.rearrange("b p -> p b")).then_inc(ids_in, 16)
                        for m, name in enumerate(("L0_attn_bq", "L0_attn_bk", "L0_attn_bv")):
                            sp.dma_start(bias_in_t[:, m, :], io[name].rearrange("(c p) -> p c", p=P)).then_inc(bias_in, 16)
                    sp.dma_start(bias_o[:], io["L0_attn_bout"].rearrange("(a d) -> a d", a=1).broadcast_to((P, DIM)))\
                      .then_inc(bias_in, 16)
                    sp.dma_start(router_raw[0:EXPERTS, :], io["L0_ffn_W_router"]).then_inc(router_in, 16)
                    sp.dma_start(router_raw[EXPERTS:LOGITS, :], io["L0_ffn_W_sgate"]).then_inc(router_in, 16)
                    for s in stages:
                        s.credit(sp)
                    sp.sem_inc(credits_given, 1)
            sp.wait_ge(k_zeroed, 2)

            def wait(sem, count):
                sp.wait_ge(sem, count)
                sp.sem_inc(sp_go, 1)

            def spread(c, i):
                wait(*k_lo_done.done(c, i))
                wait(*scored.done(c * TB - TB - 1, i))
                for r in range(4):
                    rows = slice(r * HD, (r + 1) * HD)
                    sp.dma_start(k_diag[c % 2][rows, :, :, r, :].bitcast(F32), k_parts[c % 2][rows].bitcast(F32))\
                      .then_inc(k_spread.sems[c % 2], 16)

            def group(i, flags):
                own, more, before = flags
                for s in range(UNITS):
                    for use in fill(s, *flags):
                        if use[0] == "k":
                            spread(use[1], group_of(use, i))
                        if use[0] == "o":
                            b = use[1]
                            wait(*h2_done.done(b, i - 1))
                            sp.dma_start(scratch["h2"][bass.ds(((i - 1) * TB + b) * P, P), :], res[b][:])\
                              .then_inc(*h2_out.inc(b))
                    if before and s in H2_ROWS:
                        b = H2_ROWS[s]
                        wait(*xn2_done.done(b, i - 1))
                        sp.dma_start(scratch["xn2"][bass.ds(((i - 1) * TB + b) * P, P), :], xn2[b % 2])\
                          .then_inc(*xn2_out.inc(b))

            spread(0, 0)
            group(0, FIRST)
            with sp.Fori(1, last) as i:
                group(i, MIDDLE)
            group(last, FINAL)
            group(groups, TAIL)
            for b in range(TB):
                sp.wait_ge(*h2_out.done(b, last))
                sp.wait_ge(*xn2_out.done(b, last))

        @block.gpsimd
        def _(pool):
            pool.memset(eye[:], 0.0).then_inc(eye_zeroed, 1)
            pool.wait_ge(eye_zeroed, 1)
            pool.affine_select(out=eye[:], in_=eye[:], compare_op=ALU.not_equal, fill=1.0, base=0,
                               pattern=[[-1, P]], channel_multiplier=1).then_inc(eye_ready, 1)
            pool.wait_ge(credits_given, 1)
            pool.wait_ge(ids_in, 16)

            def gather(ids_tile, b, dst, inc):
                pool.indirect_dma_start(
                    out=dst, out_offset=None, in_=table,
                    in_offset=bass.IndirectOffsetOnAxis(ap=ids_tile[:, b:b + 1].bitcast(U32), axis=0)).then_inc(*inc)

            def group(i, more, before):
                if more:
                    pool.wait_ge(*xn_turned.done(TB - 1, i))
                if before:
                    for b in range(TB):
                        pool.wait_ge(*h2_out.done(b, i - 2))
                        pool.wait_ge(*xn2_done.done(b, i - 2))
                pool.sem_inc(pool_go, 1)
                if more:
                    pool.tensor_copy(ids_now[:], ids[:, bass.ds((i + 1) * TB, TB)])
                if before:
                    pool.tensor_copy(ids_then[:], ids[:, bass.ds((i - 1) * TB, TB)])
                pool.drain().then_inc(*ids_copied.inc())
                pool.wait_ge(*ids_copied.done(0, i + 1))
                pool.sem_inc(pool_go, 1)
                if more:
                    for b in range(TB):
                        gather(ids_now, b, h[b][:], h_in.inc(b))
                if before:
                    for b in range(TB):
                        gather(ids_then, b, res[b][:], res_in.inc(b))
                if more:
                    for b in range(TB):
                        pool.wait_ge(*h_in.done(b, i + 1))
                if before:
                    for b in range(TB):
                        pool.wait_ge(*res_in.done(b, i - 1))
                        pool.tensor_tensor(res[b][:], res[b][:], bias_o[:], ALU.add).then_inc(*res_done.inc())

            pool.tensor_copy(ids_now[:], ids[:, 0:TB]).then_inc(*ids_copied.inc())
            pool.wait_ge(*ids_copied.done(0, 0))
            for b in range(TB):
                gather(ids_now, b, h[b][:], h_in.inc(b))
            for tile in k_diag:
                pool.memset(tile[:].bitcast(F32), 0.0).then_inc(k_zeroed, 1)
            pool.memset(v_rows[:, :, :, HD:HD + 1], 1.0).then_inc(ones_ready, 1)
            for b in range(TB):
                pool.wait_ge(*h_in.done(b, 0))
            group(0, True, False)
            pool.wait_ge(bias_done, 1)
            with pool.Fori(1, last) as i:
                group(i, True, True)
            group(last, False, True)
            group(groups, False, True)

        @block.scalar
        def _(act):
            act.preload_act_table_set("natural_log_exp_and_others")
            steps = Count(act_step)

            def rsqrt(slot, i):
                act.wait_ge(*var_done[slot // TB].done(slot % TB, i))
                act.activation(small[:, slot, 1:2], small[:, slot, 0:1], ACT.Ln).then_inc(*steps.tick())
                act.wait_ge(*steps.so_far())
                act.activation(small[:, slot, 2:3], small[:, slot, 1:2], ACT.Exp, scale=-0.5)\
                   .then_inc(*y0_done[slot // TB].inc())

            def xt_split(b, i, src):
                act.wait_ge(*xn_turned.done(b, i))
                act.wait_ge(*q_made.done(NC - 1, i - 1))
                act.activation(xt_hi[:, :, b * P:(b + 1) * P], chunks(src[:]), ACT.Copy).then_inc(*xt_hi_done.inc())

            def drain(use, i, src):
                kind, n = use
                if kind == "q":
                    act.wait_ge(*q_made.done(n, i))
                    act.wait_ge(*scored.done(n * TB - TB - 1, i))
                    act.activation(q_hi[n % 2][:], src[:], ACT.Identity, bias=bias_q[:, n:n + 1]).then_inc(*q_hi_done.inc())
                elif kind == "k":
                    act.wait_ge(*k_made.done(n, i))
                    act.wait_ge(*k_spread.done(n - 2, i))
                    act.activation(k_parts[n % 2][:, 0, :, :].rearrange("p b k -> p (b k)"), src[:], ACT.Identity,
                                   bias=bias_in_t[:, 1, n:n + 1]).then_inc(*k_hi_done.inc())
                elif kind == "v":
                    act.wait_ge(*v_made.done(n, i))
                    act.wait_ge(*av_made.done(UNITS - TB + n, i - 1))
                    act.activation(v_rows[:, n, :, 0:HD], src[:].rearrange("p (h d) -> p h d", d=HD), ACT.Copy)\
                       .then_inc(*v_done.inc())
                elif kind == "xt":
                    xt_split(n, i, src)
                elif kind == "ot":
                    act.wait_ge(*att_turned.done(n, i))
                    act.wait_ge(*o_made.done(n, i - 1))
                    act.activation(att_t[n][0][:], chunks(src[:]), ACT.Copy).then_inc(*att_hi_done.inc())
                elif kind == "o":
                    rsqrt(TB + n, i)
                elif kind == "x2t":
                    act.wait_ge(*xn2_turned.done(n, i))
                    act.wait_ge(*logits_made.done(n - 2, i))
                    act.activation(xn2_t[n % 2], chunks(src[:]), ACT.Copy).then_inc(*xn2_t_done.inc())

            act.wait_ge(bias_in, 64)
            act.activation(bias_q[:], bias_in_t[:, 0, :], ACT.Copy, scale=SCALE).then_inc(*steps.tick())
            act.wait_ge(*steps.so_far())
            for n in range(len(weights) * NC):
                w = "qkvo"[n // NC]
                act.wait_ge(w_turned, n + 1)
                act.activation(w_hi[w][:, n % NC, :], px[n % 2][:], ACT.Copy, scale=SCALE if w == "q" else 1.0)\
                   .then_inc(w_hi_done, 1)
            act.activation(xt_hi[:, :, 0:P], bias_in_t[:, 2, :].unsqueeze(2).broadcast_to((P, NC, P)), ACT.Copy)\
               .then_inc(bv_hi_done, 1)
            act.wait_ge(k_zeroed, 2)
            act.wait_ge(ones_ready, 1)
            act.wait_ge(credits_given, 1)
            for b in range(TB):
                rsqrt(b, 0)
            act.wait_ge(bias_made, 1)
            for b in range(TB):
                xt_split(b, 0, px[b % 2])
            drain(("q", 0), 0, px[0])
            drain(("k", 0), 0, px[1])

            def group(i, flags, carry=True):
                own, more, before = flags
                for s in range(UNITS):
                    if own:
                        act.wait_ge(*scored.done(s, i))
                        act.wait_ge(*max_done.done(s, i))
                        act.wait_ge(*prob_turned.done(s - 2, i))
                        for r in range(4):
                            x = act.activation(prob[s % 2][:, r, :], score[s % 2][:, r, :], ACT.Exp,
                                               bias=minus_max[:, s % 2, r:r + 1])
                        x.then_inc(*exp_done.inc())
                    u = s - 2
                    if (u >= 0 and own) or (u < 0 and carry):
                        act.wait_ge(*prob_turned.done(u, i))
                        act.wait_ge(*av_made.done(u - 2, i))
                        act.activation(prob_t[u % 2], pt[u % 2][:], ACT.Copy).then_inc(*prob_t_done.inc())
                    for use in fill(s, *flags):
                        drain(use, group_of(use, i), bank(use))
                    if more and s in NORM1_STATS:
                        rsqrt(NORM1_STATS[s], i + 1)

            group(0, FIRST, carry=False)
            with act.Fori(1, last) as i:
                steps.enter(i - 1, 2 * TB)
                group(i, MIDDLE)
                steps.leave(last - 1)
            group(last, FINAL)
            group(groups, TAIL)

        @block.vector
        def _(dve):
            steps = Count(dve_step)

            def link(ins):
                ins.then_inc(*steps.tick())
                dve.wait_ge(*steps.so_far())

            def norm_stats(slot, src):
                dve.bn_stats(stats[:, slot, :], src).then_inc(*steps.tick())
                dve.wait_ge(*steps.so_far())
                dve.sem_inc(dve_go, 1)
                link(dve.bn_aggr(mean_var[:, slot, :], stats[:, slot, :]))
                dve.tensor_scalar(small[:, slot, 0:1], mean_var[:, slot, 1:2], EPS, None, ALU.add)\
                   .then_inc(*var_done[slot // TB].inc())

            def norm_rows(slot, i, src, dst):
                s = small[:, slot, :]
                dve.wait_ge(*y0_done[slot // TB].done(slot % TB, i))
                link(dve.scalar_tensor_tensor(out=s[:, 3:4], in0=s[:, 2:3], scalar=s[:, 0:1], in1=s[:, 2:3],
                                              op0=ALU.mult, op1=ALU.mult))
                link(dve.tensor_scalar(s[:, 4:5], s[:, 3:4], -0.5, 1.5, ALU.mult, ALU.add))
                link(dve.tensor_tensor(s[:, 5:6], s[:, 2:3], s[:, 4:5], ALU.mult))
                return dve.tensor_scalar(dst, src, mean_var[:, slot, 0:1], s[:, 5:6], ALU.subtract, ALU.mult)

            def norm1_stats(b, i):
                dve.wait_ge(*h_in.done(b, i))
                norm_stats(b, h[b][:])

            def norm1_rows(b, i):
                norm_rows(b, i, h[b][:], h[b][:]).then_inc(*xn_done.inc())

            def lo_part(src, hi, lo, inc):
                dve.tensor_tensor(lo, src, hi.bitcast(F32), ALU.subtract).then_inc(*inc)

            def drain(use, i, src):
                kind, n = use
                if kind == "q":
                    dve.wait_ge(*q_hi_done.done(n, i))
                    dve.scalar_tensor_tensor(out=q_lo[n % 2][:], in0=src[:], scalar=bias_q[:, n:n + 1],
                                             in1=q_hi[n % 2][:].bitcast(F32), op0=ALU.add, op1=ALU.subtract)\
                       .then_inc(*q_lo_done.inc())
                elif kind == "k":
                    hi, lo = (k_parts[n % 2][:, m, :, :].rearrange("p b k -> p (b k)") for m in range(2))
                    dve.wait_ge(*k_hi_done.done(n, i))
                    dve.scalar_tensor_tensor(out=lo, in0=src[:], scalar=bias_in_t[:, 1, n:n + 1], in1=hi.bitcast(F32),
                                             op0=ALU.add, op1=ALU.subtract).then_inc(*k_lo_done.inc())
                elif kind == "xt":
                    cols = slice(n * P, (n + 1) * P)
                    dve.wait_ge(*xt_hi_done.done(n, i))
                    lo_part(chunks(src[:]), xt_hi[:, :, cols], xt_lo[:, :, cols], xt_lo_done.inc())
                elif kind == "ot":
                    dve.wait_ge(*att_hi_done.done(n, i))
                    lo_part(chunks(src[:]), att_t[n][0][:], att_t[n][1][:], att_lo_done.inc())
                elif kind == "o":
                    dve.wait_ge(*o_made.done(n, i))
                    dve.wait_ge(*res_done.done(n, i))
                    dve.tensor_tensor(res[n][:], src[:], res[n][:], ALU.add).then_inc(*h2_done.inc())
                    dve.wait_ge(*h2_done.done(n, i))
                    norm_stats(TB + n, res[n][:])
                elif kind == "logit":
                    dve.wait_ge(*logits_made.done(n, i))
                    dve.tensor_copy(keep["logits"][:, bass.ds(i * TB + n, 1), :], src[:, 0:LOGITS].unsqueeze(1))\
                       .then_inc(*logits_done.inc())

            for n in range(len(weights) * NC):
                w, c = "qkvo"[n // NC], n % NC
                dve.wait_ge(w_hi_done, n + 1)
                dve.scalar_tensor_tensor(out=w_lo[w][:, c, :], in0=px[n % 2][:], scalar=SCALE if w == "q" else 1.0,
                                         in1=w_hi[w][:, c, :].bitcast(F32), op0=ALU.mult, op1=ALU.subtract)\
                   .then_inc(w_lo_done, 1)
            dve.wait_ge(w_turned, len(weights) * NC + 1)
            dve.tensor_copy(router_t[:], px[0][:, 0:NC * LOGITS].rearrange("p (c n) -> p c n", c=NC)).then_inc(w_lo_done, 1)
            dve.wait_ge(bv_hi_done, 1)
            dve.wait_ge(bias_in, 64)
            lo_part(bias_in_t[:, 2, :].unsqueeze(2).broadcast_to((P, NC, P)), xt_hi[:, :, 0:P], xt_lo[:, :, 0:P],
                    (bv_lo_done, 1))
            dve.wait_ge(credits_given, 1)
            for b in range(TB):
                norm1_stats(b, 0)
            dve.wait_ge(bias_made, 1)
            dve.tensor_tensor(bias_o[:], px[1][:], bias_o[:], ALU.add).then_inc(bias_done, 1)
            for b in range(TB):
                norm1_rows(b, 0)
            for b in range(TB):
                drain(("xt", b), 0, px[b % 2])
            drain(("q", 0), 0, px[0])
            drain(("k", 0), 0, px[1])

            def group(i, flags, carry=True):
                own, more, before = flags
                for s in range(UNITS):
                    if own:
                        dve.wait_ge(*scored.done(s, i))
                        dve.wait_ge(*exp_done.done(s - 2, i))
                        dve.reduce_max(minus_max[:, s % 2, :], score[s % 2][:], AX_X, negate=True)\
                           .then_inc(*max_done.inc())
                    if before and s in H2_ROWS:
                        b = H2_ROWS[s]
                        dve.wait_ge(*xn2_out.done(b - 2, i - 1))
                        dve.wait_ge(*xn2_turned.done(b - 2, i - 1))
                        norm_rows(TB + b, i - 1, res[b][:], xn2[b % 2]).then_inc(*xn2_done.inc())
                    if more and s in NORM1_ROWS:
                        norm1_rows(NORM1_ROWS[s], i + 1)
                    u = s - 4
                    if (u >= 0 and own) or (u < 0 and carry):
                        c, b, inv = u % UNITS // TB, u % TB, inv_sum[:, u % 2, :]
                        dve.wait_ge(*av_made.done(u, i))
                        link(dve.reciprocal(inv.unsqueeze(2), av[u % 2][:, :, HD:HD + 1]))
                        dve.wait_ge(*att_turned.done(b, (i if u >= 0 else i - 1) - 1))
                        dve.tensor_tensor(att[b][:, 4 * c:4 * c + 4, :], av[u % 2][:, :, 0:HD],
                                          inv.unsqueeze(2).broadcast_to((P, 4, HD)), ALU.mult).then_inc(*att_done.inc())
                    for use in fill(s, *flags):
                        drain(use, group_of(use, i), bank(use))
                    if more and s in NORM1_STATS:
                        norm1_stats(NORM1_STATS[s], i + 1)

            group(0, FIRST, carry=False)
            with dve.Fori(1, last) as i:
                steps.enter(i - 1, UNITS + 2 * TB * (2 + 3))
                group(i, MIDDLE)
                steps.leave(last - 1)
            group(last, FINAL)
            group(groups, TAIL)

        @block.tensor
        def _(pe):
            pe.wait_ge(eye_ready, 1)

            def turn(dst, src, rows=P):
                for c in range(NC):
                    x = pe.transpose(dst[:, c * rows:(c + 1) * rows], src(c), eye[0:rows, 0:rows])
                return x

            def project(dst, stationary, moving):
                for ic in range(NC):
                    x = split_product(pe, dst[:], stationary(ic), moving(ic), ic == 0, ic == NC - 1)
                return x

            def make(use, i, dst):
                kind, n = use
                cols = slice(n * P, (n + 1) * P)
                xt, both = (xt_hi, xt_lo), (w_hi, w_lo)
                if kind in "qk":
                    if n == 0:
                        pe.wait_ge(*xt_lo_done.done(TB - 1, i))
                    project(dst, lambda ic: [m[kind][:, ic, cols] for m in both], lambda ic: [m[:, ic, :] for m in xt])\
                        .then_inc(*(q_made if kind == "q" else k_made).inc())
                elif kind == "v":
                    project(dst, lambda ic: [m[:, ic, cols] for m in xt], lambda ic: [m["v"][:, ic, :] for m in both])\
                        .then_inc(*v_made.inc())
                elif kind == "xt":
                    pe.wait_ge(*xn_done.done(n, i))
                    turn(dst, lambda c: h[n][:, c * P:(c + 1) * P]).then_inc(*xn_turned.inc())
                elif kind == "ot":
                    pe.wait_ge(*att_done.done(UNITS - TB + n, i))
                    rows = att[n][:].rearrange("p h d -> p (h d)")
                    turn(dst, lambda c: rows[:, c * P:(c + 1) * P]).then_inc(*att_turned.inc())
                elif kind == "o":
                    pe.wait_ge(*att_lo_done.done(n, i))
                    project(dst, lambda ic: [m[:, ic, :] for m in att_t[n]], lambda ic: [m["o"][:, ic, :] for m in both])\
                        .then_inc(*o_made.inc())
                elif kind == "x2t":
                    pe.wait_ge(*xn2_done.done(n, i))
                    turn(dst, lambda c: xn2[n % 2][:, c * P:(c + 1) * P]).then_inc(*xn2_turned.inc())
                elif kind == "logit":
                    pe.wait_ge(*xn2_t_done.done(n, i))
                    for c in range(NC):
                        x = pe.matmul(dst[:, 0:LOGITS], xn2_t[n % 2][:, c, :], router_t[:, c, :],
                                      start=c == 0, stop=c == NC - 1)
                    x.then_inc(*logits_made.inc())

            for n in range(len(weights) * NC):
                w, c = n // NC, n % NC
                if c == 0:
                    pe.wait_ge(w_in[w], 16)
                if n >= 2:
                    pe.wait_ge(w_lo_done, n - 1)
                turn(px[n % 2], lambda oc: w_raw[w % 2][:, oc, c * P:(c + 1) * P]).then_inc(w_turned, 1)
            pe.wait_ge(router_in, 32)
            pe.wait_ge(w_lo_done, len(weights) * NC - 1)
            turn(px[0], lambda c: router_raw[:, c * P:(c + 1) * P], rows=LOGITS).then_inc(w_turned, 1)
            pe.wait_ge(bv_lo_done, 1)
            project(px[1], lambda ic: [m[:, ic, 0:P] for m in (xt_hi, xt_lo)], lambda ic: [m["o"][:, ic, :] for m in (w_hi, w_lo)])\
                .then_inc(bias_made, 1)
            pe.wait_ge(credits_given, 1)
            pe.wait_ge(w_lo_done, len(weights) * NC + 1)
            pe.wait_ge(bias_done, 1)
            for b in range(TB):
                if b >= 2:
                    pe.wait_ge(*xt_lo_done.done(b - 2, 0))
                make(("xt", b), 0, px[b % 2])
            pe.wait_ge(*xt_lo_done.done(TB - 1, 0))
            make(("q", 0), 0, px[0])
            make(("k", 0), 0, px[1])
            pe.wait_ge(*q_lo_done.done(0, 0))
            pe.wait_ge(*k_lo_done.done(0, 0))

            def group(i, flags, flags_before, carry=True):
                own, more, before = flags
                for s in range(UNITS):
                    if own:
                        c, b = s // TB, s % TB
                        if b == 0:
                            pe.wait_ge(*q_lo_done.done(c, i))
                            pe.wait_ge(*k_spread.done(c, i))
                        pe.wait_ge(*exp_done.done(s - 2, i))
                        split_product(pe, score[s % 2][:].rearrange("p h k -> p (h k)"),
                                      [m[c % 2][:, b * P:(b + 1) * P] for m in (q_hi, q_lo)],
                                      [k_diag[c % 2][:, m, b, :, :].rearrange("p h k -> p (h k)") for m in range(2)],
                                      True, True).then_inc(*scored.inc())
                    u = s - 2
                    if (u >= 0 and own) or (u < 0 and carry):
                        pe.wait_ge(*prob_t_done.done(u - 2, i))
                        pe.wait_ge(*exp_done.done(u, i))
                        for r in range(4):
                            x = pe.transpose(pt[u % 2][:, r, :], prob[u % 2][:, r, :], eye[:])
                        x.then_inc(*prob_turned.inc())
                    u = s - 3
                    if (u >= 0 and own) or (u < 0 and carry):
                        c, b = u % UNITS // TB, u % TB
                        if u >= 0 and c == 0:
                            pe.wait_ge(*v_done.done(b, i))
                        pe.wait_ge(*att_done.done(u - 2, i))
                        pe.wait_ge(*prob_t_done.done(u, i))
                        for r in range(4):
                            x = pe.matmul(av[u % 2][:, r, :], prob_t[u % 2][:, r, :], v_rows[:, b, 4 * c + r, :],
                                          start=True, stop=True)
                        x.then_inc(*av_made.inc())
                    for use in fill(s, *flags):
                        if flags_before is not None or use not in (uses_of(*flags)[0:2]):
                            pe.wait_ge(*bank_free(use, i, flags, flags_before or flags))
                        make(use, group_of(use, i), bank(use))

            group(0, FIRST, None, carry=False)
            pe.wait_ge(*q_lo_done.done(0, 1))
            pe.wait_ge(*k_lo_done.done(0, 1))
            with pe.Fori(1, last) as i:
                group(i, MIDDLE, MIDDLE)
            group(last, FINAL, MIDDLE)
            group(groups, TAIL, FINAL)


def routing_phase(nc, new_sem, keep, io, scratch):
    logits, gates, slots = keep["logits"], keep["gates"], keep["slots"]
    tiles = logits.shape[1]
    slot_cols = keep["slot_token"].shape[1]
    slot_tiles = slot_cols // TB
    E = EXPERTS

    with ExitStack() as mem:
        def sb(name, shape, dt=F32):
            return mem.enter_context(nc.sbuf_tensor(name, shape, dt))

        def over_experts(x):
            return x.broadcast_to((P, tiles, E))

        shifted = sb("shifted", [P, tiles, E])
        expd = sb("expd", [P, tiles, E])
        probs = sb("probs", [P, tiles, E])
        row = sb("row", [P, tiles, 1])
        row_inv = sb("row_inv", [P, tiles, 1])
        first_of = sb("first_of", [P, 1, E])
        equal = sb("equal", [P, tiles, E])
        index = sb("index", [P, tiles, E])
        least = sb("least", [P, tiles, 1])
        rest = sb("rest", [P, tiles, E])
        chosen = [sb(f"chosen{k}", [P, tiles, E]) for k in range(TOPK)]
        either = sb("either", [P, tiles, E])
        before = sb("before", [P, P])
        ones = sb("ones", [P, P])
        totals = sb("totals", [P, tiles, E])
        run = [sb(f"run{n}", [P, 2 * tiles, E]) for n in range(2)]
        tile_run = [sb(f"tile_run{n}", [P, 2 * E]) for n in range(2)]
        count_int = sb("count_int", [P, E], I32)
        tiles_int = sb("tiles_int", [P, E], I32)
        tiles_of = sb("tiles_of", [P, E])
        base = sb("base", [P, 1, E])
        slot_of = sb("slot_of", [P, tiles, E])
        slot_f = sb("slot_f", [P, TOPK, tiles])
        slot_part = [sb(f"slot_part{n}", [P, TOPK, tiles], I32) for n in range(2)]
        slot_lo = sb("slot_lo", [P, TOPK * tiles])
        slot_hi = sb("slot_hi", [P, TOPK * tiles])
        int_iota = sb("int_iota", [P, P], I32)
        lane = sb("lane", [P, P])
        token_int = sb("token_int", [P, tiles], I32)
        token = sb("token", [P, tiles])
        under = sb("under", [P, slot_tiles, E])
        expert_f = sb("expert_f", [P, slot_tiles, 1])
        expert_int = keep["tile_expert"]
        hot_lo = [sb(f"hot_lo{n}", [P, P], F32R) for n in range(2)]
        hot_hi = [sb(f"hot_hi{n}", [P, slot_cols], F32R) for n in range(2)]
        rank_ps = mem.enter_context(nc.psum_tensor("rank_ps", [P, tiles * E], F32))
        total_ps = mem.enter_context(nc.psum_tensor("total_ps", [P, tiles * E], F32))
        slot_ps = mem.enter_context(nc.psum_tensor("slot_ps", [P, slot_cols], F32))

        iotas, ones_set, before_set, before_cut = (new_sem(n) for n in ("iotas", "ones_set", "before_set", "before_cut"))
        step = new_sem("route_step")
        shifted_done, exp_ready, either_done = new_sem("shifted_done"), new_sem("exp_ready"), new_sem("either_done")
        gate_done = new_sem("gate_done")
        ranked, hot_made, hot_used = new_sem("ranked"), new_sem("hot_made"), new_sem("hot_used")
        block = mem.enter_context(nc.Block())

        @block.gpsimd
        def _(pool):
            pool.memset(before[:], 0.0).then_inc(before_set, 1)
            pool.memset(ones[:], 1.0).then_inc(ones_set, 1)
            pool.iota(int_iota[:], pattern=[[1, P]], base=0, channel_multiplier=0).then_inc(iotas, 1)
            pool.iota(token_int[:], pattern=[[P, tiles]], base=0, channel_multiplier=1).then_inc(iotas, 1)
            pool.wait_ge(before_set, 1)
            pool.affine_select(out=before[:], in_=before[:], compare_op=ALU.is_ge, fill=1.0, base=0,
                               pattern=[[-1, P]], channel_multiplier=1).then_inc(before_cut, 1)

        @block.scalar
        def _(act):
            act.wait_ge(shifted_done, 1)
            act.activation(expd[:], shifted[:], ACT.Exp).then_inc(exp_ready, 1)
            act.activation(gates[:, :, TOPK:TOPK + 1], logits[:, :, E:E + 1], ACT.Sigmoid).then_inc(gate_done, 1)
            act.wait_ge(gate_done, 1)

        @block.tensor
        def _(pe):
            pe.wait_ge(either_done, 1)
            pe.wait_ge(before_cut, 1)
            pe.wait_ge(ones_set, 1)
            picked = either[:].rearrange("p t e -> p (t e)")
            pe.matmul(rank_ps[:], before[:], picked, start=True, stop=True).then_inc(ranked, 1)
            pe.matmul(total_ps[:], ones[:], picked, start=True, stop=True).then_inc(ranked, 1)
            n = TOPK * tiles
            pe.wait_ge(hot_made, 1)
            pe.matmul(slot_ps[:], hot_lo[0][:], hot_hi[0][:], start=True, stop=False).then_inc(hot_used, 1)
            for k in range(1, n):
                pe.wait_ge(hot_made, k + 1)
                pe.matmul(slot_ps[:], hot_lo[k % 2][:], hot_hi[k % 2][:], start=False, stop=k == n - 1).then_inc(hot_used, 1)

        @block.vector
        def _(dve):
            steps = Count(step)

            def link(ins):
                ins.then_inc(*steps.tick())
                dve.wait_ge(*steps.so_far())

            scores = logits[:, :, 0:E]
            link(dve.reduce_max(row[:], scores, AX_X))
            dve.tensor_tensor(shifted[:], scores, over_experts(row[:]), ALU.subtract).then_inc(shifted_done, 1)
            dve.wait_ge(iotas, 2)
            dve.tensor_copy(lane[:], int_iota[:]).then_inc(*steps.tick())
            dve.tensor_copy(token[:], token_int[:]).then_inc(*steps.tick())
            dve.tensor_scalar(first_of[:, 0, :], int_iota[:, 0:E], float(-E), None, ALU.add).then_inc(*steps.tick())
            for r in (*run, *tile_run):
                dve.memset(r[:], 0.0).then_inc(*steps.tick())
            dve.wait_ge(exp_ready, 1)
            link(dve.tensor_reduce(row[:], expd[:], AX_X, ALU.add))
            link(dve.reciprocal(row_inv[:], row[:]))
            link(dve.tensor_tensor(probs[:], expd[:], over_experts(row_inv[:]), ALU.mult))
            left = probs
            for k in range(TOPK):
                best = gates[:, :, k:k + 1]
                link(dve.reduce_max(best, left[:], AX_X))
                link(dve.tensor_tensor(equal[:], left[:], over_experts(best), ALU.is_equal))
                link(dve.tensor_tensor(index[:], equal[:], first_of[:].broadcast_to((P, tiles, E)), ALU.mult))
                link(dve.tensor_reduce(least[:], index[:], AX_X, ALU.min))
                link(dve.tensor_tensor(chosen[k][:], index[:], over_experts(least[:]), ALU.is_equal))
                if k == 0:
                    link(dve.scalar_tensor_tensor(out=rest[:], in0=chosen[k][:], scalar=-2.0, in1=probs[:],
                                                  op0=ALU.mult, op1=ALU.add))
                    left = rest
            dve.tensor_tensor(either[:], chosen[0][:], chosen[1][:], ALU.add).then_inc(either_done, 1)
            dve.wait_ge(ranked, 2)
            tot = total_ps[:].rearrange("p (t e) -> p t e", e=E)
            link(dve.tensor_copy(totals[:], tot))
            link(dve.tensor_copy(run[0][:, tiles:, :], totals[:]))
            cur, shift = 0, 1
            while shift < tiles:
                link(dve.tensor_tensor(run[1 - cur][:, tiles:, :], run[cur][:, tiles:, :],
                                       run[cur][:, tiles - shift:2 * tiles - shift, :], ALU.add))
                cur, shift = 1 - cur, 2 * shift
            through = run[cur][:, tiles:, :]
            link(dve.tensor_scalar(count_int[:], through[:, tiles - 1, :], float(GT - 1), None, ALU.add))
            link(dve.tensor_scalar(tiles_int[:], count_int[:], GT.bit_length() - 1, None, ALU.arith_shift_right))
            link(dve.tensor_copy(tiles_of[:], tiles_int[:]))
            link(dve.tensor_copy(tile_run[0][:, E:], tiles_of[:]))
            at, shift = 0, 1
            while shift < E:
                link(dve.tensor_tensor(tile_run[1 - at][:, E:], tile_run[at][:, E:],
                                       tile_run[at][:, E - shift:2 * E - shift], ALU.add))
                at, shift = 1 - at, 2 * shift
            ends = tile_run[at][:, E:]
            link(dve.tensor_tensor(base[:, 0, :], ends, tiles_of[:], ALU.subtract))
            link(dve.tensor_scalar(base[:, 0, :], base[:, 0, :], float(GT), None, ALU.mult))
            link(dve.tensor_tensor(slot_of[:], rank_ps[:].rearrange("p (t e) -> p t e", e=E), through, ALU.add))
            link(dve.tensor_tensor(slot_of[:], slot_of[:], totals[:], ALU.subtract))
            link(dve.tensor_tensor(slot_of[:], slot_of[:], base[:].broadcast_to((P, tiles, E)), ALU.add))
            for k in range(TOPK):
                link(dve.tensor_tensor(index[:], chosen[k][:], slot_of[:], ALU.mult))
                link(dve.tensor_reduce(slot_f[:, k, :].unsqueeze(2), index[:], AX_X, ALU.add))
            link(dve.tensor_copy(slots[:], slot_f[:]))
            link(dve.tensor_scalar(slot_part[0][:], slots[:], P - 1, None, ALU.bitwise_and))
            link(dve.tensor_scalar(slot_part[1][:], slots[:], P.bit_length() - 1, None, ALU.arith_shift_right))
            link(dve.tensor_copy(slot_lo[:], slot_part[0][:].rearrange("p k t -> p (k t)")))
            link(dve.tensor_copy(slot_hi[:], slot_part[1][:].rearrange("p k t -> p (k t)")))
            link(dve.tensor_tensor(under[:], ends.unsqueeze(1).broadcast_to((P, slot_tiles, E)),
                                   lane[:, 0:slot_tiles].unsqueeze(2).broadcast_to((P, slot_tiles, E)), ALU.is_le))
            link(dve.tensor_reduce(expert_f[:], under[:], AX_X, ALU.add))
            link(dve.tensor_scalar(expert_int[:], expert_f[:, :, 0], float(E - 1), None, ALU.min))
            for n in range(TOPK * tiles):
                if n >= 2:
                    dve.wait_ge(hot_used, n - 1)
                dve.tensor_scalar(hot_lo[n % 2][:], lane[:], slot_lo[:, n:n + 1], None, ALU.is_equal)
                dve.tensor_scalar(hot_hi[n % 2][:], lane[:, 0:slot_cols], slot_hi[:, n:n + 1],
                                  token[:, n % tiles:n % tiles + 1], ALU.is_equal, ALU.mult).then_inc(hot_made, 1)
            dve.wait_ge(hot_used, TOPK * tiles)
            link(dve.tensor_copy(keep["slot_token"][:], slot_ps[:]))


def ffn_phase(nc, new_sem, keep, io, scratch, shared):
    eye = keep["eye"]
    tag = "s" if shared else "e"
    inner = I_SH if shared else I_MOE
    NM = -(-inner // P)
    size = [min(P, inner - m * P) for m in range(NM)]
    tiles = (scratch["h2"].shape[0] // GT) if shared else keep["slot_token"].shape[1] // TB
    last = tiles - 1
    SQ = 2 * (I_SH // P)
    assert NM % 2 == 1

    with ExitStack() as mem:
        def sb(name, shape, dt=F32):
            return mem.enter_context(nc.sbuf_tensor(f"{tag}_{name}", shape, dt))

        def ps(name, shape):
            return mem.enter_context(nc.psum_tensor(f"{tag}_{name}", shape, F32))

        def stage(name, per, **kw):
            s = Stage(new_sem, f"{tag}_{name}", per, **kw)
            stages.append(s)
            return s

        stages = []
        if shared:
            gu_hi, gu_lo = keep["gu_hi"], keep["gu_lo"]
            dn_hi, dn_lo = sb("dn_hi", [P, NM, DIM], F32R), sb("dn_lo", [P, NM, DIM], F32R)
            dn_raw = [sb(f"dn_raw{n}", [P, DIM]) for n in range(2)]
        else:
            gu_hi, gu_lo = sb("gu_hi", [P, 2, NC, inner], F32R), sb("gu_lo", [P, 2, NC, inner], F32R)
            gu_raw = [sb(f"gu_raw{m}", [P, 2, NC, size[m]]) for m in range(NM)]
            dn_hi, dn_lo = sb("dn_hi", [P, NM, DIM], F32R), sb("dn_lo", [P, NM, DIM], F32R)
            dn_raw = [sb(f"dn_raw{m}", [P, DIM]) for m in range(NM)]
            sh_raw = [sb(f"sh_raw{n}", [P, NC, P]) for n in range(1)]
            rows_now = sb("rows_now", [P, TB], I32)
        x = [sb(f"x{b}", [P, DIM]) for b in range(TB)]
        xt_hi, xt_lo = sb("xt_hi", [P, NC, GT], F32R), sb("xt_lo", [P, NC, GT], F32R)
        silu = [sb(f"silu{n}", [P, GT]) for n in range(2)]
        act_f = [sb(f"act{n}", [P, GT]) for n in range(2)]
        act_hi = [sb(f"act_hi{n}", [P, GT], F32R) for n in range(2)]
        act_lo = [sb(f"act_lo{n}", [P, GT], F32R) for n in range(2)]
        out = [sb(f"out{n}", [P, DIM]) for n in range(TB if shared else 2)]
        if shared:
            picked = [[sb(f"picked{k}{n}", [P, DIM]) for n in range(2)] for k in range(TOPK)]
            slots_now = sb("slots_now", [P, TOPK, TB], I32)
            gates_now = sb("gates_now", [P, TB, TOPK + 1])
        banks = [ps(f"bank{n}", [P, GT]) for n in range(4)]
        acc = [ps(f"acc{b}", [P, DIM]) for b in range(TB)]

        x_turned = stage("x_turned", TB)
        gate_made, up_made = stage("gate_made", NM), stage("up_made", NM)
        down_made = stage("down_made", NM)
        xt_hi_done = stage("xt_hi_done", TB)
        silu_done, act_hi_done = stage("silu_done", NM), stage("act_hi_done", NM)
        xt_lo_done = stage("xt_lo_done", TB)
        act_done, act_lo_done = stage("act_done", NM), stage("act_lo_done", NM)
        if shared:
            x_in = stage("x_in", TB, dma=True, lanes=TB)
            res_in = stage("res_in", TB, dma=True, lanes=TB)
            picked_in = [stage(f"picked_in{k}", TB, dma=True, lanes=2, credit=False) for k in range(TOPK)]
            slots_copied, gates_copied = stage("slots_copied", 1), stage("gates_copied", 1)
            joined = [stage(f"joined{n}", TB) for n in range(1 + TOPK)]
            acc_read = joined[0]
            dn_in = [new_sem(f"s_dn_in{n}") for n in range(2)]
            dn_hi_ready, dn_lo_ready = new_sem("s_dn_hi_ready"), new_sem("s_dn_lo_ready")
        else:
            x_in = stage("x_in", TB, dma=True, lanes=TB, credit=False)
            acc_read = stage("acc_read", TB)
            gu_in = stage("gu_in", NM, dma=True, lanes=NM)
            gu_in.unit = 32
            dn_in = stage("dn_in", NM, dma=True, lanes=NM)
            gu_hi_done, gu_lo_done = stage("gu_hi_done", NM), stage("gu_lo_done", NM)
            dn_hi_done, dn_lo_done = stage("dn_hi_done", NM), stage("dn_lo_done", NM)
            sh_in = stage("sh_in", 1, dma=True)
            sh_hi_done, sh_lo_done = stage("sh_hi_done", 1), stage("sh_lo_done", 1)
            rows_copied = new_sem("e_rows_copied")
        out_sent = stage("out_sent", TB, dma=True, lanes=len(out))
        pool_go, sp_go = keep["pool_go"], keep["sp_go"]
        credits_given = new_sem(f"{tag}_credits")

        uses = []
        for m in range(NM):
            first = 0 if m % 2 else 2
            uses += [(("gate", m), first, silu_done), (("up", m), first + 1, act_done)]
            if m == NM - 1:
                uses += [(("x", b), b % 2, xt_lo_done) for b in range(TB)]

        def bank(kind, n):
            return next(banks[w] for use, w, _ in uses if use == (kind, n))

        def bank_free(kind, n, i, more=True):
            own = [u for u in uses if more or u[0][0] != "x"]
            at = next(k for k, u in enumerate(own) if u[0] == (kind, n))
            where = own[at][1]
            if any(u[1] == where for u in own[:at]):
                (what, k), _, by = [u for u in own[:at] if u[1] == where][-1]
                back = 0
            else:
                (what, k), _, by = [u for u in uses if u[1] == where][-1]
                back = 1
            return by.done(k, i - back + (what == "x"))

        def gu_parts(which, m):
            if shared:
                q = which * NM + m
                return lambda ic: [w[:, q, ic, :] for w in (gu_hi, gu_lo)]
            return lambda ic: [w[:, which, ic, m * P:m * P + size[m]] for w in (gu_hi, gu_lo)]

        block = mem.enter_context(nc.Block())

        @block.sync
        def _(sp):
            for s in stages:
                s.credit(sp)
            sp.sem_inc(credits_given, 1)
            if shared:
                def load_x(i):
                    for b in range(TB):
                        sp.wait_ge(*x_turned.done(b, i - 1))
                        sp.dma_start(x[b][:], scratch["xn2"][bass.ds((i * TB + b) * P, P), :]).then_inc(*x_in.inc(b))

                def load_residual(i):
                    for b in range(TB):
                        sp.wait_ge(*out_sent.done(b, i - 1))
                        sp.dma_start(out[b][:], scratch["h2"][bass.ds((i * TB + b) * P, P), :]).then_inc(*res_in.inc(b))

                def send(i):
                    for b in range(TB):
                        sp.wait_ge(*joined[TOPK].done(b, i))
                        sp.dma_start(io["out"][bass.ds((i * TB + b) * P, P), :], out[b][:]).then_inc(*out_sent.inc(b))

                load_x(0)
                for m in range(NM):
                    if m >= 2:
                        sp.wait_ge(dn_lo_ready, m - 1)
                    sp.dma_start(dn_raw[m % 2][:], io["L0_ffn_Ws_down"][m * P:(m + 1) * P, :]).then_inc(dn_in[m % 2], 16)
                    if m == 1:
                        load_residual(0)
                        load_x(1)
                with sp.Fori(1, last) as i:
                    load_x(i + 1)
                    send(i - 1)
                    load_residual(i)
                send(last - 1)
                load_residual(last)
                send(last)
                for b in range(TB):
                    sp.wait_ge(*out_sent.done(b, last))
            else:
                def tile(j, more):
                    sp.sem_inc(sp_go, 1)
                    e = sp.value_load(keep["tile_expert"][0:1, bass.ds(j, 1)], min_val=0, max_val=EXPERTS - 1)
                    gu = io["L0_ffn_We_gate_up"][bass.ds(e, 1)].rearrange("a (c p) (w n) -> p (a w) c n", p=P, w=2)
                    dn = io["L0_ffn_We_down"][bass.ds(e, 1)].rearrange("a i n -> (a i) n")
                    for m in range(NM):
                        sp.wait_ge(*gu_lo_done.done(m, j - 1))
                        for w in range(2):
                            sp.dma_start(gu_raw[m][:, w, :, :], gu[:, w, :, m * P:m * P + size[m]])\
                              .then_inc(gu_in.sems[m], 16)
                    for m in range(NM):
                        sp.wait_ge(*dn_lo_done.done(m, j - 1))
                        sp.dma_start(dn_raw[m][0:size[m], :], dn[m * P:m * P + size[m], :]).then_inc(*dn_in.inc(m))
                    if more:
                        sp.wait_ge(*sh_lo_done.done(0, j - 1))
                        sp.dma_start(sh_raw[0][:], io["L0_ffn_Ws_gate_up"][:, bass.ds(j * P, P)]
                                     .rearrange("(c p) n -> p c n", p=P)).then_inc(*sh_in.inc())

                assert last == SQ
                with sp.Fori(0, last) as j:
                    tile(j, True)
                tile(last, False)

        @block.gpsimd
        def _(pool):
            if shared:
                with pool.Fori(0, tiles) as i:
                    pool.wait_ge(*joined[TOPK].done(TB - 1, i - 1))
                    pool.sem_inc(pool_go, 1)
                    pool.tensor_copy(slots_now[:], keep["slots"][:, :, bass.ds(i * TB, TB)]).then_inc(*slots_copied.inc())
                    pool.wait_ge(*slots_copied.done(0, i))
                    for b in range(TB):
                        pool.wait_ge(*joined[TOPK].done(b - 2, i))
                        pool.sem_inc(pool_go, 1)
                        for k in range(TOPK):
                            pool.indirect_dma_start(
                                out=picked[k][b % 2][:], out_offset=None, in_=scratch["expert_rows"],
                                in_offset=bass.IndirectOffsetOnAxis(ap=slots_now[:, k, b:b + 1].bitcast(U32), axis=0),
                            ).then_inc(*picked_in[k].inc(b))
            else:
                def gather(j):
                    pool.tensor_copy(rows_now[:], keep["slot_token"][:, bass.ds(j * TB, TB)]).then_inc(rows_copied, 1)
                    pool.wait_ge(rows_copied, j + 1)
                    pool.sem_inc(pool_go, 1)
                    for b in range(TB):
                        pool.indirect_dma_start(
                            out=x[b][:], out_offset=None, in_=scratch["xn2"],
                            in_offset=bass.IndirectOffsetOnAxis(ap=rows_now[:, b:b + 1].bitcast(U32), axis=0),
                        ).then_inc(*x_in.inc(b))

                pool.wait_ge(credits_given, 1)
                gather(0)
                with pool.Fori(1, tiles) as j:
                    for b in range(TB):
                        pool.wait_ge(*x_in.done(b, j - 1))
                    pool.wait_ge(*x_turned.done(TB - 1, j - 1))
                    pool.sem_inc(pool_go, 1)
                    gather(j)

        @block.scalar
        def _(act):
            act.preload_act_table(ACT.Silu)
            act.wait_ge(credits_given, 1)

            def x_split(b, i):
                act.wait_ge(*x_turned.done(b, i))
                act.wait_ge(*up_made.done(NM - 1, i - 1))
                act.activation(xt_hi[:, :, b * P:(b + 1) * P], bank("x", b)[:].rearrange("p (c n) -> p c n", c=NC),
                               ACT.Copy).then_inc(*xt_hi_done.inc())

            def gu_split(m, j):
                act.wait_ge(*gu_in.done(m, j))
                act.wait_ge(*up_made.done(m, j - 1))
                for w in range(2):
                    y = act.activation(gu_hi[:, w, :, m * P:m * P + size[m]], gu_raw[m][:, w, :, :], ACT.Copy)
                y.then_inc(*gu_hi_done.inc())

            def dn_split(m, j):
                act.wait_ge(*dn_in.done(m, j))
                act.wait_ge(*down_made.done(m, j - 1))
                act.activation(dn_hi[0:size[m], m, :], dn_raw[m][0:size[m], :], ACT.Copy).then_inc(*dn_hi_done.inc())

            if not shared:
                for m in range(NM):
                    gu_split(m, 0)
            for b in range(TB):
                x_split(b, 0)

            def tile(i, more, first=False):
                for m in range(NM):
                    n = size[m]
                    if shared and first:
                        act.wait_ge(dn_in[m % 2], 16 * (m // 2 + 1))
                        act.activation(dn_hi[:, m, :], dn_raw[m % 2][:], ACT.Copy).then_inc(dn_hi_ready, 1)
                    act.wait_ge(*gate_made.done(m, i))
                    act.wait_ge(*act_done.done(m - 2, i))
                    act.activation(silu[m % 2][0:n, :], bank("gate", m)[0:n, :], ACT.Silu).then_inc(*silu_done.inc())
                    act.wait_ge(*act_done.done(m, i))
                    act.wait_ge(*down_made.done(m - 2, i))
                    act.activation(act_hi[m % 2][0:n, :], act_f[m % 2][0:n, :], ACT.Copy).then_inc(*act_hi_done.inc())
                    if not shared:
                        if m == 0:
                            dn_split(0, i)
                            dn_split(1, i)
                        if m == 1:
                            dn_split(2, i)
                            if more:
                                act.wait_ge(*sh_in.done(0, i))
                                act.activation(keep["gu_hi"][:, bass.ds(i, 1), :, :].rearrange("p a c n -> p (a c) n"),
                                               sh_raw[0][:], ACT.Copy).then_inc(*sh_hi_done.inc())
                        if more and m < NM - 1:
                            gu_split(m, i + 1)
                if more:
                    for b in range(TB):
                        x_split(b, i + 1)
                if not shared:
                    for b in range(TB):
                        act.wait_ge(*down_made.done(NM - 1, i))
                        act.wait_ge(*out_sent.done(b - 2, i))
                        act.activation(out[b % 2][:], acc[b][:], ACT.Copy).then_inc(*acc_read.inc())
                        act.wait_ge(*acc_read.done(b, i))
                        act.dma_start(scratch["expert_rows"][bass.ds((i * TB + b) * P, P), :], out[b % 2][:])\
                           .then_inc(*out_sent.inc(b))
                    if more:
                        gu_split(NM - 1, i + 1)

            tile(0, True, first=True)
            with act.Fori(1, last) as i:
                tile(i, True)
            tile(last, False)
            if not shared:
                for b in (TB - 2, TB - 1):
                    act.wait_ge(*out_sent.done(b, last))

        @block.vector
        def _(dve):
            dve.wait_ge(credits_given, 1)

            def x_split(b, i):
                cols = slice(b * P, (b + 1) * P)
                dve.wait_ge(*xt_hi_done.done(b, i))
                dve.tensor_tensor(xt_lo[:, :, cols], bank("x", b)[:].rearrange("p (c n) -> p c n", c=NC),
                                  xt_hi[:, :, cols].bitcast(F32), ALU.subtract).then_inc(*xt_lo_done.inc())

            def gu_split(m, j):
                dve.wait_ge(*gu_hi_done.done(m, j))
                for w in range(2):
                    cols = slice(m * P, m * P + size[m])
                    y = dve.tensor_tensor(gu_lo[:, w, :, cols], gu_raw[m][:, w, :, :], gu_hi[:, w, :, cols].bitcast(F32),
                                          ALU.subtract)
                y.then_inc(*gu_lo_done.inc())

            def dn_split(m, j):
                n = size[m]
                dve.wait_ge(*dn_hi_done.done(m, j))
                dve.tensor_tensor(dn_lo[0:n, m, :], dn_raw[m][0:n, :], dn_hi[0:n, m, :].bitcast(F32), ALU.subtract)\
                   .then_inc(*dn_lo_done.inc())

            if not shared:
                for m in range(NM):
                    gu_split(m, 0)
            for b in range(TB):
                x_split(b, 0)

            def join(b, i):
                for k in range(TOPK):
                    dve.wait_ge(*picked_in[k].done(b, i))
                    dve.wait_ge(*joined[k].done(b, i))
                    dve.scalar_tensor_tensor(out=out[b][:], in0=picked[k][b % 2][:], scalar=gates_now[:, b, k:k + 1],
                                             in1=out[b][:], op0=ALU.mult, op1=ALU.add).then_inc(*joined[k + 1].inc())

            def tile(i, more, first=False):
                for m in range(NM):
                    n = size[m]
                    if shared and first:
                        dve.wait_ge(dn_hi_ready, m + 1)
                        dve.tensor_tensor(dn_lo[:, m, :], dn_raw[m % 2][:], dn_hi[:, m, :].bitcast(F32), ALU.subtract)\
                           .then_inc(dn_lo_ready, 1)
                    dve.wait_ge(*silu_done.done(m, i))
                    dve.wait_ge(*up_made.done(m, i))
                    dve.wait_ge(*act_lo_done.done(m - 2, i))
                    dve.tensor_tensor(act_f[m % 2][0:n, :], bank("up", m)[0:n, :], silu[m % 2][0:n, :], ALU.mult)\
                       .then_inc(*act_done.inc())
                    dve.wait_ge(*act_hi_done.done(m, i))
                    dve.tensor_tensor(act_lo[m % 2][0:n, :], act_f[m % 2][0:n, :], act_hi[m % 2][0:n, :].bitcast(F32),
                                      ALU.subtract).then_inc(*act_lo_done.inc())
                    if not shared:
                        if m == 0:
                            dn_split(0, i)
                            dn_split(1, i)
                        if m == 1:
                            dn_split(2, i)
                            if more:
                                block_now = bass.ds(i, 1)
                                dve.wait_ge(*sh_hi_done.done(0, i))
                                dve.tensor_tensor(keep["gu_lo"][:, block_now, :, :].rearrange("p a c n -> p (a c) n"),
                                                  sh_raw[0][:],
                                                  keep["gu_hi"][:, block_now, :, :].rearrange("p a c n -> p (a c) n")
                                                  .bitcast(F32), ALU.subtract).then_inc(*sh_lo_done.inc())
                        if more and m < NM - 1:
                            gu_split(m, i + 1)
                    if shared and m < TB and not first:
                        join(m, i - 1)
                if more:
                    for b in range(TB):
                        x_split(b, i + 1)
                if shared:
                    dve.wait_ge(*joined[TOPK].done(TB - 1, i - 1))
                    dve.tensor_copy(gates_now[:], keep["gates"][:, bass.ds(i * TB, TB), :]).then_inc(*gates_copied.inc())
                    dve.wait_ge(*gates_copied.done(0, i))
                    dve.wait_ge(*down_made.done(NM - 1, i))
                    for b in range(TB):
                        dve.wait_ge(*res_in.done(b, i))
                        dve.scalar_tensor_tensor(out=out[b][:], in0=acc[b][:], scalar=gates_now[:, b, TOPK:TOPK + 1],
                                                 in1=out[b][:], op0=ALU.mult, op1=ALU.add).then_inc(*joined[0].inc())
                elif more:
                    gu_split(NM - 1, i + 1)

            tile(0, True, first=True)
            with dve.Fori(1, last) as i:
                tile(i, True)
            tile(last, False)
            if shared:
                for b in range(TB):
                    join(b, last)

        @block.tensor
        def _(pe):
            pe.wait_ge(credits_given, 1)

            def x_turn(b, i, free):
                pe.wait_ge(*x_in.done(b, i))
                pe.wait_ge(*free)
                for c in range(NC):
                    y = pe.transpose(bank("x", b)[:, c * P:(c + 1) * P], x[b][:, c * P:(c + 1) * P], eye[:])
                y.then_inc(*x_turned.inc())

            for b in range(TB):
                x_turn(b, 0, xt_lo_done.done(b - 2, 0))

            def tile(i, more, first=False):
                def down(m, part=range(TB)):
                    n = size[m]
                    if shared and first:
                        pe.wait_ge(dn_lo_ready, m + 1)
                    if not shared:
                        pe.wait_ge(*dn_lo_done.done(m, i))
                    pe.wait_ge(*act_lo_done.done(m, i))
                    for b in part:
                        if m == 0:
                            pe.wait_ge(*acc_read.done(b, i - 1))
                        cols = slice(b * P, (b + 1) * P)
                        y = split_product(pe, acc[b][:], [a[m % 2][0:n, cols] for a in (act_hi, act_lo)],
                                          [w[0:n, m, :] for w in (dn_hi, dn_lo)], m == 0, m == NM - 1)
                    if b == TB - 1:
                        y.then_inc(*down_made.inc())

                pe.wait_ge(*xt_lo_done.done(TB - 1, i))
                for m in range(NM):
                    if not shared:
                        pe.wait_ge(*gu_lo_done.done(m, i))
                    for w, (kind, made) in enumerate((("gate", gate_made), ("up", up_made))):
                        parts = gu_parts(w, m)
                        pe.wait_ge(*bank_free(kind, m, i, more))
                        for ic in range(NC):
                            y = split_product(pe, bank(kind, m)[0:size[m], :], parts(ic),
                                              [a[:, ic, :] for a in (xt_hi, xt_lo)], ic == 0, ic == NC - 1)
                        y.then_inc(*made.inc())
                    if m >= 1:
                        down(m - 1)
                for pair in (range(0, 2), range(2, TB)):
                    if more:
                        for b in pair:
                            x_turn(b, i + 1, bank_free("x", b, i))
                    down(NM - 1, pair)

            tile(0, True, first=True)
            with pe.Fori(1, last) as i:
                tile(i, True)
            tile(last, False)


def program(nc, io):
    tokens = io["x"].shape[0] * io["x"].shape[1]
    assert io["x"].shape[1] == P
    slot_tiles = (tokens * TOPK + EXPERTS * (GT - 1)) // GT
    with ExitStack() as ctx:
        def new_sem(name):
            return ctx.enter_context(nc.semaphore(name))

        def sb(name, shape, dt=F32):
            return ctx.enter_context(nc.sbuf_tensor(name, shape, dt))

        scratch = {name: nc.dram_tensor(f"{name}_dram", (rows, DIM), F32, kind="Internal").ap()
                   for name, rows in (("h2", tokens), ("xn2", tokens), ("expert_rows", slot_tiles * GT))}
        keep = {
            "eye": sb("eye", [P, P]),
            "logits": sb("logits", [P, tokens // P, LOGITS]),
            "gates": sb("gates", [P, tokens // P, TOPK + 1]),
            "slots": sb("slots", [P, TOPK, tokens // P], I32),
            "slot_token": sb("slot_token", [P, slot_tiles * TB], I32),
            "tile_expert": sb("tile_expert", [P, slot_tiles], I32),
            "pool_go": new_sem("pool_go"), "sp_go": new_sem("sp_go"),
        }
        attention_phase(nc, new_sem, keep, io, scratch)
        routing_phase(nc, new_sem, keep, io, scratch)
        blocks = 2 * (I_SH // P)
        keep["gu_hi"] = sb("gu_hi", [P, blocks, NC, P], F32R)
        keep["gu_lo"] = sb("gu_lo", [P, blocks, NC, P], F32R)
        ffn_phase(nc, new_sem, keep, io, scratch, shared=False)
        ffn_phase(nc, new_sem, keep, io, scratch, shared=True)


_INS = ["x", "L0_tok_weight", "L0_attn_Wq", "L0_attn_bq", "L0_attn_Wk", "L0_attn_bk", "L0_attn_Wv", "L0_attn_bv",
        "L0_attn_Wout", "L0_attn_bout", "L0_ffn_W_router", "L0_ffn_W_sgate", "L0_ffn_Ws_gate_up", "L0_ffn_Ws_down",
        "L0_ffn_We_gate_up", "L0_ffn_We_down"]


def kernel(**inputs):
    import numpy as _np
    import concourse.bacc as _bacc
    from concourse import mybir as _mybir
    from concourse.bass_utils import run_bass_kernel_spmd as _run

    nc = _bacc.Bacc("TRN2", target_bir_lowering=False, num_devices=1)
    arrays, io = {}, {}
    for name in _INS:
        a = _np.ascontiguousarray(inputs[name])
        arrays[f"in_{name}_dram"] = a
        io[name] = nc.dram_tensor(f"in_{name}_dram", a.shape, _mybir.dt.from_np(a.dtype), kind="ExternalInput").ap()
    shape = (*inputs["x"].shape, DIM)
    out = nc.dram_tensor("out_0_dram", shape, _mybir.dt.float32, kind="ExternalOutput").ap()
    io["out"] = out.rearrange("s t d -> (s t) d")
    program(nc, io)
    r = _run(nc, [arrays], core_ids=[0])
    return r.results[0]["out_0_dram"]
```

```python
from contextlib import ExitStack

import concourse.bass as bass
from concourse import mybir

F32 = mybir.dt.float32
F32R = mybir.dt.float32r
I32 = mybir.dt.int32
U32 = mybir.dt.uint32
ACT = mybir.ActivationFunctionType
ALU = mybir.AluOpType
AX_X = mybir.AxisListType.X

P = 128
DIM = 512
NC = DIM // P
HEADS = 16
HD = DIM // HEADS
EXPERTS = 8
I_MOE = 352
I_SH = 1408
TOPK = 2
TB = 4
GT = TB * P
EPS = 1e-5
LOGITS = EXPERTS + 1


class Stage:

    def __init__(self, new_sem, name, per, dma=False, lanes=1, credit=True, ahead=False):
        assert per % lanes == 0
        self.ahead = ahead
        self.credits = per // lanes if credit else 0
        self.per, self.lanes, self.unit = per, lanes, 16 if dma else 1
        self.sems = [new_sem(name if lanes == 1 else f"{name}{n}") for n in range(lanes)]

    def inc(self, n=0):
        return self.sems[n % self.lanes], self.unit

    def done(self, n, i=0):
        per = self.per // self.lanes
        return self.sems[n % self.lanes], (i * per + (self.credits + n // self.lanes + 1)) * self.unit

    def credit(self, eng):
        if self.credits:
            for s in self.sems:
                eng.sem_inc(s, self.credits * self.unit * (2 if self.ahead else 1))


class Count:

    def __init__(self, sem):
        self.sem, self.base, self.lap, self.k = sem, 0, 0, 0

    def tick(self):
        self.k += 1
        return self.sem, 1

    def so_far(self):
        return self.sem, self.base + self.lap + self.k

    def enter(self, i, per):
        self.base, self.lap, self.k, self.per = self.base + self.k, i * per, 0, per

    def leave(self, n):
        assert self.k == self.per, (self.sem, self.k)
        self.base, self.lap, self.k = self.base + n * self.per, 0, 0


def split_product(pe, out, stationary, moving, first, last):
    (sh, sl), (mh, ml) = stationary, moving
    pe.matmul(out, sh, mh, start=first, stop=False)
    pe.matmul(out, sh, ml, start=False, stop=False)
    return pe.matmul(out, sl, mh, start=False, stop=last)


def attention_phase(nc, new_sem, keep, io, scratch):
    x_ids, table = io["x"], io["L0_tok_weight"]
    groups = x_ids.shape[0] // TB
    last = groups - 1
    SCALE = float(HD) ** -0.5

    with ExitStack() as mem:
        def sb(name, shape, dt=F32):
            return mem.enter_context(nc.sbuf_tensor(name, shape, dt))

        def ps(name, shape):
            return mem.enter_context(nc.psum_tensor(name, shape, F32))

        def stage(name, per, **kw):
            s = Stage(new_sem, name, per, **kw)
            stages.append(s)
            return s

        stages = []
        eye = keep["eye"]
        weights = {"k": "L0_attn_Wk", "q": "L0_attn_Wq", "v": "L0_attn_Wv", "o": "L0_attn_Wout"}
        w_hi = {w: sb(f"w_{w}_hi", [P, NC, DIM], F32R) for w in weights}
        w_lo = {w: sb(f"w_{w}_lo", [P, NC, DIM], F32R) for w in weights}
        arena = sb("arena", [P, 2 * NC, DIM])
        w_raw = [arena[:, n * NC:(n + 1) * NC, :] for n in range(2)]
        router_t = sb("router_t", [P, NC, LOGITS])
        bias_in_t = sb("bias_in_t", [P, 3, NC])
        bias_q = sb("bias_q", [P, NC])
        bias_o = sb("bias_o", [P, DIM])
        ids = sb("ids", [P, groups * TB], I32)
        ids_now, ids_then = sb("ids_now", [P, TB], I32), sb("ids_then", [P, TB], I32)

        h = [sb(f"h{b}", [P, DIM]) for b in range(TB)]
        res = [sb(f"res{b}", [P, DIM]) for b in range(TB)]
        xt_hi = sb("xt_hi", [P, NC, GT], F32R)
        xt_lo = sb("xt_lo", [P, NC, GT], F32R)
        q_hi, q_lo = ([sb(f"q_{part}{n}", [P, GT], F32R) for n in range(2)] for part in ("hi", "lo"))
        k_parts = [sb(f"k_parts{n}", [P, 2, TB, P], F32R) for n in range(2)]
        k_diag = [sb(f"k_diag{n}", [P, 2, TB, 4, P], F32R) for n in range(2)]
        v_rows = sb("v_rows", [P, TB, HEADS, HD + 1])
        stats = sb("stats", [P, 2 * TB, 6])
        mean_var = sb("mean_var", [P, 2 * TB, 2])
        small = sb("small", [P, 2 * TB, 6])
        minus_max = sb("minus_max", [P, 2, 4])
        prob, prob_t = ([arena[:, m + n, :].rearrange("p (h k) -> p h k", k=P) for n in range(2)] for m in (0, 2))
        xn2 = [arena[:, 4 + n, :] for n in range(2)]
        xn2_t = [arena[:, 6 + n, :].rearrange("p (c n) -> p c n", c=NC) for n in range(2)]
        inv_sum = sb("inv_sum", [P, 2, 4])
        att = [sb(f"att{b}", [P, HEADS, HD]) for b in range(TB)]
        att_t = [(sb(f"att_t_hi{b}", [P, NC, P], F32R), sb(f"att_t_lo{b}", [P, NC, P], F32R)) for b in range(TB)]
        router_raw = att[0][0:LOGITS].rearrange("p h d -> p (h d)")

        px = [ps(f"px{n}", [P, DIM]) for n in range(2)]
        score = [ps(f"score{n}", [P, 4, P]) for n in range(2)]
        pt = [ps(f"pt{n}", [P, 4, P]) for n in range(2)]
        av = [ps(f"av{n}", [P, 4, HD + 1]) for n in range(2)]

        UNITS = NC * TB

        h_in = stage("h_in", TB, dma=True, lanes=TB, credit=False)
        res_in = stage("res_in", TB, dma=True, lanes=TB, credit=False)
        ids_copied = stage("ids_copied", 1)
        res_done = stage("res_done", TB)
        xn_turned = stage("xn_turned", TB)
        q_made, k_made, v_made = stage("q_made", NC), stage("k_made", NC), stage("v_made", TB)
        scored = stage("scored", UNITS)
        prob_turned = stage("prob_turned", UNITS)
        av_made = stage("av_made", UNITS)
        att_turned = stage("att_turned", TB)
        o_made = stage("o_made", TB)
        xn2_turned = stage("xn2_turned", TB)
        logits_made = stage("logits_made", TB)
        xt_hi_done = stage("xt_hi_done", TB)
        q_hi_done, k_hi_done, v_done = stage("q_hi_done", NC), stage("k_hi_done", NC), stage("v_done", TB)
        exp_done = stage("exp_done", UNITS)
        prob_t_done = stage("prob_t_done", UNITS)
        att_hi_done = stage("att_hi_done", TB)
        xn2_t_done = stage("xn2_t_done", TB)
        y0_done = [stage(f"y0_done{n}", TB) for n in (1, 2)]
        var_done = [stage(f"var_done{n}", TB) for n in (1, 2)]
        xn_done = stage("xn_done", TB)
        xt_lo_done = stage("xt_lo_done", TB)
        q_lo_done, k_lo_done = stage("q_lo_done", NC), stage("k_lo_done", NC)
        max_done = stage("max_done", UNITS)
        att_done = stage("att_done", UNITS)
        att_lo_done = stage("att_lo_done", TB)
        h2_done = stage("h2_done", TB)
        xn2_done = stage("xn2_done", TB)
        logits_done = stage("logits_done", TB)
        k_spread = stage("k_spread", NC, dma=True, lanes=2)
        k_spread.unit = 4 * 16
        h2_out = stage("h2_out", TB, dma=True, lanes=TB)
        xn2_out = stage("xn2_out", TB, dma=True, lanes=2)

        credits_given = keep["credits_given"]
        eye_zeroed, eye_ready, ones_ready = new_sem("eye_zeroed"), new_sem("eye_ready"), new_sem("ones_ready")
        k_zeroed = new_sem("k_zeroed")
        w_in = [new_sem(f"w_in_{w}") for w in weights]
        router_in, bias_in, ids_in = new_sem("router_in"), new_sem("bias_in"), new_sem("ids_in")
        pool_go, sp_go = keep["pool_go"], keep["sp_go"]
        w_turned, w_hi_done, w_lo_done = new_sem("w_turned"), new_sem("w_hi_done"), new_sem("w_lo_done")
        bv_hi_done, bv_lo_done, bias_made, bias_done = (new_sem(n) for n in ("bv_hi_done", "bv_lo_done", "bias_made", "bias_done"))
        dve_step, dve_go, act_step = new_sem("dve_step"), new_sem("dve_go"), new_sem("act_step")

        START = ([("w", n) for n in range(2 * NC)] + [("xt", b) for b in range(TB)] + [("w", 2 * NC), ("w", 2 * NC + 1)]
                 + [("k", 0), ("q", 0)] + [("w", n) for n in range(2 * NC + 2, 4 * NC)] + [("router", 4 * NC), ("bias", 0)])
        start_banks = [t[:].rearrange("p h k -> p (h k)") if t not in px else t[:] for t in (*px, *score, *pt)]

        def start_bank(use):
            return start_banks[START.index(use) % len(start_banks)]

        def started(use):
            kind, n = use
            if kind in ("w", "router"):
                return w_lo_done, n + 1
            return (bias_done, 1) if kind == "bias" else drained_by[kind].done(n, 0)

        FILL = {
            0: [("v", 0), ("k", 1)], 1: [("ot", 0), ("v", 1), ("q", 1)], 2: [("ot", 1), ("v", 2)], 3: [("ot", 2), ("v", 3)],
            4: [("ot", 3), ("k", 2)], 5: [("q", 2)], 6: [("o", 0)], 7: [("o", 1)],
            8: [("x2t", 0), ("k", 3)], 9: [("x2t", 1), ("logit", 0), ("q", 3)],
            10: [("logit", 1), ("xt", 0), ("xt", 1)], 11: [("xt", 2), ("o", 2), ("xt", 3)],
            12: [("o", 3), ("k", 0)], 13: [("x2t", 2), ("q", 0)], 14: [("x2t", 3), ("logit", 2)], 15: [("logit", 3)],
        }
        TAIL_FILL = {
            1: [("ot", 0)], 2: [("ot", 1)], 3: [("ot", 2)], 4: [("ot", 3)], 5: [("o", 0), ("o", 1)], 6: [("o", 2)],
            7: [("x2t", 0)], 8: [("o", 3), ("x2t", 1)], 9: [("logit", 0)], 10: [("x2t", 2)], 11: [("logit", 1)],
            12: [("x2t", 3)], 13: [("logit", 2)], 14: [("logit", 3)],
        }
        OF_NEXT = {("q", 0), ("k", 0)} | {("xt", b) for b in range(TB)}
        OF_BEFORE = ("ot", "o", "x2t", "logit")
        H2_ROWS = {7: 0, 8: 1, 12: 2, 13: 3}
        TAIL_ROWS = {7: 0, 8: 1, 9: 2, 11: 3}
        NORM1_STATS = {1: 0, 2: 1, 3: 2, 4: 3}
        NORM1_ROWS = {3: 0, 4: 1, 5: 2, 6: 3}
        drained_by = {"q": q_lo_done, "k": k_lo_done, "v": v_done, "xt": xt_lo_done, "ot": att_lo_done, "o": h2_done,
                      "x2t": xn2_t_done, "logit": logits_done}

        def group_of(use, i):
            return i + 1 if use in OF_NEXT else i - 1 if use[0] in OF_BEFORE else i

        def plan(flags):
            return TAIL_FILL if flags is TAIL else FILL

        def rows_plan(flags):
            return TAIL_ROWS if flags is TAIL else H2_ROWS

        def fill(s, flags):
            own, more, before = flags
            return [u for u in plan(flags).get(s, [])
                    if (before if u[0] in OF_BEFORE else more if u in OF_NEXT else own)]

        def lane(use, flags):
            return [u for s in range(UNITS) for u in plan(flags).get(s, [])].index(use) % 2

        def bank(use, flags):
            return px[lane(use, flags)][:]

        def uses_of(flags):
            return [u for s in range(UNITS) for u in fill(s, flags)]

        def bank_free(use, i, flags, flags_before):
            at, now = lane(use, flags), uses_of(flags)
            same = [u for u in now[:now.index(use)] if lane(u, flags) == at]
            if same:
                return drained_by[same[-1][0]].done(same[-1][1], group_of(same[-1], i))
            if flags_before is None:
                return None
            prior = [u for u in uses_of(flags_before) if lane(u, flags_before) == at][-1]
            return drained_by[prior[0]].done(prior[1], group_of(prior, i - 1))

        FIRST, MIDDLE, FINAL, TAIL = (True, True, False), (True, True, True), (True, False, True), (False, False, True)

        def chunks(t):
            return t.rearrange("p (c n) -> p c n", c=NC)

        block = mem.enter_context(nc.Block())

        @block.sync
        def _(sp):
            with nc.allow_non_contiguous_dma(reason="token ids, one per partition"):
                sp.dma_start(ids[:], x_ids.rearrange("b p -> p b")).then_inc(ids_in, 16)
            for n, w in enumerate(weights):
                if n >= 2:
                    sp.wait_ge(w_turned, NC * (n - 1))
                sp.dma_start(w_raw[n % 2], io[weights[w]].rearrange("(c p) n -> p c n", p=P)).then_inc(w_in[n], 16)
                if n == 1:
                    for s in stages:
                        s.credit(sp)
                    sp.sem_inc(credits_given, 1)
                    with nc.allow_non_contiguous_dma(reason="biases, one per partition"):
                        for m, name in enumerate(("L0_attn_bq", "L0_attn_bk", "L0_attn_bv")):
                            sp.dma_start(bias_in_t[:, m, :], io[name].rearrange("(c p) -> p c", p=P)).then_inc(bias_in, 16)
                    sp.dma_start(bias_o[:], io["L0_attn_bout"].rearrange("(a d) -> a d", a=1).broadcast_to((P, DIM)))\
                      .then_inc(bias_in, 16)
                    sp.dma_start(router_raw[0:EXPERTS, :], io["L0_ffn_W_router"]).then_inc(router_in, 16)
                    sp.dma_start(router_raw[EXPERTS:LOGITS, :], io["L0_ffn_W_sgate"]).then_inc(router_in, 16)
            sp.wait_ge(k_zeroed, 2)

            def wait(sem, count):
                sp.wait_ge(sem, count)
                sp.sem_inc(sp_go, 1)

            def spread(c, i):
                wait(*k_lo_done.done(c, i))
                wait(*scored.done(c * TB - TB - 1, i))
                for r in range(4):
                    rows = slice(r * HD, (r + 1) * HD)
                    sp.dma_start(k_diag[c % 2][rows, :, :, r, :].bitcast(F32), k_parts[c % 2][rows].bitcast(F32))\
                      .then_inc(k_spread.sems[c % 2], 16)

            def group(i, flags):
                own, more, before = flags
                for s in range(UNITS):
                    for use in fill(s, flags):
                        if use[0] == "k":
                            spread(use[1], group_of(use, i))
                        if use[0] == "o":
                            b = use[1]
                            wait(*h2_done.done(b, i - 1))
                            sp.dma_start(scratch["h2"][bass.ds(((i - 1) * TB + b) * P, P), :], res[b][:])\
                              .then_inc(*h2_out.inc(b))
                    if before and s in rows_plan(flags):
                        b = rows_plan(flags)[s]
                        wait(*xn2_done.done(b, i - 1))
                        sp.dma_start(scratch["xn2"][bass.ds(((i - 1) * TB + b) * P, P), :], xn2[b % 2])\
                          .then_inc(*xn2_out.inc(b))

            spread(0, 0)
            group(0, FIRST)
            with sp.Fori(1, last) as i:
                group(i, MIDDLE)
            group(last, FINAL)
            group(groups, TAIL)
            for b in range(TB):
                sp.wait_ge(*h2_out.done(b, last))
                sp.wait_ge(*xn2_out.done(b, last))

        @block.gpsimd
        def _(pool):
            pool.memset(eye[:], 0.0).then_inc(eye_zeroed, 1)
            pool.wait_ge(eye_zeroed, 1)
            pool.affine_select(out=eye[:], in_=eye[:], compare_op=ALU.not_equal, fill=1.0, base=0,
                               pattern=[[-1, P]], channel_multiplier=1).then_inc(eye_ready, 1)
            pool.wait_ge(credits_given, 1)
            pool.wait_ge(ids_in, 16)

            def gather(ids_tile, b, dst, inc):
                pool.indirect_dma_start(
                    out=dst, out_offset=None, in_=table,
                    in_offset=bass.IndirectOffsetOnAxis(ap=ids_tile[:, b:b + 1].bitcast(U32), axis=0)).then_inc(*inc)

            def group(i, more, before):
                if more:
                    pool.wait_ge(*xn_turned.done(TB - 1, i))
                if before:
                    for b in range(TB):
                        pool.wait_ge(*h2_out.done(b, i - 2))
                        pool.wait_ge(*xn2_done.done(b, i - 2))
                pool.sem_inc(pool_go, 1)
                if more:
                    pool.tensor_copy(ids_now[:], ids[:, bass.ds((i + 1) * TB, TB)])
                if before:
                    pool.tensor_copy(ids_then[:], ids[:, bass.ds((i - 1) * TB, TB)])
                pool.drain().then_inc(*ids_copied.inc())
                pool.wait_ge(*ids_copied.done(0, i + 1))
                pool.sem_inc(pool_go, 1)
                if more:
                    for b in range(TB):
                        gather(ids_now, b, h[b][:], h_in.inc(b))
                if before:
                    for b in range(TB):
                        gather(ids_then, b, res[b][:], res_in.inc(b))
                if more:
                    for b in range(TB):
                        pool.wait_ge(*h_in.done(b, i + 1))
                if before:
                    for b in range(TB):
                        pool.wait_ge(*res_in.done(b, i - 1))
                        pool.tensor_tensor(res[b][:], res[b][:], bias_o[:], ALU.add).then_inc(*res_done.inc())

            pool.tensor_copy(ids_now[:], ids[:, 0:TB]).then_inc(*ids_copied.inc())
            pool.wait_ge(*ids_copied.done(0, 0))
            for b in range(TB):
                gather(ids_now, b, h[b][:], h_in.inc(b))
            for tile in k_diag:
                pool.memset(tile[:].bitcast(F32), 0.0).then_inc(k_zeroed, 1)
            pool.memset(v_rows[:, :, :, HD:HD + 1], 1.0).then_inc(ones_ready, 1)
            for b in range(TB):
                pool.wait_ge(*h_in.done(b, 0))
            group(0, True, False)
            pool.wait_ge(bias_done, 1)
            with pool.Fori(1, last) as i:
                group(i, True, True)
            group(last, False, True)
            group(groups, False, True)

        @block.scalar
        def _(act):
            act.preload_act_table_set("natural_log_exp_and_others")
            steps = Count(act_step)

            def rsqrt(slot, i):
                act.wait_ge(*var_done[slot // TB].done(slot % TB, i))
                act.activation(small[:, slot, 1:2], small[:, slot, 0:1], ACT.Ln).then_inc(*steps.tick())
                act.wait_ge(*steps.so_far())
                act.activation(small[:, slot, 2:3], small[:, slot, 1:2], ACT.Exp, scale=-0.5)\
                   .then_inc(*y0_done[slot // TB].inc())

            def xt_split(b, i, src):
                act.wait_ge(*xn_turned.done(b, i))
                act.wait_ge(*q_made.done(NC - 1, i - 1))
                act.activation(xt_hi[:, :, b * P:(b + 1) * P], chunks(src), ACT.Copy).then_inc(*xt_hi_done.inc())

            def drain(use, i, src):
                kind, n = use
                if kind == "q":
                    act.wait_ge(*q_made.done(n, i))
                    act.wait_ge(*scored.done(n * TB - TB - 1, i))
                    act.activation(q_hi[n % 2][:], src, ACT.Identity, bias=bias_q[:, n:n + 1]).then_inc(*q_hi_done.inc())
                elif kind == "k":
                    act.wait_ge(*k_made.done(n, i))
                    act.wait_ge(*k_spread.done(n - 2, i))
                    act.activation(k_parts[n % 2][:, 0, :, :].rearrange("p b k -> p (b k)"), src, ACT.Identity,
                                   bias=bias_in_t[:, 1, n:n + 1]).then_inc(*k_hi_done.inc())
                elif kind == "v":
                    act.wait_ge(*v_made.done(n, i))
                    act.wait_ge(*av_made.done(UNITS - TB + n, i - 1))
                    act.activation(v_rows[:, n, :, 0:HD], src.rearrange("p (h d) -> p h d", d=HD), ACT.Copy)\
                       .then_inc(*v_done.inc())
                elif kind == "xt":
                    xt_split(n, i, src)
                elif kind == "ot":
                    act.wait_ge(*att_turned.done(n, i))
                    act.wait_ge(*o_made.done(n, i - 1))
                    act.activation(att_t[n][0][:], chunks(src), ACT.Copy).then_inc(*att_hi_done.inc())
                elif kind == "o":
                    rsqrt(TB + n, i)
                elif kind == "x2t":
                    act.wait_ge(*xn2_turned.done(n, i))
                    act.wait_ge(*logits_made.done(n - 2, i))
                    act.activation(xn2_t[n % 2], chunks(src), ACT.Copy).then_inc(*xn2_t_done.inc())

            act.wait_ge(credits_given, 1)
            for use in START:
                kind, n = use
                src = start_bank(use)
                if kind == "w":
                    w = list(weights)[n // NC]
                    act.wait_ge(w_turned, n + 1)
                    act.activation(w_hi[w][:, n % NC, :], src, ACT.Copy, scale=SCALE if w == "q" else 1.0)\
                       .then_inc(w_hi_done, 1)
                elif kind == "router":
                    act.activation(att_t[0][0][:], bias_in_t[:, 2, :].unsqueeze(2).broadcast_to((P, NC, P)), ACT.Copy)\
                       .then_inc(bv_hi_done, 1)
                elif kind in ("xt", "k", "q"):
                    if use == ("xt", 0):
                        for b in range(TB):
                            rsqrt(b, 0)
                    if use == ("k", 0):
                        act.wait_ge(bias_in, 64)
                        act.activation(bias_q[:], bias_in_t[:, 0, :], ACT.Copy, scale=SCALE).then_inc(*steps.tick())
                        act.wait_ge(*steps.so_far())
                    drain(use, 0, src)
            act.wait_ge(bias_made, 1)
            act.wait_ge(k_zeroed, 2)
            act.wait_ge(ones_ready, 1)

            def group(i, flags, carry=True):
                own, more, before = flags
                for s in range(UNITS):
                    if own:
                        act.wait_ge(*scored.done(s, i))
                        act.wait_ge(*max_done.done(s, i))
                        act.wait_ge(*prob_turned.done(s - 2, i))
                        for r in range(4):
                            x = act.activation(prob[s % 2][:, r, :], score[s % 2][:, r, :], ACT.Exp,
                                               bias=minus_max[:, s % 2, r:r + 1])
                        x.then_inc(*exp_done.inc())
                    u = s - 2
                    if (u >= 0 and own) or (u < 0 and carry):
                        act.wait_ge(*prob_turned.done(u, i))
                        act.wait_ge(*av_made.done(u - 2, i))
                        act.activation(prob_t[u % 2], pt[u % 2][:], ACT.Copy).then_inc(*prob_t_done.inc())
                    for use in fill(s, flags):
                        drain(use, group_of(use, i), bank(use, flags))
                    if more and s in NORM1_STATS:
                        rsqrt(NORM1_STATS[s], i + 1)

            group(0, FIRST, carry=False)
            with act.Fori(1, last) as i:
                steps.enter(i - 1, 2 * TB)
                group(i, MIDDLE)
                steps.leave(last - 1)
            group(last, FINAL)
            group(groups, TAIL)

        @block.vector
        def _(dve):
            steps = Count(dve_step)

            def link(ins):
                ins.then_inc(*steps.tick())
                dve.wait_ge(*steps.so_far())

            def norm_stats(slot, src):
                dve.bn_stats(stats[:, slot, :], src).then_inc(*steps.tick())
                dve.wait_ge(*steps.so_far())
                dve.sem_inc(dve_go, 1)
                link(dve.bn_aggr(mean_var[:, slot, :], stats[:, slot, :]))
                dve.tensor_scalar(small[:, slot, 0:1], mean_var[:, slot, 1:2], EPS, None, ALU.add)\
                   .then_inc(*var_done[slot // TB].inc())

            def norm_rows(slot, i, src, dst):
                s = small[:, slot, :]
                dve.wait_ge(*y0_done[slot // TB].done(slot % TB, i))
                link(dve.scalar_tensor_tensor(out=s[:, 3:4], in0=s[:, 2:3], scalar=s[:, 0:1], in1=s[:, 2:3],
                                              op0=ALU.mult, op1=ALU.mult))
                link(dve.tensor_scalar(s[:, 4:5], s[:, 3:4], -0.5, 1.5, ALU.mult, ALU.add))
                link(dve.tensor_tensor(s[:, 5:6], s[:, 2:3], s[:, 4:5], ALU.mult))
                return dve.tensor_scalar(dst, src, mean_var[:, slot, 0:1], s[:, 5:6], ALU.subtract, ALU.mult)

            def norm1_stats(b, i):
                dve.wait_ge(*h_in.done(b, i))
                norm_stats(b, h[b][:])

            def norm1_rows(b, i):
                norm_rows(b, i, h[b][:], h[b][:]).then_inc(*xn_done.inc())

            def lo_part(src, hi, lo, inc):
                dve.tensor_tensor(lo, src, hi.bitcast(F32), ALU.subtract).then_inc(*inc)

            def drain(use, i, src):
                kind, n = use
                if kind == "q":
                    dve.wait_ge(*q_hi_done.done(n, i))
                    dve.scalar_tensor_tensor(out=q_lo[n % 2][:], in0=src, scalar=bias_q[:, n:n + 1],
                                             in1=q_hi[n % 2][:].bitcast(F32), op0=ALU.add, op1=ALU.subtract)\
                       .then_inc(*q_lo_done.inc())
                elif kind == "k":
                    hi, lo = (k_parts[n % 2][:, m, :, :].rearrange("p b k -> p (b k)") for m in range(2))
                    dve.wait_ge(*k_hi_done.done(n, i))
                    dve.scalar_tensor_tensor(out=lo, in0=src, scalar=bias_in_t[:, 1, n:n + 1], in1=hi.bitcast(F32),
                                             op0=ALU.add, op1=ALU.subtract).then_inc(*k_lo_done.inc())
                elif kind == "xt":
                    cols = slice(n * P, (n + 1) * P)
                    dve.wait_ge(*xt_hi_done.done(n, i))
                    lo_part(chunks(src), xt_hi[:, :, cols], xt_lo[:, :, cols], xt_lo_done.inc())
                elif kind == "ot":
                    dve.wait_ge(*att_hi_done.done(n, i))
                    lo_part(chunks(src), att_t[n][0][:], att_t[n][1][:], att_lo_done.inc())
                elif kind == "o":
                    dve.wait_ge(*o_made.done(n, i))
                    dve.wait_ge(*res_done.done(n, i))
                    dve.tensor_tensor(res[n][:], src, res[n][:], ALU.add).then_inc(*h2_done.inc())
                    dve.wait_ge(*h2_done.done(n, i))
                    norm_stats(TB + n, res[n][:])
                elif kind == "logit":
                    dve.wait_ge(*logits_made.done(n, i))
                    dve.tensor_copy(keep["logits"][:, bass.ds(i * TB + n, 1), :], src[:, 0:LOGITS].unsqueeze(1))\
                       .then_inc(*logits_done.inc())

            dve.wait_ge(credits_given, 1)
            for use in START:
                kind, n = use
                src = start_bank(use)
                if kind == "w":
                    w, c = list(weights)[n // NC], n % NC
                    dve.wait_ge(w_hi_done, n + 1)
                    dve.scalar_tensor_tensor(out=w_lo[w][:, c, :], in0=src, scalar=SCALE if w == "q" else 1.0,
                                             in1=w_hi[w][:, c, :].bitcast(F32), op0=ALU.mult, op1=ALU.subtract)\
                       .then_inc(w_lo_done, 1)
                elif kind == "router":
                    dve.wait_ge(w_turned, n + 1)
                    dve.tensor_copy(router_t[:], src[:, 0:NC * LOGITS].rearrange("p (c n) -> p c n", c=NC)).then_inc(w_lo_done, 1)
                    dve.wait_ge(bv_hi_done, 1)
                    lo_part(bias_in_t[:, 2, :].unsqueeze(2).broadcast_to((P, NC, P)), att_t[0][0][:], att_t[0][1][:],
                            (bv_lo_done, 1))
                elif kind == "bias":
                    dve.wait_ge(bias_made, 1)
                    dve.wait_ge(bias_in, 64)
                    dve.tensor_tensor(bias_o[:], src, bias_o[:], ALU.add).then_inc(bias_done, 1)
                else:
                    if use == ("xt", 0):
                        for b in range(TB):
                            norm1_stats(b, 0)
                        for b in range(TB):
                            norm1_rows(b, 0)
                    drain(use, 0, src)

            def group(i, flags, carry=True):
                own, more, before = flags
                for s in range(UNITS):
                    if own:
                        dve.wait_ge(*scored.done(s, i))
                        dve.wait_ge(*exp_done.done(s - 2, i))
                        dve.reduce_max(minus_max[:, s % 2, :], score[s % 2][:], AX_X, negate=True)\
                           .then_inc(*max_done.inc())
                    if before and s in rows_plan(flags):
                        b = rows_plan(flags)[s]
                        dve.wait_ge(*xn2_out.done(b - 2, i - 1))
                        dve.wait_ge(*xn2_turned.done(b - 2, i - 1))
                        norm_rows(TB + b, i - 1, res[b][:], xn2[b % 2]).then_inc(*xn2_done.inc())
                    if more and s in NORM1_ROWS:
                        norm1_rows(NORM1_ROWS[s], i + 1)
                    u = s - 4
                    if (u >= 0 and own) or (u < 0 and carry):
                        c, b, inv = u % UNITS // TB, u % TB, inv_sum[:, u % 2, :]
                        dve.wait_ge(*av_made.done(u, i))
                        link(dve.reciprocal(inv.unsqueeze(2), av[u % 2][:, :, HD:HD + 1]))
                        dve.wait_ge(*att_turned.done(b, (i if u >= 0 else i - 1) - 1))
                        dve.tensor_tensor(att[b][:, 4 * c:4 * c + 4, :], av[u % 2][:, :, 0:HD],
                                          inv.unsqueeze(2).broadcast_to((P, 4, HD)), ALU.mult).then_inc(*att_done.inc())
                    for use in fill(s, flags):
                        drain(use, group_of(use, i), bank(use, flags))
                    if more and s in NORM1_STATS:
                        norm1_stats(NORM1_STATS[s], i + 1)

            group(0, FIRST, carry=False)
            with dve.Fori(1, last) as i:
                steps.enter(i - 1, UNITS + 2 * TB * (2 + 3))
                group(i, MIDDLE)
                steps.leave(last - 1)
            group(last, FINAL)
            group(groups, TAIL)

        @block.tensor
        def _(pe):
            pe.wait_ge(eye_ready, 1)

            def turn(dst, src, rows=P):
                for c in range(NC):
                    x = pe.transpose(dst[:, c * rows:(c + 1) * rows], src(c), eye[0:rows, 0:rows])
                return x

            def project(dst, stationary, moving):
                for ic in range(NC):
                    x = split_product(pe, dst, stationary(ic), moving(ic), ic == 0, ic == NC - 1)
                return x

            def make(use, i, dst):
                kind, n = use
                cols = slice(n * P, (n + 1) * P)
                xt, both = (xt_hi, xt_lo), (w_hi, w_lo)
                if kind in "qk":
                    if n == 0:
                        pe.wait_ge(*xt_lo_done.done(TB - 1, i))
                    project(dst, lambda ic: [m[kind][:, ic, cols] for m in both], lambda ic: [m[:, ic, :] for m in xt])\
                        .then_inc(*(q_made if kind == "q" else k_made).inc())
                elif kind == "v":
                    project(dst, lambda ic: [m[:, ic, cols] for m in xt], lambda ic: [m["v"][:, ic, :] for m in both])\
                        .then_inc(*v_made.inc())
                elif kind == "xt":
                    pe.wait_ge(*xn_done.done(n, i))
                    turn(dst, lambda c: h[n][:, c * P:(c + 1) * P]).then_inc(*xn_turned.inc())
                elif kind == "ot":
                    pe.wait_ge(*att_done.done(UNITS - TB + n, i))
                    rows = att[n][:].rearrange("p h d -> p (h d)")
                    turn(dst, lambda c: rows[:, c * P:(c + 1) * P]).then_inc(*att_turned.inc())
                elif kind == "o":
                    pe.wait_ge(*att_lo_done.done(n, i))
                    project(dst, lambda ic: [m[:, ic, :] for m in att_t[n]], lambda ic: [m["o"][:, ic, :] for m in both])\
                        .then_inc(*o_made.inc())
                elif kind == "x2t":
                    pe.wait_ge(*xn2_done.done(n, i))
                    turn(dst, lambda c: xn2[n % 2][:, c * P:(c + 1) * P]).then_inc(*xn2_turned.inc())
                elif kind == "logit":
                    pe.wait_ge(*xn2_t_done.done(n, i))
                    for c in range(NC):
                        x = pe.matmul(dst[:, 0:LOGITS], xn2_t[n % 2][:, c, :], router_t[:, c, :],
                                      start=c == 0, stop=c == NC - 1)
                    x.then_inc(*logits_made.inc())

            pe.wait_ge(credits_given, 1)
            for at, use in enumerate(START):
                kind, n = use
                dst = start_bank(use)
                if at >= len(start_banks):
                    pe.wait_ge(*started(START[at - len(start_banks)]))
                if kind == "w":
                    w, c = n // NC, n % NC
                    if c == 0:
                        pe.wait_ge(w_in[w], 16)
                    turn(dst, lambda oc: w_raw[w % 2][:, oc, c * P:(c + 1) * P]).then_inc(w_turned, 1)
                elif kind == "router":
                    pe.wait_ge(router_in, 32)
                    turn(dst, lambda c: router_raw[:, c * P:(c + 1) * P], rows=LOGITS).then_inc(w_turned, 1)
                elif kind == "bias":
                    pe.wait_ge(bv_lo_done, 1)
                    pe.wait_ge(w_lo_done, 4 * NC)
                    project(dst, lambda ic: [m[:, ic, :] for m in att_t[0]], lambda ic: [m["o"][:, ic, :] for m in (w_hi, w_lo)])\
                        .then_inc(bias_made, 1)
                else:
                    if use == ("k", 0):
                        pe.wait_ge(w_lo_done, 2 * NC)
                    make(use, 0, dst)
            for use in START[-len(start_banks):]:
                pe.wait_ge(*started(use))

            def group(i, flags, flags_before, carry=True):
                own, more, before = flags
                for s in range(UNITS):
                    if own:
                        c, b = s // TB, s % TB
                        if b == 0:
                            pe.wait_ge(*q_lo_done.done(c, i))
                            pe.wait_ge(*k_spread.done(c, i))
                        pe.wait_ge(*exp_done.done(s - 2, i))
                        split_product(pe, score[s % 2][:].rearrange("p h k -> p (h k)"),
                                      [m[c % 2][:, b * P:(b + 1) * P] for m in (q_hi, q_lo)],
                                      [k_diag[c % 2][:, m, b, :, :].rearrange("p h k -> p (h k)") for m in range(2)],
                                      True, True).then_inc(*scored.inc())
                    u = s - 2
                    if (u >= 0 and own) or (u < 0 and carry):
                        pe.wait_ge(*prob_t_done.done(u - 2, i))
                        pe.wait_ge(*exp_done.done(u, i))
                        for r in range(4):
                            x = pe.transpose(pt[u % 2][:, r, :], prob[u % 2][:, r, :], eye[:])
                        x.then_inc(*prob_turned.inc())
                    u = s - 3
                    if (u >= 0 and own) or (u < 0 and carry):
                        c, b = u % UNITS // TB, u % TB
                        if u >= 0 and c == 0:
                            pe.wait_ge(*v_done.done(b, i))
                        pe.wait_ge(*att_done.done(u - 2, i))
                        pe.wait_ge(*prob_t_done.done(u, i))
                        for r in range(4):
                            x = pe.matmul(av[u % 2][:, r, :], prob_t[u % 2][:, r, :], v_rows[:, b, 4 * c + r, :],
                                          start=True, stop=True)
                        x.then_inc(*av_made.inc())
                    for use in fill(s, flags):
                        free = bank_free(use, i, flags, flags_before)
                        if free is not None:
                            pe.wait_ge(*free)
                        make(use, group_of(use, i), bank(use, flags))

            group(0, FIRST, None, carry=False)
            pe.wait_ge(*q_lo_done.done(0, 1))
            pe.wait_ge(*k_lo_done.done(0, 1))
            with pe.Fori(1, last) as i:
                group(i, MIDDLE, MIDDLE)
            group(last, FINAL, MIDDLE)
            group(groups, TAIL, FINAL)


def routing_phase(nc, new_sem, keep, io, scratch):
    logits, gates, slots = keep["logits"], keep["gates"], keep["slots"]
    tiles = logits.shape[1]
    slot_tiles = keep["tile_expert"].shape[1]
    slot_cols = slot_tiles * TB
    E = EXPERTS

    with ExitStack() as mem:
        def sb(name, shape, dt=F32):
            return mem.enter_context(nc.sbuf_tensor(name, shape, dt))

        def over_experts(x):
            return x.broadcast_to((P, tiles, E))

        shifted = sb("shifted", [P, tiles, E])
        expd = sb("expd", [P, tiles, E])
        probs = sb("probs", [P, tiles, E])
        row = sb("row", [P, tiles, 1])
        row_inv = sb("row_inv", [P, tiles, 1])
        first_of = sb("first_of", [P, 1, E])
        equal = sb("equal", [P, tiles, E])
        index = sb("index", [P, tiles, E])
        least = sb("least", [P, tiles, 1])
        rest = sb("rest", [P, tiles, E])
        chosen = [sb(f"chosen{k}", [P, tiles, E]) for k in range(TOPK)]
        either = sb("either", [P, tiles, E])
        before = sb("before", [P, P])
        ones = sb("ones", [P, P])
        totals = sb("totals", [P, tiles, E])
        run = [sb(f"run{n}", [P, 2 * tiles, E]) for n in range(2)]
        tile_run = [sb(f"tile_run{n}", [P, 2 * E]) for n in range(2)]
        count_int = sb("count_int", [P, E], I32)
        tiles_int = sb("tiles_int", [P, E], I32)
        tiles_of = sb("tiles_of", [P, E])
        base = sb("base", [P, 1, E])
        slot_of = sb("slot_of", [P, tiles, E])
        slot_f = sb("slot_f", [P, TOPK, tiles])
        slot_part = [sb(f"slot_part{n}", [P, TOPK, tiles], I32) for n in range(2)]
        slot_lo = sb("slot_lo", [P, TOPK * tiles])
        slot_hi = sb("slot_hi", [P, TOPK * tiles])
        int_iota = sb("int_iota", [P, P], I32)
        lane = sb("lane", [P, P])
        token_int = sb("token_int", [P, tiles], I32)
        token = sb("token", [P, tiles])
        under = sb("under", [P, slot_tiles, E])
        expert_f = sb("expert_f", [P, slot_tiles, 1])
        expert_int = keep["tile_expert"]
        HOT, SHARE = 6, 3
        hot_lo = [sb(f"hot_lo{n}", [P, P], F32R) for n in range(HOT)]
        hot_hi = [sb(f"hot_hi{n}", [P, slot_cols], F32R) for n in range(HOT)]
        rank_ps = mem.enter_context(nc.psum_tensor("rank_ps", [P, tiles * E], F32))
        total_ps = mem.enter_context(nc.psum_tensor("total_ps", [P, tiles * E], F32))
        slot_ps = mem.enter_context(nc.psum_tensor("slot_ps", [P, slot_cols], F32))

        masks_made = new_sem("masks_made")
        step = new_sem("route_step")
        shifted_done, exp_ready, either_done = new_sem("shifted_done"), new_sem("exp_ready"), new_sem("either_done")
        gate_done = new_sem("gate_done")
        ranked, slots_ready, hot_used = new_sem("ranked"), new_sem("slots_ready"), new_sem("hot_used")
        hot_made, hot_hi_made = new_sem("hot_made"), new_sem("hot_hi_made")
        def make_hot_hi(eng, n):
            return eng.tensor_scalar(hot_hi[n % HOT][:], lane[:, 0:slot_cols], slot_hi[:, n:n + 1],
                                     token[:, n % tiles:n % tiles + 1], ALU.is_equal, ALU.mult)

        block = mem.enter_context(nc.Block())

        @block.gpsimd
        def _(pool):
            pool.memset(before[:], 0.0).then_inc(masks_made, 1)
            pool.memset(ones[:], 1.0).then_inc(masks_made, 1)
            pool.iota(int_iota[:], pattern=[[1, P]], base=0, channel_multiplier=0).then_inc(masks_made, 1)
            pool.iota(token_int[:], pattern=[[P, tiles]], base=0, channel_multiplier=1).then_inc(masks_made, 1)
            pool.wait_ge(masks_made, 1)
            pool.affine_select(out=before[:], in_=before[:], compare_op=ALU.is_ge, fill=1.0, base=0,
                               pattern=[[-1, P]], channel_multiplier=1).then_inc(masks_made, 1)
            pool.wait_ge(slots_ready, 1)
            for n in range(0, TOPK * tiles, SHARE):
                if n >= HOT:
                    pool.wait_ge(hot_used, n - HOT + 1)
                make_hot_hi(pool, n).then_inc(hot_hi_made, 1)

        @block.scalar
        def _(act):
            act.wait_ge(shifted_done, 1)
            act.activation(expd[:], shifted[:], ACT.Exp).then_inc(exp_ready, 1)
            act.activation(gates[:, :, TOPK:TOPK + 1], logits[:, :, E:E + 1], ACT.Sigmoid).then_inc(gate_done, 1)
            act.wait_ge(gate_done, 1)

        @block.tensor
        def _(pe):
            pe.wait_ge(either_done, 1)
            pe.wait_ge(masks_made, 5)
            picked = either[:].rearrange("p t e -> p (t e)")
            pe.matmul(rank_ps[:], before[:], picked, start=True, stop=True).then_inc(ranked, 1)
            pe.matmul(total_ps[:], ones[:], picked, start=True, stop=True).then_inc(ranked, 1)
            n = TOPK * tiles
            for k in range(n):
                pe.wait_ge(hot_made, k + 1)
                pe.wait_ge(hot_hi_made, k // SHARE + 1)
                pe.matmul(slot_ps[:], hot_lo[k % HOT][:], hot_hi[k % HOT][:], start=k == 0, stop=k == n - 1)\
                  .then_inc(hot_used, 1)

        @block.vector
        def _(dve):
            steps = Count(step)

            def link(ins):
                ins.then_inc(*steps.tick())
                dve.wait_ge(*steps.so_far())

            scores = logits[:, :, 0:E]
            link(dve.reduce_max(row[:], scores, AX_X))
            dve.tensor_tensor(shifted[:], scores, over_experts(row[:]), ALU.subtract).then_inc(shifted_done, 1)
            dve.wait_ge(masks_made, 4)
            dve.tensor_copy(lane[:], int_iota[:]).then_inc(*steps.tick())
            dve.tensor_copy(token[:], token_int[:]).then_inc(*steps.tick())
            dve.tensor_copy(keep["slot_token"][:, slot_cols:], token_int[:, 0:TB]).then_inc(*steps.tick())
            dve.tensor_scalar(first_of[:, 0, :], int_iota[:, 0:E], float(-E), None, ALU.add).then_inc(*steps.tick())
            for r in (*run, *tile_run):
                dve.memset(r[:], 0.0).then_inc(*steps.tick())
            dve.wait_ge(exp_ready, 1)
            link(dve.tensor_reduce(row[:], expd[:], AX_X, ALU.add))
            link(dve.reciprocal(row_inv[:], row[:]))
            link(dve.tensor_tensor(probs[:], expd[:], over_experts(row_inv[:]), ALU.mult))
            left = probs
            for k in range(TOPK):
                best = gates[:, :, k:k + 1]
                link(dve.reduce_max(best, left[:], AX_X))
                link(dve.tensor_tensor(equal[:], left[:], over_experts(best), ALU.is_equal))
                link(dve.tensor_tensor(index[:], equal[:], first_of[:].broadcast_to((P, tiles, E)), ALU.mult))
                link(dve.tensor_reduce(least[:], index[:], AX_X, ALU.min))
                link(dve.tensor_tensor(chosen[k][:], index[:], over_experts(least[:]), ALU.is_equal))
                if k == 0:
                    link(dve.scalar_tensor_tensor(out=rest[:], in0=chosen[k][:], scalar=-2.0, in1=probs[:],
                                                  op0=ALU.mult, op1=ALU.add))
                    left = rest
            dve.tensor_tensor(either[:], chosen[0][:], chosen[1][:], ALU.add).then_inc(either_done, 1)
            dve.wait_ge(ranked, 2)
            tot = total_ps[:].rearrange("p (t e) -> p t e", e=E)
            link(dve.tensor_copy(totals[:], tot))
            link(dve.tensor_copy(run[0][:, tiles:, :], totals[:]))
            cur, shift = 0, 1
            while shift < tiles:
                link(dve.tensor_tensor(run[1 - cur][:, tiles:, :], run[cur][:, tiles:, :],
                                       run[cur][:, tiles - shift:2 * tiles - shift, :], ALU.add))
                cur, shift = 1 - cur, 2 * shift
            through = run[cur][:, tiles:, :]
            link(dve.tensor_scalar(count_int[:], through[:, tiles - 1, :], float(GT - 1), None, ALU.add))
            link(dve.tensor_scalar(tiles_int[:], count_int[:], GT.bit_length() - 1, None, ALU.arith_shift_right))
            link(dve.tensor_copy(tiles_of[:], tiles_int[:]))
            link(dve.tensor_copy(tile_run[0][:, E:], tiles_of[:]))
            at, shift = 0, 1
            while shift < E:
                link(dve.tensor_tensor(tile_run[1 - at][:, E:], tile_run[at][:, E:],
                                       tile_run[at][:, E - shift:2 * E - shift], ALU.add))
                at, shift = 1 - at, 2 * shift
            ends = tile_run[at][:, E:]
            link(dve.tensor_tensor(base[:, 0, :], ends, tiles_of[:], ALU.subtract))
            link(dve.tensor_scalar(base[:, 0, :], base[:, 0, :], float(GT), None, ALU.mult))
            link(dve.tensor_tensor(slot_of[:], rank_ps[:].rearrange("p (t e) -> p t e", e=E), through, ALU.add))
            link(dve.tensor_tensor(slot_of[:], slot_of[:], totals[:], ALU.subtract))
            link(dve.tensor_tensor(slot_of[:], slot_of[:], base[:].broadcast_to((P, tiles, E)), ALU.add))
            for k in range(TOPK):
                link(dve.tensor_tensor(index[:], chosen[k][:], slot_of[:], ALU.mult))
                link(dve.tensor_reduce(slot_f[:, k, :].unsqueeze(2), index[:], AX_X, ALU.add))
            link(dve.tensor_copy(slots[:], slot_f[:]))
            link(dve.tensor_scalar(slot_part[0][:], slots[:], P - 1, None, ALU.bitwise_and))
            link(dve.tensor_scalar(slot_part[1][:], slots[:], P.bit_length() - 1, None, ALU.arith_shift_right))
            link(dve.tensor_copy(slot_lo[:], slot_part[0][:].rearrange("p k t -> p (k t)")))
            dve.tensor_copy(slot_hi[:], slot_part[1][:].rearrange("p k t -> p (k t)")).then_inc(slots_ready, 1)
            link(dve.tensor_tensor(under[:], ends.unsqueeze(1).broadcast_to((P, slot_tiles, E)),
                                   lane[:, 0:slot_tiles].unsqueeze(2).broadcast_to((P, slot_tiles, E)), ALU.is_le))
            link(dve.tensor_reduce(expert_f[:], under[:], AX_X, ALU.add))
            link(dve.tensor_scalar(expert_int[:], expert_f[:, :, 0], float(E - 1), None, ALU.min))
            for n in range(TOPK * tiles):
                if n >= HOT:
                    dve.wait_ge(hot_used, n - HOT + 1)
                x = dve.tensor_scalar(hot_lo[n % HOT][:], lane[:], slot_lo[:, n:n + 1], None, ALU.is_equal)
                if n % SHARE:
                    x = make_hot_hi(dve, n)
                x.then_inc(hot_made, 1)
            dve.wait_ge(hot_used, TOPK * tiles)
            link(dve.tensor_copy(keep["slot_token"][:, 0:slot_cols], slot_ps[:]))


def ffn_phase(nc, new_sem, keep, io, scratch, shared):
    eye = keep["eye"]
    tag = "s" if shared else "e"
    inner = I_SH if shared else I_MOE
    NM = -(-inner // P)
    size = [min(P, inner - m * P) for m in range(NM)]
    tiles = (scratch["h2"].shape[0] // GT) if shared else keep["tile_expert"].shape[1]
    last = tiles - 1
    SQ = 2 * (I_SH // P)
    assert NM % 2 == 1

    with ExitStack() as mem:
        def sb(name, shape, dt=F32):
            return mem.enter_context(nc.sbuf_tensor(f"{tag}_{name}", shape, dt))

        def ps(name, shape):
            return mem.enter_context(nc.psum_tensor(f"{tag}_{name}", shape, F32))

        def stage(name, per, **kw):
            s = Stage(new_sem, f"{tag}_{name}", per, **kw)
            stages.append(s)
            return s

        stages = []
        if shared:
            gu_hi, gu_lo = keep["gu_hi"], keep["gu_lo"]
            dn_hi, dn_lo = sb("dn_hi", [P, NM, DIM], F32R), sb("dn_lo", [P, NM, DIM], F32R)
            dn_raw = [sb(f"dn_raw{n}", [P, DIM]) for n in range(2)]
        else:
            gu_hi, gu_lo = sb("gu_hi", [P, 2, NC, inner], F32R), sb("gu_lo", [P, 2, NC, inner], F32R)
            gu_raw = [sb(f"gu_raw{m}", [P, 2, NC, size[m]]) for m in range(NM)]
            dn_hi, dn_lo = sb("dn_hi", [P, NM, DIM], F32R), sb("dn_lo", [P, NM, DIM], F32R)
            dn_raw = [sb(f"dn_raw{m}", [P, DIM]) for m in range(NM)]
            sh_raw = [sb(f"sh_raw{n}", [P, NC, P]) for n in range(1)]
            rows_now = sb("rows_now", [P, TB], I32)
        x, xt_hi, xt_lo = keep["x"], keep["xt_hi"], keep["xt_lo"]
        silu = [sb(f"silu{n}", [P, GT]) for n in range(2)]
        act_f = [sb(f"act{n}", [P, GT]) for n in range(2)]
        act_hi = [sb(f"act_hi{n}", [P, GT], F32R) for n in range(2)]
        act_lo = [sb(f"act_lo{n}", [P, GT], F32R) for n in range(2)]
        out = [sb(f"out{b}", [P, DIM]) for b in range(TB)]
        if shared:
            picked = [[sb(f"picked{k}{n}", [P, DIM]) for n in range(2)] for k in range(TOPK)]
            slots_now = sb("slots_now", [P, TOPK, TB], I32)
            gates_now = sb("gates_now", [P, TB, TOPK + 1])
        banks = [ps(f"bank{n}", [P, GT]) for n in range(4)]
        acc = [ps(f"acc{b}", [P, DIM]) for b in range(TB)]

        x_turned = stage("x_turned", TB, ahead=shared)
        gate_made, up_made = stage("gate_made", NM), stage("up_made", NM)
        down_made = stage("down_made", NM)
        xt_hi_done = stage("xt_hi_done", TB, ahead=shared)
        silu_done, act_hi_done = stage("silu_done", NM), stage("act_hi_done", NM)
        xt_lo_done = stage("xt_lo_done", TB, ahead=shared)
        act_done, act_lo_done = stage("act_done", NM), stage("act_lo_done", NM)
        if shared:
            x_in = stage("x_in", TB, dma=True, lanes=TB, ahead=True)
            res_in = stage("res_in", TB, dma=True, lanes=TB)
            picked_in = [stage(f"picked_in{k}", TB, dma=True, lanes=2, credit=False) for k in range(TOPK)]
            slots_copied, gates_copied = stage("slots_copied", 1), stage("gates_copied", 1)
            joined = [stage(f"joined{n}", TB) for n in range(1 + TOPK)]
            acc_read = joined[0]
            dn_in = [new_sem(f"s_dn_in{n}") for n in range(2)]
            dn_hi_ready, dn_lo_ready = new_sem("s_dn_hi_ready"), new_sem("s_dn_lo_ready")
        else:
            x_in = stage("x_in", TB, dma=True, lanes=TB, credit=False)
            acc_read = stage("acc_read", TB)
            gu_in = stage("gu_in", NM, dma=True, lanes=NM)
            gu_in.unit = 32
            dn_in = stage("dn_in", NM, dma=True, lanes=NM)
            gu_hi_done, gu_lo_done = stage("gu_hi_done", NM), stage("gu_lo_done", NM)
            dn_hi_done, dn_lo_done = stage("dn_hi_done", NM), stage("dn_lo_done", NM)
            sh_in = stage("sh_in", 1, dma=True)
            sh_hi_done, sh_lo_done = stage("sh_hi_done", 1), stage("sh_lo_done", 1)
            rows_copied = new_sem("e_rows_copied")
        out_sent = stage("out_sent", TB, dma=True, lanes=len(out))
        pool_go, sp_go = keep["pool_go"], keep["sp_go"]
        credits_given, lap = keep["credits_given"], 3 if shared else 2

        uses = []
        for m in range(NM):
            first = 0 if m % 2 else 2
            uses += [(("gate", m), first, silu_done), (("up", m), first + 1, act_done)]
            if m == NM - 1:
                uses += [(("x", b), b % 2, xt_lo_done) for b in range(TB)]

        def bank(kind, n):
            return next(banks[w] for use, w, _ in uses if use == (kind, n))

        def bank_free(kind, n, i, more=True):
            own = [u for u in uses if more or u[0][0] != "x"]
            at = next(k for k, u in enumerate(own) if u[0] == (kind, n))
            where = own[at][1]
            if any(u[1] == where for u in own[:at]):
                (what, k), _, by = [u for u in own[:at] if u[1] == where][-1]
                back = 0
            else:
                (what, k), _, by = [u for u in uses if u[1] == where][-1]
                back = 1
            return by.done(k, i - back + (what == "x"))

        def gu_parts(which, m):
            if shared:
                q = which * NM + m
                return lambda ic: [w[:, q, ic, :] for w in (gu_hi, gu_lo)]
            return lambda ic: [w[:, which, ic, m * P:m * P + size[m]] for w in (gu_hi, gu_lo)]

        block = mem.enter_context(nc.Block())

        @block.sync
        def _(sp):
            for s in stages:
                s.credit(sp)
            sp.sem_inc(credits_given, 1)
            if shared:
                def load_x(i):
                    for b in range(TB):
                        sp.wait_ge(*x_turned.done(b, i - 1))
                        sp.dma_start(x[b][:], scratch["xn2"][bass.ds((i * TB + b) * P, P), :]).then_inc(*x_in.inc(b))

                def load_residual(i):
                    for b in range(TB):
                        sp.wait_ge(*out_sent.done(b, i - 1))
                        sp.dma_start(out[b][:], scratch["h2"][bass.ds((i * TB + b) * P, P), :]).then_inc(*res_in.inc(b))

                def send(i):
                    for b in range(TB):
                        sp.wait_ge(*joined[TOPK].done(b, i))
                        sp.dma_start(io["out"][bass.ds((i * TB + b) * P, P), :], out[b][:]).then_inc(*out_sent.inc(b))

                for m in range(NM):
                    if m >= 2:
                        sp.wait_ge(dn_lo_ready, m - 1)
                    sp.dma_start(dn_raw[m % 2][:], io["L0_ffn_Ws_down"][m * P:(m + 1) * P, :]).then_inc(dn_in[m % 2], 16)
                    if m == 1:
                        load_residual(0)
                        load_x(1)
                with sp.Fori(1, last) as i:
                    load_x(i + 1)
                    send(i - 1)
                    load_residual(i)
                send(last - 1)
                load_residual(last)
                send(last)
                for b in range(TB):
                    sp.wait_ge(*out_sent.done(b, last))
            else:
                def tile(j, more):
                    sp.sem_inc(sp_go, 1)
                    e = sp.value_load(keep["tile_expert"][0:1, bass.ds(j, 1)], min_val=0, max_val=EXPERTS - 1)
                    gu = io["L0_ffn_We_gate_up"][bass.ds(e, 1)].rearrange("a (c p) (w n) -> p (a w) c n", p=P, w=2)
                    dn = io["L0_ffn_We_down"][bass.ds(e, 1)].rearrange("a i n -> (a i) n")
                    for m in range(NM):
                        sp.wait_ge(*gu_lo_done.done(m, j - 1))
                        for w in range(2):
                            sp.dma_start(gu_raw[m][:, w, :, :], gu[:, w, :, m * P:m * P + size[m]])\
                              .then_inc(gu_in.sems[m], 16)
                    for m in range(NM):
                        sp.wait_ge(*dn_lo_done.done(m, j - 1))
                        sp.dma_start(dn_raw[m][0:size[m], :], dn[m * P:m * P + size[m], :]).then_inc(*dn_in.inc(m))
                    if more:
                        sp.wait_ge(*sh_lo_done.done(0, j - 1))
                        sp.dma_start(sh_raw[0][:], io["L0_ffn_Ws_gate_up"][:, bass.ds(j * P, P)]
                                     .rearrange("(c p) n -> p c n", p=P)).then_inc(*sh_in.inc())

                assert last == SQ
                with sp.Fori(0, last) as j:
                    tile(j, True)
                tile(last, False)

        @block.gpsimd
        def _(pool):
            if shared:
                with pool.Fori(0, tiles) as i:
                    pool.wait_ge(*joined[TOPK].done(TB - 1, i - 1))
                    pool.sem_inc(pool_go, 1)
                    pool.tensor_copy(slots_now[:], keep["slots"][:, :, bass.ds(i * TB, TB)]).then_inc(*slots_copied.inc())
                    pool.wait_ge(*slots_copied.done(0, i))
                    for b in range(TB):
                        pool.wait_ge(*joined[TOPK].done(b - 2, i))
                        pool.sem_inc(pool_go, 1)
                        for k in range(TOPK):
                            pool.indirect_dma_start(
                                out=picked[k][b % 2][:], out_offset=None, in_=scratch["expert_rows"],
                                in_offset=bass.IndirectOffsetOnAxis(ap=slots_now[:, k, b:b + 1].bitcast(U32), axis=0),
                            ).then_inc(*picked_in[k].inc(b))
            else:
                def gather(j):
                    pool.tensor_copy(rows_now[:], keep["slot_token"][:, bass.ds(j * TB, TB)]).then_inc(rows_copied, 1)
                    pool.wait_ge(rows_copied, j + 1)
                    pool.sem_inc(pool_go, 1)
                    for b in range(TB):
                        pool.indirect_dma_start(
                            out=x[b][:], out_offset=None, in_=scratch["xn2"],
                            in_offset=bass.IndirectOffsetOnAxis(ap=rows_now[:, b:b + 1].bitcast(U32), axis=0),
                        ).then_inc(*x_in.inc(b))

                pool.wait_ge(credits_given, lap)
                gather(0)
                with pool.Fori(1, tiles + 1) as j:
                    for b in range(TB):
                        pool.wait_ge(*x_in.done(b, j - 1))
                    pool.wait_ge(*x_turned.done(TB - 1, j - 1))
                    pool.sem_inc(pool_go, 1)
                    gather(j)

        @block.scalar
        def _(act):
            act.preload_act_table(ACT.Silu)
            act.wait_ge(credits_given, lap)

            def x_split(b, i):
                act.wait_ge(*x_turned.done(b, i))
                act.wait_ge(*up_made.done(NM - 1, i - 1))
                act.activation(xt_hi[:, :, b * P:(b + 1) * P], bank("x", b)[:].rearrange("p (c n) -> p c n", c=NC),
                               ACT.Copy).then_inc(*xt_hi_done.inc())

            def gu_split(m, j):
                act.wait_ge(*gu_in.done(m, j))
                act.wait_ge(*up_made.done(m, j - 1))
                for w in range(2):
                    y = act.activation(gu_hi[:, w, :, m * P:m * P + size[m]], gu_raw[m][:, w, :, :], ACT.Copy)
                y.then_inc(*gu_hi_done.inc())

            def dn_split(m, j):
                act.wait_ge(*dn_in.done(m, j))
                act.wait_ge(*down_made.done(m, j - 1))
                act.activation(dn_hi[0:size[m], m, :], dn_raw[m][0:size[m], :], ACT.Copy).then_inc(*dn_hi_done.inc())

            if not shared:
                for b in range(TB):
                    if b == 2:
                        gu_split(0, 0)
                    x_split(b, 0)
                for m in range(1, NM):
                    gu_split(m, 0)

            def tile(i, more, first=False):
                for m in range(NM):
                    n = size[m]
                    if shared and first:
                        act.wait_ge(dn_in[m % 2], 16 * (m // 2 + 1))
                        act.activation(dn_hi[:, m, :], dn_raw[m % 2][:], ACT.Copy).then_inc(dn_hi_ready, 1)
                    act.wait_ge(*gate_made.done(m, i))
                    act.wait_ge(*act_done.done(m - 2, i))
                    act.activation(silu[m % 2][0:n, :], bank("gate", m)[0:n, :], ACT.Silu).then_inc(*silu_done.inc())
                    act.wait_ge(*act_done.done(m, i))
                    act.wait_ge(*down_made.done(m - 2, i))
                    act.activation(act_hi[m % 2][0:n, :], act_f[m % 2][0:n, :], ACT.Copy).then_inc(*act_hi_done.inc())
                    if not shared:
                        if m == 0:
                            dn_split(0, i)
                            dn_split(1, i)
                        if m == 1:
                            dn_split(2, i)
                            if more:
                                act.wait_ge(*sh_in.done(0, i))
                                act.activation(keep["gu_hi"][:, bass.ds(i, 1), :, :].rearrange("p a c n -> p (a c) n"),
                                               sh_raw[0][:], ACT.Copy).then_inc(*sh_hi_done.inc())
                        if more and m < NM - 1:
                            gu_split(m, i + 1)
                if more or not shared:
                    for b in range(TB):
                        x_split(b, i + 1)
                if not shared:
                    for b in range(TB):
                        act.wait_ge(*down_made.done(NM - 1, i))
                        act.wait_ge(*out_sent.done(b, i - 1))
                        act.activation(out[b][:], acc[b][:], ACT.Copy).then_inc(*acc_read.inc())
                    for b in range(TB):
                        act.wait_ge(*acc_read.done(b, i))
                        act.dma_start(scratch["expert_rows"][bass.ds((i * TB + b) * P, P), :], out[b][:])\
                           .then_inc(*out_sent.inc(b))
                    if more:
                        gu_split(NM - 1, i + 1)

            tile(0, True, first=True)
            with act.Fori(1, last) as i:
                tile(i, True)
            tile(last, False)
            if not shared:
                for b in range(TB):
                    act.wait_ge(*out_sent.done(b, last))

        @block.vector
        def _(dve):
            dve.wait_ge(credits_given, lap)

            def x_split(b, i):
                cols = slice(b * P, (b + 1) * P)
                dve.wait_ge(*xt_hi_done.done(b, i))
                dve.tensor_tensor(xt_lo[:, :, cols], bank("x", b)[:].rearrange("p (c n) -> p c n", c=NC),
                                  xt_hi[:, :, cols].bitcast(F32), ALU.subtract).then_inc(*xt_lo_done.inc())

            def gu_split(m, j):
                dve.wait_ge(*gu_hi_done.done(m, j))
                for w in range(2):
                    cols = slice(m * P, m * P + size[m])
                    y = dve.tensor_tensor(gu_lo[:, w, :, cols], gu_raw[m][:, w, :, :], gu_hi[:, w, :, cols].bitcast(F32),
                                          ALU.subtract)
                y.then_inc(*gu_lo_done.inc())

            def dn_split(m, j):
                n = size[m]
                dve.wait_ge(*dn_hi_done.done(m, j))
                dve.tensor_tensor(dn_lo[0:n, m, :], dn_raw[m][0:n, :], dn_hi[0:n, m, :].bitcast(F32), ALU.subtract)\
                   .then_inc(*dn_lo_done.inc())

            if not shared:
                for b in range(TB):
                    if b == 2:
                        gu_split(0, 0)
                    x_split(b, 0)
                for m in range(1, NM):
                    gu_split(m, 0)

            def join(b, i):
                for k in range(TOPK):
                    dve.wait_ge(*picked_in[k].done(b, i))
                    dve.wait_ge(*joined[k].done(b, i))
                    dve.scalar_tensor_tensor(out=out[b][:], in0=picked[k][b % 2][:], scalar=gates_now[:, b, k:k + 1],
                                             in1=out[b][:], op0=ALU.mult, op1=ALU.add).then_inc(*joined[k + 1].inc())

            def tile(i, more, first=False):
                for m in range(NM):
                    n = size[m]
                    if shared and first:
                        dve.wait_ge(dn_hi_ready, m + 1)
                        dve.tensor_tensor(dn_lo[:, m, :], dn_raw[m % 2][:], dn_hi[:, m, :].bitcast(F32), ALU.subtract)\
                           .then_inc(dn_lo_ready, 1)
                    dve.wait_ge(*silu_done.done(m, i))
                    dve.wait_ge(*up_made.done(m, i))
                    dve.wait_ge(*act_lo_done.done(m - 2, i))
                    dve.tensor_tensor(act_f[m % 2][0:n, :], bank("up", m)[0:n, :], silu[m % 2][0:n, :], ALU.mult)\
                       .then_inc(*act_done.inc())
                    dve.wait_ge(*act_hi_done.done(m, i))
                    dve.tensor_tensor(act_lo[m % 2][0:n, :], act_f[m % 2][0:n, :], act_hi[m % 2][0:n, :].bitcast(F32),
                                      ALU.subtract).then_inc(*act_lo_done.inc())
                    if not shared:
                        if m == 0:
                            dn_split(0, i)
                            dn_split(1, i)
                        if m == 1:
                            dn_split(2, i)
                            if more:
                                block_now = bass.ds(i, 1)
                                dve.wait_ge(*sh_hi_done.done(0, i))
                                dve.tensor_tensor(keep["gu_lo"][:, block_now, :, :].rearrange("p a c n -> p (a c) n"),
                                                  sh_raw[0][:],
                                                  keep["gu_hi"][:, block_now, :, :].rearrange("p a c n -> p (a c) n")
                                                  .bitcast(F32), ALU.subtract).then_inc(*sh_lo_done.inc())
                        if more and m < NM - 1:
                            gu_split(m, i + 1)
                    if shared and m < TB and not first:
                        join(m, i - 1)
                if more or not shared:
                    for b in range(TB):
                        x_split(b, i + 1)
                if shared:
                    dve.wait_ge(*joined[TOPK].done(TB - 1, i - 1))
                    dve.tensor_copy(gates_now[:], keep["gates"][:, bass.ds(i * TB, TB), :]).then_inc(*gates_copied.inc())
                    dve.wait_ge(*gates_copied.done(0, i))
                    dve.wait_ge(*down_made.done(NM - 1, i))
                    for b in range(TB):
                        dve.wait_ge(*res_in.done(b, i))
                        dve.scalar_tensor_tensor(out=out[b][:], in0=acc[b][:], scalar=gates_now[:, b, TOPK:TOPK + 1],
                                                 in1=out[b][:], op0=ALU.mult, op1=ALU.add).then_inc(*joined[0].inc())
                elif more:
                    gu_split(NM - 1, i + 1)

            tile(0, True, first=True)
            with dve.Fori(1, last) as i:
                tile(i, True)
            tile(last, False)
            if shared:
                for b in range(TB):
                    join(b, last)

        @block.tensor
        def _(pe):
            pe.wait_ge(credits_given, lap)

            def x_turn(b, i, free):
                pe.wait_ge(*x_in.done(b, i))
                pe.wait_ge(*free)
                for c in range(NC):
                    y = pe.transpose(bank("x", b)[:, c * P:(c + 1) * P], x[b][:, c * P:(c + 1) * P], eye[:])
                y.then_inc(*x_turned.inc())

            if not shared:
                for b in range(TB):
                    x_turn(b, 0, xt_lo_done.done(b - 2, 0))

            def tile(i, more, first=False):
                def down(m, part=range(TB)):
                    n = size[m]
                    if shared and first:
                        pe.wait_ge(dn_lo_ready, m + 1)
                    if not shared:
                        pe.wait_ge(*dn_lo_done.done(m, i))
                    pe.wait_ge(*act_lo_done.done(m, i))
                    for b in part:
                        if m == 0:
                            pe.wait_ge(*acc_read.done(b, i - 1))
                        cols = slice(b * P, (b + 1) * P)
                        y = split_product(pe, acc[b][:], [a[m % 2][0:n, cols] for a in (act_hi, act_lo)],
                                          [w[0:n, m, :] for w in (dn_hi, dn_lo)], m == 0, m == NM - 1)
                    if b == TB - 1:
                        y.then_inc(*down_made.inc())

                pe.wait_ge(*xt_lo_done.done(TB - 1, i))
                for m in range(NM):
                    if not shared:
                        pe.wait_ge(*gu_lo_done.done(m, i))
                    for w, (kind, made) in enumerate((("gate", gate_made), ("up", up_made))):
                        parts = gu_parts(w, m)
                        pe.wait_ge(*bank_free(kind, m, i, more))
                        for ic in range(NC):
                            y = split_product(pe, bank(kind, m)[0:size[m], :], parts(ic),
                                              [a[:, ic, :] for a in (xt_hi, xt_lo)], ic == 0, ic == NC - 1)
                        y.then_inc(*made.inc())
                    if m >= 1:
                        down(m - 1)
                for pair in (range(0, 2), range(2, TB)):
                    if more or not shared:
                        for b in pair:
                            x_turn(b, i + 1, bank_free("x", b, i))
                    down(NM - 1, pair)

            tile(0, True, first=True)
            with pe.Fori(1, last) as i:
                tile(i, True)
            tile(last, False)


def program(nc, io):
    tokens = io["x"].shape[0] * io["x"].shape[1]
    assert io["x"].shape[1] == P
    slot_tiles = (tokens * TOPK + EXPERTS * (GT - 1)) // GT
    with ExitStack() as ctx:
        def new_sem(name):
            return ctx.enter_context(nc.semaphore(name))

        def sb(name, shape, dt=F32):
            return ctx.enter_context(nc.sbuf_tensor(name, shape, dt))

        scratch = {name: nc.dram_tensor(f"{name}_dram", (rows, DIM), F32, kind="Internal").ap()
                   for name, rows in (("h2", tokens), ("xn2", tokens), ("expert_rows", slot_tiles * GT))}
        keep = {
            "eye": sb("eye", [P, P]),
            "logits": sb("logits", [P, tokens // P, LOGITS]),
            "gates": sb("gates", [P, tokens // P, TOPK + 1]),
            "slots": sb("slots", [P, TOPK, tokens // P], I32),
            "slot_token": sb("slot_token", [P, (slot_tiles + 1) * TB], I32),
            "tile_expert": sb("tile_expert", [P, slot_tiles], I32),
            "credits_given": new_sem("credits_given"),
            "pool_go": new_sem("pool_go"), "sp_go": new_sem("sp_go"),
        }
        attention_phase(nc, new_sem, keep, io, scratch)
        routing_phase(nc, new_sem, keep, io, scratch)
        blocks = 2 * (I_SH // P)
        keep["gu_hi"] = sb("gu_hi", [P, blocks, NC, P], F32R)
        keep["gu_lo"] = sb("gu_lo", [P, blocks, NC, P], F32R)
        keep["x"] = [sb(f"x{b}", [P, DIM]) for b in range(TB)]
        keep["xt_hi"], keep["xt_lo"] = sb("ffn_xt_hi", [P, NC, GT], F32R), sb("ffn_xt_lo", [P, NC, GT], F32R)
        ffn_phase(nc, new_sem, keep, io, scratch, shared=False)
        ffn_phase(nc, new_sem, keep, io, scratch, shared=True)


_INS = ["x", "L0_tok_weight", "L0_attn_Wq", "L0_attn_bq", "L0_attn_Wk", "L0_attn_bk", "L0_attn_Wv", "L0_attn_bv",
        "L0_attn_Wout", "L0_attn_bout", "L0_ffn_W_router", "L0_ffn_W_sgate", "L0_ffn_Ws_gate_up", "L0_ffn_Ws_down",
        "L0_ffn_We_gate_up", "L0_ffn_We_down"]


def kernel(**inputs):
    import numpy as _np
    import concourse.bacc as _bacc
    from concourse import mybir as _mybir
    from concourse.bass_utils import run_bass_kernel_spmd as _run

    nc = _bacc.Bacc("TRN2", target_bir_lowering=False, num_devices=1)
    arrays, io = {}, {}
    for name in _INS:
        a = _np.ascontiguousarray(inputs[name])
        arrays[f"in_{name}_dram"] = a
        io[name] = nc.dram_tensor(f"in_{name}_dram", a.shape, _mybir.dt.from_np(a.dtype), kind="ExternalInput").ap()
    shape = (*inputs["x"].shape, DIM)
    out = nc.dram_tensor("out_0_dram", shape, _mybir.dt.float32, kind="ExternalOutput").ap()
    io["out"] = out.rearrange("s t d -> (s t) d")
    program(nc, io)
    r = _run(nc, [arrays], core_ids=[0])
    return r.results[0]["out_0_dram"]
```
